# Optimizing a Trainium2 kernel written in Bass

```python
import numpy as np
import jax
import jax.numpy as jnp

def _softmax(x, axis=-1):
    return jax.nn.softmax(x, axis=axis)
def _gelu(x):
    return jax.nn.gelu(x, approximate=True)
def _silu(x):
    return jax.nn.silu(x)
def _sigmoid(x):
    return jax.nn.sigmoid(x)
def _layernorm(x, axis=-1, eps=1e-5):
    m = jnp.mean(x, axis=axis, keepdims=True)
    v = jnp.var(x, axis=axis, keepdims=True)
    return (x - m) / jnp.sqrt(v + eps)
def _scatter_add(tgt, idx, src, axis=0):
    return tgt.at[idx].add(src)
def _segment_sum(src, seg, n):
    return jax.ops.segment_sum(src, seg, n)

kernel_name = 'mk_dlrm_tower_d1_rec_4e8d9b'

def setup_inputs(seed: int = 0):
    np.random.seed(seed)
    _w = jnp.asarray
    def _rec_inputs():
        import jax
        import jax.numpy as jnp
        _tk = jax.random.key(seed)
        ids = jnp.stack([jax.random.randint(jax.random.fold_in(_tk, 200 + f), (1024,), 0, v, jnp.int32) for f, v in enumerate([10000, 1000000, 1000, 1000000])], axis=1)
        tbl_0 = 0.05 * jax.random.normal(jax.random.fold_in(_tk, 500 + 0), (10000, 4), jnp.float32)
        tbl_1 = 0.05 * jax.random.normal(jax.random.fold_in(_tk, 500 + 1), (1000000, 4), jnp.float32)
        tbl_2 = 0.05 * jax.random.normal(jax.random.fold_in(_tk, 500 + 2), (1000, 4), jnp.float32)
        tbl_3 = 0.05 * jax.random.normal(jax.random.fold_in(_tk, 500 + 3), (1000000, 4), jnp.float32)
        _rk = jax.random.fold_in(_tk, 7)
        r_x = 7.22013e-05 + 1.00017 * jax.random.normal(jax.random.fold_in(_rk, 101), (1024, 2048), jnp.float32)
        W_top1 = 0.0197642 * jax.random.normal(jax.random.fold_in(_tk, 801), (2560, 512), jnp.float32)
        W_top2 = 0.0441942 * jax.random.normal(jax.random.fold_in(_tk, 802), (512, 256), jnp.float32)
        W_top3 = 0.0625 * jax.random.normal(jax.random.fold_in(_tk, 803), (256, 1), jnp.float32)
        b_top1 = jnp.zeros((512,), jnp.float32)
        b_top2 = jnp.zeros((256,), jnp.float32)
        return r_x, ids, tbl_0, tbl_1, tbl_2, tbl_3, W_top1, b_top1, W_top2, b_top2, W_top3
    r_x, ids, tbl_0, tbl_1, tbl_2, tbl_3, W_top1, b_top1, W_top2, b_top2, W_top3 = _rec_inputs()
    def _L0_rec_setup():
        import jax, jax.numpy as jnp
        import numpy as np
        B, IN, HID, D, N, OUT = (4096, 2048, 2048, 512, 4, 512)
        H = 8
        HD = D // H

        def _ln(x, g, b):
            m = x.mean(-1, keepdims=True)
            v = ((x - m) ** 2).mean(-1, keepdims=True)
            return (x - m) / jnp.sqrt(v + 1e-05) * g + b
        key = jax.random.key(seed)
        ks = jax.random.split(key, 32)

        def nrm(k, shape, scale=0.02):
            return jax.random.normal(k, shape, jnp.float32) * scale
        inp = {}
        inp['x'] = jax.random.normal(ks[0], (B, IN), jnp.float32)
        inp['strength'] = jax.random.uniform(ks[1], (B, N, N), jnp.float32)
        for t, i in (('er', 2), ('ei', 4)):
            inp[t + '_W1'] = nrm(ks[i], (HID, IN))
            inp[t + '_b1'] = jnp.zeros((HID,), jnp.float32)
            inp[t + '_g1'] = jnp.ones((HID,), jnp.float32)
            inp[t + '_be1'] = jnp.zeros((HID,), jnp.float32)
            inp[t + '_W2'] = nrm(ks[i + 1], (N * D, HID))
            inp[t + '_b2'] = jnp.zeros((N * D,), jnp.float32)
        names = ['Wq_r', 'Wq_i', 'Wk_r', 'Wk_i', 'Wv_r', 'Wv_i', 'Wo_r', 'Wo_i']
        for j, nm in enumerate(names):
            inp[nm] = nrm(ks[6 + j], (D, D))
            inp['b' + nm[1:]] = jnp.zeros((D,), jnp.float32)
        inp['int_Wr'] = jnp.tile(jnp.eye(D, dtype=jnp.float32)[None], (N, 1, 1))
        inp['int_Wi'] = jnp.zeros((N, D, D), jnp.float32)
        inp['meas_Mr'] = nrm(ks[20], (OUT, D), 1.0 / np.sqrt(D))
        inp['meas_Mi'] = nrm(ks[21], (OUT, D), 1.0 / np.sqrt(D))
        inp['post_W'] = nrm(ks[22], (OUT, OUT))
        inp['post_b'] = jnp.zeros((OUT,), jnp.float32)
        inp['post_g'] = jnp.ones((OUT,), jnp.float32)
        inp['post_be'] = jnp.zeros((OUT,), jnp.float32)
        return inp
    _L0_rec_all = _L0_rec_setup()
    _L0_rec_in = {k: v for k, v in _L0_rec_all.items() if k in ('er_W1', 'er_b1', 'er_g1', 'er_be1', 'er_W2', 'er_b2', 'ei_W1', 'ei_b1', 'ei_g1', 'ei_be1', 'ei_W2', 'ei_b2', 'Wq_r', 'bq_r', 'Wq_i', 'bq_i', 'Wk_r', 'bk_r', 'Wk_i', 'bk_i', 'Wv_r', 'bv_r', 'Wv_i', 'bv_i', 'Wo_r', 'bo_r', 'Wo_i', 'bo_i', 'int_Wr', 'int_Wi', 'meas_Mr', 'meas_Mi', 'post_W', 'post_b', 'post_g', 'post_be', )}
    del _L0_rec_all

    return {
        "r_x": r_x,
        "ids": ids,
        "tbl_0": tbl_0,
        "tbl_1": tbl_1,
        "tbl_2": tbl_2,
        "tbl_3": tbl_3,
        "W_top1": W_top1,
        "b_top1": b_top1,
        "W_top2": W_top2,
        "b_top2": b_top2,
        "W_top3": W_top3,
        "L0_rec_er_W1": _L0_rec_in["er_W1"],
        "L0_rec_er_b1": _L0_rec_in["er_b1"],
        "L0_rec_er_g1": _L0_rec_in["er_g1"],
        "L0_rec_er_be1": _L0_rec_in["er_be1"],
        "L0_rec_er_W2": _L0_rec_in["er_W2"],
        "L0_rec_er_b2": _L0_rec_in["er_b2"],
        "L0_rec_ei_W1": _L0_rec_in["ei_W1"],
        "L0_rec_ei_b1": _L0_rec_in["ei_b1"],
        "L0_rec_ei_g1": _L0_rec_in["ei_g1"],
        "L0_rec_ei_be1": _L0_rec_in["ei_be1"],
        "L0_rec_ei_W2": _L0_rec_in["ei_W2"],
        "L0_rec_ei_b2": _L0_rec_in["ei_b2"],
        "L0_rec_Wq_r": _L0_rec_in["Wq_r"],
        "L0_rec_bq_r": _L0_rec_in["bq_r"],
        "L0_rec_Wq_i": _L0_rec_in["Wq_i"],
        "L0_rec_bq_i": _L0_rec_in["bq_i"],
        "L0_rec_Wk_r": _L0_rec_in["Wk_r"],
        "L0_rec_bk_r": _L0_rec_in["bk_r"],
        "L0_rec_Wk_i": _L0_rec_in["Wk_i"],
        "L0_rec_bk_i": _L0_rec_in["bk_i"],
        "L0_rec_Wv_r": _L0_rec_in["Wv_r"],
        "L0_rec_bv_r": _L0_rec_in["bv_r"],
        "L0_rec_Wv_i": _L0_rec_in["Wv_i"],
        "L0_rec_bv_i": _L0_rec_in["bv_i"],
        "L0_rec_Wo_r": _L0_rec_in["Wo_r"],
        "L0_rec_bo_r": _L0_rec_in["bo_r"],
        "L0_rec_Wo_i": _L0_rec_in["Wo_i"],
        "L0_rec_bo_i": _L0_rec_in["bo_i"],
        "L0_rec_int_Wr": _L0_rec_in["int_Wr"],
        "L0_rec_int_Wi": _L0_rec_in["int_Wi"],
        "L0_rec_meas_Mr": _L0_rec_in["meas_Mr"],
        "L0_rec_meas_Mi": _L0_rec_in["meas_Mi"],
        "L0_rec_post_W": _L0_rec_in["post_W"],
        "L0_rec_post_b": _L0_rec_in["post_b"],
        "L0_rec_post_g": _L0_rec_in["post_g"],
        "L0_rec_post_be": _L0_rec_in["post_be"],
    }

def reference(r_x, ids, tbl_0, tbl_1, tbl_2, tbl_3, W_top1, b_top1, W_top2, b_top2, W_top3, L0_rec_er_W1, L0_rec_er_b1, L0_rec_er_g1, L0_rec_er_be1, L0_rec_er_W2, L0_rec_er_b2, L0_rec_ei_W1, L0_rec_ei_b1, L0_rec_ei_g1, L0_rec_ei_be1, L0_rec_ei_W2, L0_rec_ei_b2, L0_rec_Wq_r, L0_rec_bq_r, L0_rec_Wq_i, L0_rec_bq_i, L0_rec_Wk_r, L0_rec_bk_r, L0_rec_Wk_i, L0_rec_bk_i, L0_rec_Wv_r, L0_rec_bv_r, L0_rec_Wv_i, L0_rec_bv_i, L0_rec_Wo_r, L0_rec_bo_r, L0_rec_Wo_i, L0_rec_bo_i, L0_rec_int_Wr, L0_rec_int_Wi, L0_rec_meas_Mr, L0_rec_meas_Mi, L0_rec_post_W, L0_rec_post_b, L0_rec_post_g, L0_rec_post_be):
    import jax
    import jax.numpy as jnp
    def _L0_rec_ref(x, strength, er_W1, er_b1, er_g1, er_be1, er_W2, er_b2, ei_W1, ei_b1, ei_g1, ei_be1, ei_W2, ei_b2, Wq_r, bq_r, Wq_i, bq_i, Wk_r, bk_r, Wk_i, bk_i, Wv_r, bv_r, Wv_i, bv_i, Wo_r, bo_r, Wo_i, bo_i, int_Wr, int_Wi, meas_Mr, meas_Mi, post_W, post_b, post_g, post_be):
        import jax, jax.numpy as jnp
        import numpy as np
        B, IN, HID, D, N, OUT = (4096, 2048, 2048, 512, 4, 512)
        H = 8
        HD = D // H

        def _ln(x, g, b):
            m = x.mean(-1, keepdims=True)
            v = ((x - m) ** 2).mean(-1, keepdims=True)
            return (x - m) / jnp.sqrt(v + 1e-05) * g + b
        Bsz = x.shape[0]

        def enc(W1, b1, g, be, W2, b2):
            h = jax.nn.gelu(_ln(x @ W1.T + b1, g, be), approximate=False)
            return (h @ W2.T + b2).reshape(Bsz, N, D)
        sr = enc(er_W1, er_b1, er_g1, er_be1, er_W2, er_b2)
        si = enc(ei_W1, ei_b1, ei_g1, ei_be1, ei_W2, ei_b2)

        def heads(t):
            return t.reshape(Bsz, N, H, HD).transpose(0, 2, 1, 3)
        qr = heads(sr @ Wq_r.T + bq_r)
        qi = heads(si @ Wq_i.T + bq_i)
        kr = heads(sr @ Wk_r.T + bk_r)
        ki = heads(si @ Wk_i.T + bk_i)
        vr = heads(sr @ Wv_r.T + bv_r)
        vi = heads(si @ Wv_i.T + bv_i)
        ar = jnp.einsum('bhnd,bhmd->bhnm', qr, kr) + jnp.einsum('bhnd,bhmd->bhnm', qi, ki)
        ai = jnp.einsum('bhnd,bhmd->bhnm', qi, kr) - jnp.einsum('bhnd,bhmd->bhnm', qr, ki)
        mag = jnp.sqrt(ar ** 2 + ai ** 2 + 1e-08) * HD ** (-0.5)
        w = jax.nn.softmax(mag, axis=-1)
        out_r = jnp.einsum('bhnm,bhmd->bhnd', w, vr).transpose(0, 2, 1, 3).reshape(Bsz, N, D)
        out_i = jnp.einsum('bhnm,bhmd->bhnd', w, vi).transpose(0, 2, 1, 3).reshape(Bsz, N, D)
        attn_r = out_r @ Wo_r.T + bo_r
        attn_i = out_i @ Wo_i.T + bo_i
        R = jnp.einsum('bnd,ned->bne', attn_r, int_Wr) - jnp.einsum('bnd,ned->bne', attn_i, int_Wi)
        I = jnp.einsum('bnd,ned->bne', attn_r, int_Wi) + jnp.einsum('bnd,ned->bne', attn_i, int_Wr)
        Ri, Ii = (R[:, :, None, :], I[:, :, None, :])
        Rj, Ij = (R[:, None, :, :], I[:, None, :, :])
        phase = jnp.arctan2(Ii * Rj - Ri * Ij, Ri * Rj + Ii * Ij)
        f = jnp.cos(phase) * strength[..., None]
        sup_r = jnp.einsum('bijd,bjd->bd', f, R)
        sup_i = jnp.einsum('bijd,bjd->bd', f, I)
        norm = jnp.sqrt(jnp.sum(sup_r ** 2 + sup_i ** 2, axis=-1, keepdims=True) + 1e-08)
        sup_r = sup_r / norm
        sup_i = sup_i / norm
        mr = sup_r @ meas_Mr.T - sup_i @ meas_Mi.T
        mi = sup_r @ meas_Mi.T + sup_i @ meas_Mr.T
        amp = jnp.sqrt(mr ** 2 + mi ** 2)
        out = jax.nn.gelu(_ln(amp @ post_W.T + post_b, post_g, post_be), approximate=False)
        return out

    e = jnp.stack([tbl_0[ids[:, 0]], tbl_1[ids[:, 1]], tbl_2[ids[:, 2]], tbl_3[ids[:, 3]]], axis=1)
    z = _L0_rec_ref(r_x, e, L0_rec_er_W1, L0_rec_er_b1, L0_rec_er_g1, L0_rec_er_be1, L0_rec_er_W2, L0_rec_er_b2, L0_rec_ei_W1, L0_rec_ei_b1, L0_rec_ei_g1, L0_rec_ei_be1, L0_rec_ei_W2, L0_rec_ei_b2, L0_rec_Wq_r, L0_rec_bq_r, L0_rec_Wq_i, L0_rec_bq_i, L0_rec_Wk_r, L0_rec_bk_r, L0_rec_Wk_i, L0_rec_bk_i, L0_rec_Wv_r, L0_rec_bv_r, L0_rec_Wv_i, L0_rec_bv_i, L0_rec_Wo_r, L0_rec_bo_r, L0_rec_Wo_i, L0_rec_bo_i, L0_rec_int_Wr, L0_rec_int_Wi, L0_rec_meas_Mr, L0_rec_meas_Mi, L0_rec_post_W, L0_rec_post_b, L0_rec_post_g, L0_rec_post_be)
    z = z.reshape(z.shape[0], -1)
    h = jnp.concatenate([z, r_x], axis=1)
    h = jnp.maximum(h @ W_top1 + b_top1, 0.0)
    h = jnp.maximum(h @ W_top2 + b_top2, 0.0)
    y = h @ W_top3
    return y


_drawn_inputs = setup_inputs


def setup_inputs(seed=0):
    import zlib

    import numpy as np

    out = dict(_drawn_inputs(seed))
    spreads = {'b_top1': (0.0, 0.1),
     'b_top2': (0.0, 0.1),
     'L0_rec_er_b1': (0.0, 0.8),
     'L0_rec_er_g1': (1.0, 0.6),
     'L0_rec_er_be1': (0.0, 0.8),
     'L0_rec_er_b2': (0.0, 0.8),
     'L0_rec_ei_b1': (0.0, 0.8),
     'L0_rec_ei_g1': (1.0, 0.6),
     'L0_rec_ei_be1': (0.0, 0.8),
     'L0_rec_ei_b2': (0.0, 0.8),
     'L0_rec_bq_r': (0.0, 0.8),
     'L0_rec_bq_i': (0.0, 0.8),
     'L0_rec_bk_r': (0.0, 0.8),
     'L0_rec_bk_i': (0.0, 0.8),
     'L0_rec_bv_r': (0.0, 0.1),
     'L0_rec_bv_i': (0.0, 0.1),
     'L0_rec_bo_r': (0.0, 0.1),
     'L0_rec_bo_i': (0.0, 0.1),
     'L0_rec_int_Wi': (0.0, 0.1),
     'L0_rec_post_b': (0.0, 0.1),
     'L0_rec_post_g': (1.0, 0.2),
     'L0_rec_post_be': (0.0, 0.1)}
    factors = {'L0_rec_Wq_r': 8.0, 'L0_rec_Wq_i': 8.0, 'L0_rec_Wk_r': 8.0, 'L0_rec_Wk_i': 8.0}
    for name, (base, spread) in spreads.items():
        noise = np.random.default_rng([zlib.crc32(name.encode()), seed]).standard_normal(out[name].shape)
        drawn = base * np.exp(spread * noise) if base else spread * noise
        out[name] = jnp.asarray(drawn.astype(out[name].dtype))
    for name, factor in factors.items():
        out[name] = (out[name] * factor).astype(out[name].dtype)
    return out
```

```python
from contextlib import ExitStack

import concourse.bass as bass
from concourse import mybir

F32 = mybir.dt.float32
F32R = mybir.dt.float32r
I32 = mybir.dt.int32
U32 = mybir.dt.uint32
ALU = mybir.AluOpType
ACT = mybir.ActivationFunctionType
AX_X = mybir.AxisListType.X

P = 128
BATCH, IN, HID, D, N, OUT, TOP = 1024, 2048, 2048, 512, 4, 512, 512
HEADS, HD = 8, 64
HALF = 512
HALVES = BATCH // HALF
BT = HALF // P
KX = IN // P
KH = HID // P
KD = D // P
STEPS = 2 * HALVES
RING = 4
G = 4
LN_EPS = 1e-5
EPS = 1e-8
SCALE = HD ** -0.5

RAW_STEP = KX + 4 * KH + N * KH + 3 * KD
USE_STEP = 4 * KH + N * KH + 3 * KD
SET0_STEP = 2 + 2 + 6
SET1_STEP = 2 + 4 + 2 + 6
RAW_MIX = N * 4 * KD + 2 * KX + 3 * KD + KD + 4
RAW_MIX0 = STEPS * RAW_STEP
USE_MIX0 = STEPS * USE_STEP
SET0_MIX, SET1_MIX = 4 * N + 5, 3 * N + 5

ENC_COLS = 3 * KH
MIX_COLS = 2 * KD + 2 * KD + 4 + 2 + 2


class Count:

    def __init__(self, sem, start=0):
        self.sem, self.start, self.n = sem, start, 0

    def at(self, start):
        self.start, self.n = start, 0

    def next(self):
        self.n += 1
        return self.start + self.n

    @property
    def now(self):
        return self.start + self.n


def build(nc, enc_w, xs, enc_rows, enc_cols, wo, int_w, post_w, top1, top2, mix_cols, post_row,
          ids, tables, y):
    ctx = ExitStack()
    with ctx:
        def sem(name):
            return ctx.enter_context(nc.semaphore(name))

        address = [(nc.sbuf_base + 31) // 32 * 32]

        def place(name, shape, dtype, offset=None):
            size = 4
            for d in shape[1:]:
                size *= d
            if offset is None:
                offset = address[0]
                address[0] += (size + 31) // 32 * 32
            return nc.alloc_sbuf_tensor_at(name, shape, dtype, offset=offset)

        a0 = address[0]
        a_hi = place("a_hi", [P, 16, HALF], F32R)
        a_lo = place("a_lo", [P, 16, HALF], F32R)
        s0 = address[0]
        s_hi = place("s_hi", [P, 16, HALF], F32R)
        s_lo = place("s_lo", [P, 16, HALF], F32R)
        hid = place("hid", [P, BT, HID], F32, s0)
        KB = 1024
        at_in = place("at_in", [P, BT, D], F32, a0 + 24 * KB)
        ph = place("ph", [P, 2, 6656], F32, a0)
        top_part = place("top_part", [P, 4, HALF], F32, a0 + 56 * KB)
        meas_r = place("meas_r", [P, 4, HALF], F32, a0 + 24 * KB)
        meas_q = place("meas_q", [P, 4, HALF], F32, a0 + 16 * KB)
        post_z = place("post_z", [P, BT, OUT], F32, a0 + 24 * KB)
        ri = place("ri", [P, BT, 2, N, D], F32, s0)
        hid2 = place("hid2", [P, 2, HALF], F32, s0 + 56 * KB)
        qk = place("qk", [P, 2, 2, 3, N, P], F32, a0)
        vv = place("vv", [P, 2, 2, N, P], F32, a0 + 24 * KB)
        prod = place("prod", [P, 4096], F32, a0 + 32 * KB)
        dots = place("dots", [P, G, N, 3, 8], F32, a0 + 48 * KB)
        sm = place("sm", [P, 6, G * N, 8], F32, a0 + 50 * KB)
        ao = place("ao", [P, 2, 2, N, P], F32, a0 + 54 * KB)

        raw = place("raw", [P, RING, 512], F32)
        w_hi = place("w_hi", [P, RING, 512], F32R)
        w_lo = place("w_lo", [P, RING, 512], F32R)
        gf = place("gf", [P, 2, HALF], F32)
        rows = place("rows", [P, HID + 3 * D], F32)
        stage = place("stage", [P, BT, D], F32)
        cols = place("cols", [P, ENC_COLS], F32)
        mcols = place("mcols", [P, MIX_COLS], F32)
        prow = place("prow", [P, OUT], F32)
        ident = place("ident", [P, P], F32)
        stats = place("stats", [P, BT, 4, 6], F32)
        mv = place("mv", [P, BT, 2], F32)
        ln = place("ln", [P, 3, BT], F32)
        epsc = place("epsc", [P, 2], F32)
        mx = place("mx", [P, 2, G * N, 2], F32)
        nrm = place("nrm", [P, 8], F32)
        ids_sb = place("ids_sb", [P, 8 * N], I32)
        strength = place("strength", [P, 8, N, N], F32)
        sh = place("sh", [P, BT, N * N], F32)
        y_sb = place("y_sb", [1, BATCH], F32)

        ps = ctx.enter_context(nc.psum_tensor("ps", [P, 8, 512], F32))

        qkv = nc.dram_tensor("qkv_scratch", [STEPS, 3, N, BT, P, D], F32).ap()
        att = nc.dram_tensor("att_scratch", [HALVES, 2, N, BT, P, D], F32).ap()

        raw_loaded = [sem(f"raw_loaded{j}") for j in range(RING)]
        hi_done = sem("hi_done")
        lo_done = sem("lo_done")
        chunk_used = sem("chunk_used")
        block_done = sem("block_done")
        turned = sem("turned")
        bank_free = [sem("banks0_free"), sem("banks1_free")]
        h_done = sem("h_done")
        rows_loaded, cols_loaded = sem("rows_loaded"), sem("cols_loaded")
        consts = sem("consts")
        stats_seen = sem("stats_seen")
        stats_done, var_done, sd_done, rstd_done = sem("stats_done"), sem("var_done"), sem("sd_done"), sem("rstd_done")
        normed = sem("normed")
        tmp_done = sem("tmp_done")
        stored = [sem(f"stored{j}") for j in range(BT)]
        qk_loaded = [sem("qk_loaded0"), sem("qk_loaded1")]
        v_loaded = [sem("v_loaded0"), sem("v_loaded1")]
        scored, weighed = sem("scored"), sem("weighed")
        products = sem("products")
        dve_step = sem("dve_step")
        mag_in, mag_out, exp_in, exp_out = sem("mag_in"), sem("mag_out"), sem("exp_in"), sem("exp_out")
        ao_stored = [sem("ao_stored0"), sem("ao_stored1")]
        at_loaded = sem("at_loaded")
        squares, sq_sum, roots, ph_free = sem("squares"), sem("sq_sum"), sem("roots"), sem("ph_free")
        sup_sq, sup_sum, sup_root, sup_ready = sem("sup_sq"), sem("sup_sum"), sem("sup_root"), sem("sup_ready")
        ids_loaded, gathered = sem("ids_loaded"), sem("gathered")
        amp_in = sem("amp_in")
        h2_done, y_stored = sem("h2_done"), sem("y_stored")

        bank = lambda s, b: ps[:, 4 * s + b, :]
        block = ctx.enter_context(nc.Block())

        @block.sync
        def _(sp):
            def load(chunk, j, src, cols_=512):
                sp.wait_ge(lo_done, chunk + 1)
                sp.dma_start(raw[:, j, 0:cols_], src).then_inc(raw_loaded[j], 16)

            with sp.Fori(0, STEPS) as t:
                c0 = t * RAW_STEP
                half, enc = t // 2, t % 2
                with sp.Fori(0, KX // 2) as q:
                    for j in range(RING):
                        k = q * 2 + j // 2
                        src = xs[half, k] if j % 2 == 0 else enc_w[enc, k]
                        load(c0 + q * RING + j, j, src)
                with sp.Fori(0, (USE_STEP - KX) // RING) as q:
                    for j in range(RING):
                        load(c0 + 2 * KX + q * RING + j, j, enc_w[enc, q * RING + (KX + j)])

            with sp.Fori(0, HALVES) as half:
                c0 = half * RAW_MIX + RAW_MIX0
                with sp.Fori(0, N) as n:
                    for q in range(4):
                        for j in range(RING):
                            src = wo[q, j] if q < 2 else int_w[n, q - 2, j]
                            load(c0 + n * 16 + (4 * q + j), j, src)
                c0 = c0 + 16 * N
                with sp.Fori(0, KX // 2) as q:
                    for j in range(RING):
                        k = q * 2 + j // 2
                        src = top1[k + KD] if j % 2 == 0 else xs[half, k]
                        load(c0 + q * RING + j, j, src)
                c0 = c0 + 2 * KX
                for q in range(3):
                    for j in range(RING):
                        load(c0 + (4 * q + j), j, post_w[q, j])
                for j in range(RING):
                    load(c0 + (12 + j), j, top1[j])
                for j in range(RING):
                    load(c0 + (16 + j), j, top2[j], 256)

        @block.gpsimd
        def _(pool):
            pool.memset(ident[:, :], 0.0).then_inc(consts, 1)
            pool.memset(epsc[:, 0:1], LN_EPS).then_inc(consts, 1)
            pool.memset(epsc[:, 1:2], EPS).then_inc(consts, 1)
            pool.wait_ge(consts, 3)
            pool.affine_select(out=ident[:, :], in_=ident[:, :], compare_op=ALU.not_equal, fill=1.0,
                               base=0, pattern=[[-1, P]], channel_multiplier=1).then_inc(consts, 1)

            def low(chunk, j, hi, lo, width=512):
                pool.wait_ge(hi_done, chunk + 1)
                pool.tensor_tensor(lo, raw[:, j, 0:width], hi.bitcast(F32), ALU.subtract)\
                    .then_inc(lo_done, 1)

            with pool.Fori(0, STEPS) as t:
                c0 = t * RAW_STEP
                for k in range(KX):
                    low(c0 + 2 * k, 2 * k % RING, a_hi[:, k, :], a_lo[:, k, :])
                    low(c0 + (2 * k + 1), (2 * k + 1) % RING, w_hi[:, k % RING, :], w_lo[:, k % RING, :])
                with pool.Fori(0, (USE_STEP - KX) // RING) as q:
                    for j in range(RING):
                        low(c0 + 2 * KX + q * RING + j, j, w_hi[:, j, :], w_lo[:, j, :])

            pool.wait_ge(ids_loaded, 16)
            for b in range(BATCH // P):
                for f in range(N):
                    pool.indirect_dma_start(
                        strength[:, b, f, :], None, tables[f],
                        bass.IndirectOffsetOnAxis(ap=ids_sb[:, N * b + f:N * b + f + 1].bitcast(U32), axis=0))\
                        .then_inc(gathered, 16)

            with pool.Fori(0, HALVES) as half:
                c0 = half * RAW_MIX + RAW_MIX0
                with pool.Fori(0, (RAW_MIX - 4) // RING) as q:
                    for j in range(RING):
                        low(c0 + q * RING + j, j, w_hi[:, j, :], w_lo[:, j, :])
                for j in range(RING):
                    low(c0 + (RAW_MIX - 4 + j), j, w_hi[:, j, 0:256], w_lo[:, j, 0:256], 256)

        @block.scalar
        def _(act):
            act.sem_inc(lo_done, RING)
            act.dma_start(ids_sb[:, :], ids).then_inc(ids_loaded, 16)
            act.dma_start(mcols[:, :], mix_cols).then_inc(cols_loaded, 16)
            act.dma_start(prow[:, :], post_row.broadcast_to([P, OUT])).then_inc(rows_loaded, 16)
            def high(chunk, use, j, dst, width=512):
                act.wait_ge(raw_loaded[j], chunk_loads(chunk, j))
                if use is not None:
                    act.wait_ge(chunk_used, use + 1)
                act.activation(dst, raw[:, j, 0:width], ACT.Identity).then_inc(hi_done, 1)

            def chunk_loads(chunk, j):
                return (chunk - j) * 4 + 16

            def high_part(dst, s, b, bias):
                if bias is None:
                    ins = act.activation(dst, bank(s, b), ACT.Copy)
                else:
                    ins = act.activation(dst, bank(s, b), ACT.Identity, bias=bias)
                ins.then_inc(h_done, 1)

            with act.Fori(0, STEPS) as t:
                c0, u0 = t * RAW_STEP, t * USE_STEP
                act.wait_ge(bank_free[0], t * (4 * SET0_STEP) + 4)
                act.wait_ge(bank_free[1], t * (4 * SET1_STEP) + 4)
                act.dma_start(rows[:, :], enc_rows[t % 2].broadcast_to([P, HID + 3 * D])).then_inc(rows_loaded, 16)
                act.dma_start(cols[:, :], enc_cols[t % 2]).then_inc(cols_loaded, 16)
                for k in range(KX):
                    high(c0 + 2 * k, None, 2 * k % RING, a_hi[:, k, :])
                    high(c0 + (2 * k + 1), u0 + k, (2 * k + 1) % RING, w_hi[:, k % RING, :])
                with act.Fori(0, 3 * KH // RING + 1) as q:
                    for j in range(RING):
                        high(c0 + 2 * KX + q * RING + j, u0 + KX + q * RING + j, j, w_hi[:, j, :])
                act.wait_ge(consts, 4)
                act.wait_ge(var_done, (t + 1) * BT)
                act.activation(ln[:, 0, :], mv[:, :, 1], ACT.Sqrt, bias=epsc[:, 0:1]).then_inc(sd_done, 1)
                act.wait_ge(cols_loaded, t * 16 + 32)
                c1, u1 = c0 + 2 * KX + 3 * KH, u0 + 4 * KH
                for k in range(KH):
                    act.wait_ge(turned, t * KH + (k + 1))
                    act.wait_ge(tmp_done, t * KH + (k + 1))
                    act.activation(gf[:, k % 2, :], bank(1, k % 4), ACT.Gelu,
                                   scale=cols[:, k:k + 1], bias=cols[:, KH + k:KH + k + 1])
                    act.activation(a_hi[:, k, :], bank(1, k % 4), ACT.Gelu,
                                   scale=cols[:, k:k + 1], bias=cols[:, KH + k:KH + k + 1])\
                        .then_inc(bank_free[1], 1)
                    if k >= 4:
                        high(c1 + k, u1 + k, k % RING, w_hi[:, k % RING, :])
                for n in range(N):
                    q0 = c1 + (n + 1) * KH, u1 + (n + 1) * KH
                    for j in range(RING):
                        high(q0[0] + j, q0[1] + j, j, w_hi[:, j, :])
                    act.wait_ge(chunk_used, q0[1] + RING)
                    for b in range(KD):
                        high_part(s_hi[:, KD * n + b, :], n % 2, b,
                                  cols[:, 2 * KH + KD * n + b:2 * KH + KD * n + b + 1])
                    if n < N - 1:
                        with act.Fori(1, KH // RING) as q:
                            for j in range(RING):
                                high(q0[0] + q * RING + j, q0[1] + q * RING + j, j, w_hi[:, j, :])
                c2, u2 = c1 + N * KH, u1 + N * KH
                for w in range(3):
                    for n in range(N):
                        if n == N - 1 and w < 2:
                            for j in range(RING):
                                high(c2 + (KD * (w + 1) + j), u2 + (KD * (w + 1) + j), j, w_hi[:, j, :])
                        s = n % 2
                        for b in range(BT):
                            use = (4, 8)[s] + 2 * w + n // 2
                            act.wait_ge(bank_free[s], t * (4 * (SET0_STEP, SET1_STEP)[s]) + (4 * use + b + 5))
                            act.dma_start(qkv[t, w, n, b], stage[:, b, :]).then_inc(stored[b], 16)

            for b in range(BT):
                act.wait_ge(stored[b], 16 * STEPS * 3 * N + 16)

            def load_item(half, bt, g, par):
                for w in range(2):
                    for c in range(2):
                        src = qkv[half * 2 + c, w, :, bt, :, g * P:(g + 1) * P].rearrange("n p d -> p n d")
                        act.dma_start(qk[:, par, w, c, :, :], src).then_inc(qk_loaded[par], 16)

            def load_v(half, bt, g, par):
                for c in range(2):
                    src = qkv[half * 2 + c, 2, :, bt, :, g * P:(g + 1) * P].rearrange("n p d -> p n d")
                    act.dma_start(vv[:, par, c, :, :], src).then_inc(v_loaded[par], 16)

            with act.Fori(0, HALVES) as half:
                with act.Fori(0, BT) as bt:
                    it = half * BT + bt
                    for g in range(G):
                        act.wait_ge(scored, it * (G * N) + (N * g + N))
                        load_item(half, bt, g, g % 2)
                    for g in range(2):
                        act.wait_ge(weighed, it * (2 * G) + (2 * g + 2))
                        load_v(half, bt, g, g)
                    act.wait_ge(mag_in, it + 1)
                    act.activation(sm[:, 0, :, :], sm[:, 1, :, :], ACT.Sqrt).then_inc(mag_out, 1)
                    act.wait_ge(exp_in, it + 1)
                    act.activation(sm[:, 2, :, :], sm[:, 1, :, :], ACT.Exp, scale=SCALE).then_inc(exp_out, 1)
                    for g in range(G):
                        act.wait_ge(weighed, it * (2 * G) + (2 * g + 6))
                        for c in range(2):
                            dst = att[half, c, :, bt, :, g * P:(g + 1) * P].rearrange("n p d -> p n d")
                            act.dma_start(dst, ao[:, g % 2, c, :, :]).then_inc(ao_stored[g % 2], 16)
                        if g + 2 < G:
                            load_v(half, bt, g + 2, g % 2)

            for par in range(2):
                act.wait_ge(ao_stored[par], HALVES * BT * 64 + 32)

            h0, f0 = STEPS * N * KD, STEPS * KH
            with act.Fori(0, HALVES) as half:
                c0, u0 = half * RAW_MIX + RAW_MIX0, half * RAW_MIX + USE_MIX0

                def highs(first, count=RING, width=512):
                    for j in range(count):
                        high(c0 + (first + j), u0 + (first + j), j, w_hi[:, j, 0:width], width)

                with act.Fori(0, N) as n:
                    cn, un = c0 + n * 16, u0 + n * 16

                    def stream_highs(q):
                        for j in range(RING):
                            high(cn + (4 * q + j), un + (4 * q + j), j, w_hi[:, j, :])

                    for c in range(2):
                        act.wait_ge(turned, STEPS * KH + half * (8 * N + 12) + n * 8 + 4 * c)
                        act.dma_start(at_in[:, :, :], att[half, c, n].rearrange("b p d -> p b d"))\
                            .then_inc(at_loaded, 16)
                        stream_highs(c)
                        for k in range(KD):
                            act.wait_ge(turned, STEPS * KH + half * (8 * N + 12) + n * 8 + (4 * c + k + 1))
                            high_part(a_hi[:, k, :], 0, k, None)
                        act.wait_ge(chunk_used, un + (4 * c + 8))
                        for k in range(KD):
                            high_part(a_hi[:, 4 + 4 * c + k, :], 1, k, mcols[:, KD * c + k:KD * c + k + 1])
                    stream_highs(2)
                    act.wait_ge(block_done, half * (2 * N + 3) + n * 2 + (9 * STEPS + 1))
                    for b in range(BT):
                        act.activation(ri[:, b, 0, n, :], bank(0, b), ACT.Copy).then_inc(bank_free[0], 1)
                    stream_highs(3)
                    act.wait_ge(chunk_used, un + 20)
                    for b in range(BT):
                        act.activation(ri[:, b, 1, n, :], bank(1, b), ACT.Copy).then_inc(bank_free[1], 1)
                q = 16 * N
                for u in range(2 * BT):
                    bt, f = u // 2, u % 2
                    highs(q)
                    q += 4
                    uh = half * (2 * BT) + u
                    act.wait_ge(ph_free, uh + 1)
                    if u == 0:
                        act.wait_ge(bank_free[1], half * (4 * SET1_MIX) + (4 * STEPS * SET1_STEP + 4 + 12 * N))
                        act.wait_ge(bank_free[0], 4 * STEPS * SET0_STEP + 4 + half * (4 * SET0_MIX) + 16 * N)
                    for c in range(2):
                        act.activation(ph[:, u % 2, 1024 * c:1024 * c + 1024].rearrange("p (n d) -> p n d", n=N),
                                       ri[:, bt, c, :, 256 * f:256 * f + 256], ACT.Square).then_inc(squares, 1)
                    act.wait_ge(sq_sum, uh + 1)
                    act.activation(ph[:, u % 2, 1024:2048], ph[:, u % 2, 0:1024], ACT.Sqrt).then_inc(roots, 1)
                for bt in range(BT):
                    hb = half * BT + bt
                    act.wait_ge(ph_free, hb * 2 + 4)
                    for c in range(2):
                        act.activation(ri[:, bt, 1, 2 + c, :], ri[:, bt, 0, c, :], ACT.Square,
                                       accum_out=nrm[:, c:c + 1]).then_inc(sup_sq, 1)
                    act.wait_ge(sup_sum, hb + 1)
                    act.activation(nrm[:, 3:4], nrm[:, 2:3], ACT.Sqrt, bias=epsc[:, 1:2]).then_inc(sup_root, 1)
                tb = STEPS * KH + half * (8 * N + 12) + 8 * N
                highs(q)
                for c in range(2):
                    for k in range(KD):
                        act.wait_ge(turned, tb + (4 * c + k + 1))
                        high_part(a_hi[:, 4 * c + k, :], c, k, None)
                act.wait_ge(block_done, half * (2 * N + 3) + (9 * STEPS + 2 * N + 1))
                for k in range(4):
                    act.activation(meas_r[:, k, :], bank(0, k), ACT.Copy).then_inc(bank_free[0], 1)
                highs(q + 4)
                highs(q + 8)
                for k in range(4):
                    act.activation(meas_q[:, k, :], bank(1, k), ACT.Square).then_inc(bank_free[1], 1)
                fh = f0 + half * 12
                for k in range(4):
                    act.wait_ge(amp_in, half * 4 + (k + 1))
                    act.wait_ge(tmp_done, fh + (k + 1))
                    act.activation(gf[:, k % 2, :], meas_r[:, k, :], ACT.Sqrt)
                    act.activation(s_hi[:, k, :], meas_r[:, k, :], ACT.Sqrt).then_inc(h_done, 1)
                highs(q + 12)
                act.wait_ge(var_done, half * BT + (STEPS + 1) * BT)
                act.activation(ln[:, 0, :], mv[:, :, 1], ACT.Sqrt, bias=epsc[:, 0:1]).then_inc(sd_done, 1)
                for k in range(KD):
                    act.wait_ge(turned, tb + (9 + k))
                    act.wait_ge(tmp_done, fh + (5 + k))
                    for dst in (gf[:, k % 2, :], s_hi[:, 4 + k, :]):
                        ins = act.activation(dst, bank(0, k), ACT.Gelu, scale=mcols[:, 2 * KD + k:2 * KD + k + 1],
                                             bias=mcols[:, 3 * KD + k:3 * KD + k + 1])
                    ins.then_inc(bank_free[0], 1)
                highs(q + 16, width=256)
                for k in range(4):
                    act.wait_ge(bank_free[1], half * (4 * SET1_MIX) + (4 * STEPS * SET1_STEP + 4 + 12 * N + 16 + k + 1))
                    act.wait_ge(tmp_done, fh + (9 + k))
                    act.activation(gf[:, k % 2, :], post_z[:, k, :], ACT.Relu)
                    act.activation(s_hi[:, 8 + k, :], post_z[:, k, :], ACT.Relu).then_inc(h_done, 1)
                act.wait_ge(h_done, (half + 1) * (16 * N + 16) + STEPS * N * KD)
            act.wait_ge(bank_free[0], 4 * STEPS * SET0_STEP + 4 + 4 * HALVES * SET0_MIX)
            act.dma_start(y.rearrange("b o -> o b"), y_sb[:, :]).then_inc(y_stored, 16)
            act.wait_ge(y_stored, 16)

        @block.tensor
        def _(pe):
            pe.sem_inc(chunk_used, RING)
            for s in range(2):
                pe.sem_inc(bank_free[s], 4)

            def three(out, lh, ll, rh, rl, start, stop):
                pe.matmul(out, lh, rh, start=start, stop=False)
                pe.matmul(out, lh, rl, start=False, stop=False)
                return pe.matmul(out, ll, rh, start=False, stop=stop)

            def act_stationary(s, hi, lo, j, start, stop):
                for b in range(BT):
                    last = three(bank(s, b), hi[:, b * P:(b + 1) * P], lo[:, b * P:(b + 1) * P],
                                 w_hi[:, j, :], w_lo[:, j, :], start, stop)
                return last

            def weight_stationary(s, hi, lo, j, start, stop, tiles=4):
                for b in range(tiles):
                    last = three(bank(s, b), w_hi[:, j, b * P:(b + 1) * P], w_lo[:, j, b * P:(b + 1) * P],
                                 hi, lo, start, stop)
                return last

            def banks(s, value, n=4):
                pe.wait_ge(bank_free[s], value + (n - 1))

            def turn(s, b, srcs):
                for i, src in enumerate(srcs):
                    last = pe.transpose(bank(s, b)[:, i * P:(i + 1) * P], src, ident[:, :])
                last.then_inc(turned, 1)

            with pe.Fori(0, STEPS) as t:
                c0, f0, f1 = t * RAW_STEP + RING, t * (4 * SET0_STEP) + 1, t * (4 * SET1_STEP) + 1
                banks(0, f0)
                for k in range(KX):
                    pe.wait_ge(lo_done, c0 + (2 * k + 2))
                    act_stationary(0, a_hi[:, k, :], a_lo[:, k, :], k % RING, k == 0, k == KX - 1)\
                        .then_inc(chunk_used, 1)
                for m in range(1, 4):
                    s = m % 2
                    banks(s, (f0, f1)[s] + 4 * (m // 2))
                    for k in range(KX):
                        pe.wait_ge(lo_done, c0 + (2 * KX + KH * (m - 1) + k + 1))
                        act_stationary(s, a_hi[:, k, :], a_lo[:, k, :], k % RING, k == 0, k == KX - 1)\
                            .then_inc(chunk_used, 1)
                c1 = c0 + (2 * KX + 3 * KH)

                def turn_hidden(k):
                    pe.wait_ge(normed, t * (4 * BT) + BT * (k // 4 + 1))
                    pe.wait_ge(bank_free[1], f1 + (8 + k))
                    turn(1, k % 4, [hid[:, b, k * P:(k + 1) * P] for b in range(BT)])

                pe.wait_ge(consts, 4)
                for k in range(4):
                    turn_hidden(k)
                for n in range(N):
                    s = n % 2
                    banks(s, (f0 + 8, f1 + 24)[s] + 4 * (n // 2))
                    for k in range(KH):
                        if n == 0:
                            pe.wait_ge(tmp_done, t * KH + (k + 3))
                        pe.wait_ge(lo_done, c1 + (n * KH + k + 1))
                        weight_stationary(s, a_hi[:, k, :], a_lo[:, k, :], k % RING, k == 0, k == KH - 1)\
                            .then_inc(chunk_used, 1)
                        if n == 0 and k + 4 < KH:
                            turn_hidden(k + 4)
                c2 = c1 + N * KH
                for w in range(3):
                    for n in range(N):
                        s = n % 2
                        banks(s, (f0 + 16, f1 + 32)[s] + (8 * w + 4 * (n // 2)))
                        for k in range(KD):
                            if n == 0:
                                pe.wait_ge(lo_done, c2 + (KD * w + k + 1))
                            last = act_stationary(s, s_hi[:, KD * n + k, :], s_lo[:, KD * n + k, :], k,
                                                  k == 0, k == KD - 1)
                            if n == N - 1:
                                last.then_inc(chunk_used, 1)
                        if n < N - 1:
                            last.then_inc(block_done, 1)

            with pe.Fori(0, HALVES) as half:
                c0 = half * RAW_MIX + (RAW_MIX0 + RING)
                f0 = half * (4 * SET0_MIX) + (4 * STEPS * SET0_STEP + 1)
                f1 = half * (4 * SET1_MIX) + (4 * STEPS * SET1_STEP + 1)

                def product(way, s, regions, base, start, stop, chunk=None, release=True, done=None, tiles=4):
                    for k in range(KD):
                        if chunk is not None:
                            pe.wait_ge(lo_done, chunk + (k + 1))
                        hi, lo = regions
                        if way is weight_stationary:
                            last = way(s, hi[:, base + k, :], lo[:, base + k, :], k,
                                       start and k == 0, stop and k == KD - 1, tiles)
                        else:
                            last = way(s, hi[:, base + k, :], lo[:, base + k, :], k,
                                       start and k == 0, stop and k == KD - 1)
                        if release:
                            last.then_inc(chunk_used, 1)
                    if done is not None:
                        last.then_inc(done, 1)

                first, second = (a_hi, a_lo), (s_hi, s_lo)
                with pe.Fori(0, N) as n:
                    cn, g0, g1 = c0 + n * 16, f0 + n * 16, f1 + n * 12
                    for c in range(2):
                        pe.wait_ge(at_loaded, (half * (2 * N) + n * 2) * 16 + (16 * c + 16))
                        banks(0, g0 + 4 * c)
                        for k in range(KD):
                            turn(0, k, [at_in[:, b, k * P:(k + 1) * P] for b in range(BT)])
                        banks(1, g1 + 4 * c)
                        banks(0, g0 + (4 * c + 4))
                        product(weight_stationary, 1, first, 0, True, True, cn + 4 * c)
                    banks(0, g0 + 8)
                    banks(1, g1 + 8)
                    product(act_stationary, 0, first, 4, True, True, cn + 8, False, block_done)
                    product(act_stationary, 1, first, 8, True, False)
                    banks(0, g0 + 12)
                    product(act_stationary, 0, first, 8, True, True, cn + 12, False, block_done)
                    product(act_stationary, 1, first, 4, False, True)
                ct = c0 + 16 * N
                banks(1, f1 + 12 * N)
                for k in range(KX):
                    pe.wait_ge(lo_done, ct + (2 * k + 2))
                    jw, jx = 2 * k % RING, (2 * k + 1) % RING
                    for b in range(4):
                        last = three(bank(1, b), w_hi[:, jw, b * P:(b + 1) * P], w_lo[:, jw, b * P:(b + 1) * P],
                                     w_hi[:, jx, :], w_lo[:, jx, :], k == 0, k == KX - 1)
                    last.then_inc(chunk_used, 2)
                cm, e0, e1 = ct + 2 * KX, f0 + 16 * N, f1 + (12 * N + 4)
                pe.wait_ge(sup_ready, (half + 1) * BT)
                for c in range(2):
                    banks(c, (e0, e1)[c])
                    for k in range(KD):
                        turn(c, k, [ri[:, b, 0, c, k * P:(k + 1) * P] for b in range(BT)])
                banks(0, e0 + 4)
                banks(1, e1 + 4)
                product(weight_stationary, 0, first, 0, True, True, cm, False, block_done)
                product(weight_stationary, 1, first, 4, True, False)
                banks(0, e0 + 8)
                product(weight_stationary, 0, first, 4, True, True, cm + 4, False, block_done)
                product(weight_stationary, 1, first, 0, False, True)
                fh = half * 12 + STEPS * KH + 2
                pe.wait_ge(tmp_done, fh + 4)
                banks(1, e1 + 8)
                product(act_stationary, 1, second, 0, True, True, cm + 8)
                pe.wait_ge(normed, half * BT + (STEPS * 4 * BT + BT))
                banks(0, e0 + 12)
                for k in range(KD):
                    turn(0, k, [post_z[:, b, k * P:(k + 1) * P] for b in range(BT)])
                pe.wait_ge(tmp_done, fh + 8)
                banks(1, e1 + 12)
                product(weight_stationary, 1, second, 4, True, True, cm + 12)
                pe.wait_ge(tmp_done, fh + 12)
                banks(0, e0 + 16)
                product(weight_stationary, 0, second, 8, True, True, cm + 16, tiles=2)
                pe.wait_ge(h2_done, half * 2 + 2)
                for k in range(2):
                    last = pe.matmul(bank(0, 2)[0:1, :], mcols[:, MIX_COLS - 2 + k:MIX_COLS - 1 + k],
                                     hid2[:, k, :], start=(k == 0), stop=(k == 1))
                last.then_inc(block_done, 1)

        @block.vector
        def _(dve):
            dve.sem_inc(tmp_done, 2)
            for b in range(BT):
                dve.sem_inc(stored[b], 16)
            step = Count(dve_step)

            def link(ins):
                ins.then_inc(dve_step, 1)
                dve.wait_ge(dve_step, step.next())

            def low_part(lo, hi, s, b, bias):
                if bias is None:
                    ins = dve.tensor_tensor(lo, bank(s, b), hi.bitcast(F32), ALU.subtract)
                else:
                    ins = dve.scalar_tensor_tensor(out=lo, in0=bank(s, b), scalar=bias, in1=hi.bitcast(F32),
                                                   op0=ALU.add, op1=ALU.subtract)
                ins.then_inc(bank_free[s], 1)

            def norm_scales(count, var_at):
                dve.sem_inc(stats_seen, 1)
                for b in range(BT):
                    dve.bn_aggr(mv[:, b, :], stats[:, b, 0:count, :]).then_inc(var_done, 1)
                dve.wait_ge(sd_done, var_at)
                link(dve.reciprocal(ln[:, 1, :], ln[:, 0, :]))
                link(dve.scalar_tensor_tensor(out=ln[:, 2, :], in0=mv[:, :, 0], scalar=-1.0, in1=ln[:, 1, :],
                                              op0=ALU.mult, op1=ALU.mult))

            STEP_LINKS = 2
            with dve.Fori(0, STEPS) as t:
                step.at(t * STEP_LINKS)
                f = (t * (4 * SET0_STEP) + 4, t * (4 * SET1_STEP) + 4)
                u0 = t * USE_STEP + RING
                dve.wait_ge(rows_loaded, t * 16 + 32)
                dve.wait_ge(cols_loaded, t * 16 + 32)
                for m in range(4):
                    s = m % 2
                    dve.wait_ge(chunk_used, u0 + KX * (m + 1))
                    for b in range(BT):
                        dve.tensor_tensor(hid[:, b, m * 512:(m + 1) * 512], bank(s, b),
                                          rows[:, m * 512:(m + 1) * 512], ALU.add).then_inc(bank_free[s], 1)
                    for b in range(BT):
                        dve.wait_ge(bank_free[s], f[s] + (4 * (m // 2) + b + 1))
                        dve.bn_stats(stats[:, b, m, :], hid[:, b, m * 512:(m + 1) * 512]).then_inc(stats_done, 1)
                dve.wait_ge(stats_done, (t + 1) * (4 * BT))
                norm_scales(4, t + 1)
                for m in range(4):
                    for b in range(BT):
                        part = hid[:, b, m * 512:(m + 1) * 512]
                        dve.tensor_scalar(part, part, ln[:, 1, b:b + 1], ln[:, 2, b:b + 1], ALU.mult, ALU.add)\
                            .then_inc(normed, 1)
                for k in range(KH):
                    dve.wait_ge(bank_free[1], f[1] + (8 + k + 1))
                    dve.tensor_tensor(a_lo[:, k, :], gf[:, k % 2, :], a_hi[:, k, :].bitcast(F32), ALU.subtract)\
                        .then_inc(tmp_done, 1)
                for n in range(N):
                    for b in range(KD):
                        dve.wait_ge(h_done, t * (N * KD) + (KD * n + b + 1))
                        low_part(s_lo[:, KD * n + b, :], s_hi[:, KD * n + b, :], n % 2, b,
                                 cols[:, 2 * KH + KD * n + b:2 * KH + KD * n + b + 1])
                u2 = u0 + (4 * KH + N * KH)
                for w in range(3):
                    for n in range(N):
                        s = n % 2
                        if n < N - 1:
                            dve.wait_ge(block_done, t * 9 + (3 * w + n + 1))
                        else:
                            dve.wait_ge(chunk_used, u2 + KD * (w + 1))
                        for b in range(BT):
                            dve.wait_ge(stored[b], t * (16 * 3 * N) + 16 * (4 * w + n + 1))
                            dve.tensor_tensor(stage[:, b, :], bank(s, b), rows[:, HID + D * w:HID + D * (w + 1)],
                                              ALU.add).then_inc(bank_free[s], 1)

            dve.sem_inc(scored, 2 * N)
            dve.sem_inc(weighed, 4)
            for par in range(2):
                dve.sem_inc(ao_stored[par], 32)
            step0 = STEPS * STEP_LINKS
            ATT_LINKS = G * 2 + 9
            with dve.Fori(0, BATCH // P) as it:
                step.at(it * ATT_LINKS + step0)
                made = Count(products, it * (G * (N + 2)))
                dve.wait_ge(weighed, it * (2 * G) + 4)
                for g in range(G):
                    par = g % 2
                    Q, K = qk[:, par, 0], qk[:, par, 1]
                    dve.wait_ge(qk_loaded[par], it * 128 + (64 * (g // 2) + 64))
                    dve.tensor_tensor(Q[:, 2], Q[:, 0], Q[:, 1], ALU.add).then_inc(dve_step, 1)
                    step.next()
                    link(dve.tensor_tensor(K[:, 2], K[:, 0], K[:, 1], ALU.subtract))

                    def multiply(n):
                        out = prod[:, 2048 * (n % 2):2048 * (n % 2) + 1536].rearrange("p (x m d) -> p x m d", x=3, m=N)
                        q_ = Q[:, :, n:n + 1, :].broadcast_to([P, 3, N, P])
                        dve.wait_ge(scored, it * (G * N) + (N * g + n + 7))
                        dve.tensor_tensor(out, q_, K, ALU.mult).then_inc(products, 1)
                        return made.next()

                    def reduce(n, at):
                        dve.wait_ge(products, at)
                        src = prod[:, 2048 * (n % 2):2048 * (n % 2) + 1536].rearrange("p (a d) -> p a d", d=HD)
                        ins = dve.tensor_reduce(dots[:, g, n, :, :].rearrange("p x m -> p (x m)"), src, AX_X, ALU.add)
                        ins.then_inc(scored, 1)

                    ready = multiply(0)
                    for n in range(N):
                        following = multiply(n + 1) if n < N - 1 else None
                        reduce(n, ready)
                        ready = following
                dve.wait_ge(scored, it * (G * N) + (G * N + 2 * N))
                pr, pi, pm = (dots[:, :, :, x, :].rearrange("p g n m -> p (g n) m") for x in range(3))
                A = [sm[:, i, :, :] for i in range(6)]
                link(dve.tensor_tensor(A[3], pr, pi, ALU.add))
                link(dve.tensor_tensor(A[4], pm, pr, ALU.subtract))
                link(dve.tensor_tensor(A[4], A[4], pi, ALU.add))
                link(dve.tensor_tensor(A[3], A[3], A[3], ALU.mult))
                link(dve.tensor_tensor(A[4], A[4], A[4], ALU.mult))
                dve.scalar_tensor_tensor(out=A[1], in0=A[3], scalar=EPS, in1=A[4], op0=ALU.add, op1=ALU.add)\
                    .then_inc(mag_in, 1)
                dve.wait_ge(mag_out, it + 1)
                heads = lambda a: a.rearrange("p g (m h) -> p g h m", h=2)
                over = lambda a: a.rearrange("p g (m h) -> p g m h", h=2)
                spread = lambda a: a[:, :, None, :].broadcast_to([P, G * N, N, 2])
                link(dve.tensor_reduce(mx[:, 0], heads(A[0]), AX_X, ALU.max))
                dve.tensor_tensor(over(A[1]), over(A[0]), spread(mx[:, 0]), ALU.subtract).then_inc(exp_in, 1)
                dve.wait_ge(exp_out, it + 1)
                link(dve.tensor_reduce(mx[:, 1], heads(A[2]), AX_X, ALU.add))
                link(dve.reciprocal(mx[:, 0], mx[:, 1]))
                link(dve.tensor_tensor(over(A[5]), over(A[2]), spread(mx[:, 0]), ALU.mult))
                for g in range(G):
                    par = g % 2
                    dve.wait_ge(v_loaded[par], it * 64 + (32 * (g // 2) + 32))
                    dve.wait_ge(ao_stored[par], it * 64 + (32 * (g // 2) + 32))
                    w_ = A[5][:, N * g:N * g + N, :, None].broadcast_to([P, N, 8, HD])
                    for c in range(2):
                        v_ = vv[:, par, c].rearrange("p m (h d) -> p (m h) d", d=HD)[:, None, :, :]\
                            .broadcast_to([P, N, 8, HD])
                        out = prod[:, 2048 * c:2048 * c + 2048].rearrange("p (n a d) -> p n a d", n=N, a=8)
                        dve.wait_ge(weighed, it * (2 * G) + (2 * g + c + 3))
                        dve.tensor_tensor(out, w_, v_, ALU.mult).then_inc(products, 1)
                    for c in range(2):
                        dve.wait_ge(products, made.next())
                        src = prod[:, 2048 * c:2048 * c + 2048].rearrange("p (n m e) -> p n e m", n=N, m=N)
                        dve.tensor_reduce(ao[:, par, c, :, :], src, AX_X, ALU.add).then_inc(weighed, 1)
                assert step.n == ATT_LINKS

            dve.wait_ge(gathered, 16 * N * BATCH // P)
            dve.sem_inc(ph_free, 2)
            step0 = step0 + ATT_LINKS * (BATCH // P)
            MIX_LINKS = 1 + 2 * BT * 13 + BT + 4 + 2
            with dve.Fori(0, HALVES) as half:
                step.at(half * MIX_LINKS + step0)
                u0 = half * RAW_MIX + (USE_MIX0 + RING)
                h0 = half * (16 * N + 16) + STEPS * N * KD
                d0 = half * (2 * N + 3) + 9 * STEPS
                f0 = half * (4 * SET0_MIX) + (4 * STEPS * SET0_STEP + 4)
                f1 = half * (4 * SET1_MIX) + (4 * STEPS * SET1_STEP + 4)
                dve.tensor_copy(sh[:, :, :], strength[:, bass.ds(half * BT, BT), :, :]
                                .rearrange("p b i j -> p b (i j)")).then_inc(dve_step, 1)
                step.next()
                with dve.Fori(0, N) as n:
                    for c in range(2):
                        for k in range(KD):
                            dve.wait_ge(h_done, h0 + n * 16 + (8 * c + k + 1))
                            low_part(a_lo[:, k, :], a_hi[:, k, :], 0, k, None)
                        for k in range(KD):
                            dve.wait_ge(h_done, h0 + n * 16 + (8 * c + k + 5))
                            low_part(a_lo[:, 4 + 4 * c + k, :], a_hi[:, 4 + 4 * c + k, :], 1, k,
                                     mcols[:, KD * c + k:KD * c + k + 1])
                    dve.wait_ge(block_done, d0 + n * 2 + 2)
                    for b in range(BT):
                        dve.tensor_tensor(ri[:, b, 0, n, :], ri[:, b, 0, n, :], bank(0, b), ALU.subtract)\
                            .then_inc(bank_free[0], 1)

                off = {1: 0, 2: 3, 3: 5}

                def pair(i, j):
                    return off[abs(i - j)] + min(i, j)

                for u in range(2 * BT):
                    bt, f = u // 2, u % 2
                    uh = half * (2 * BT) + u
                    buf = lambda a, b: ph[:, u % 2, a:b].rearrange("p (n d) -> p n d", d=256)
                    m0, m1, ur, ui = (buf(1024 * i, 1024 * i + 1024) for i in range(4))
                    cc, ww = buf(4096, 5632), buf(5632, 6656)
                    R, I = (ri[:, bt, c, :, 256 * f:256 * f + 256] for c in range(2))
                    dve.wait_ge(squares, uh * 2 + 2)
                    dve.tensor_tensor(m0, m0, m1, ALU.add).then_inc(sq_sum, 1)
                    dve.wait_ge(roots, uh + 1)
                    link(dve.tensor_scalar(m0, m0, 0.0, None, ALU.is_equal))
                    link(dve.tensor_tensor(m1, m1, m0, ALU.add))
                    link(dve.reciprocal(m1, m1))
                    dve.tensor_tensor(ur, R, m1, ALU.mult).then_inc(dve_step, 1)
                    step.next()
                    link(dve.tensor_tensor(ui, I, m1, ALU.mult))
                    second = {1: ww[:, 0:3], 2: m1[:, 0:2], 3: m1[:, 2:3]}
                    for d in (1, 2, 3):
                        dve.tensor_tensor(cc[:, off[d]:off[d] + N - d], ur[:, 0:N - d], ur[:, d:N], ALU.mult)
                        ins = dve.tensor_tensor(second[d], ui[:, 0:N - d], ui[:, d:N], ALU.mult)
                    link(ins)
                    for more in (second, {d: m0[:, 0:N - d] for d in off}, {d: m0[:, d:N] for d in off}):
                        for d in (1, 2, 3):
                            c_ = cc[:, off[d]:off[d] + N - d]
                            ins = dve.tensor_tensor(c_, c_, more[d], ALU.add)
                        link(ins)
                    s_ = lambda i, j: sh[:, bt, N * i + j:N * i + j + 1]
                    for r in range(N - 1):
                        for j in range(N):
                            i = [i for i in range(N) if i != j][r]
                            if r == 0:
                                ins = dve.tensor_scalar(ww[:, j], cc[:, pair(i, j)], s_(i, j), s_(j, j),
                                                        ALU.mult, ALU.add)
                            else:
                                ins = dve.scalar_tensor_tensor(out=ww[:, j], in0=cc[:, pair(i, j)],
                                                               scalar=s_(i, j), in1=ww[:, j],
                                                               op0=ALU.mult, op1=ALU.add)
                        link(ins)
                    dve.tensor_tensor(ur, ww, R, ALU.mult)
                    link(dve.tensor_tensor(ui, ww, I, ALU.mult))
                    for c, x in ((0, ur), (1, ui)):
                        ins = dve.tensor_reduce(ri[:, bt, 0, c, 256 * f:256 * f + 256],
                                                x.rearrange("p n d -> p d n"), AX_X, ALU.add)
                    ins.then_inc(ph_free, 1)
                for bt in range(BT):
                    hb = half * BT + bt
                    dve.wait_ge(sup_sq, hb * 2 + 2)
                    dve.tensor_tensor(nrm[:, 2:3], nrm[:, 0:1], nrm[:, 1:2], ALU.add).then_inc(sup_sum, 1)
                    dve.wait_ge(sup_root, hb + 1)
                    link(dve.reciprocal(nrm[:, 4:5], nrm[:, 3:4]))
                    sup = ri[:, bt, 0, 0:2, :]
                    dve.tensor_scalar(sup, sup, nrm[:, 4:5], None, ALU.mult).then_inc(sup_ready, 1)
                u1 = u0 + (16 * N + 2 * KX)
                dve.wait_ge(chunk_used, u1)
                for k in range(4):
                    dve.tensor_scalar(top_part[:, k, :], bank(1, k), mcols[:, 4 * KD + k:4 * KD + k + 1], None,
                                      ALU.add).then_inc(bank_free[1], 1)
                for c in range(2):
                    for k in range(KD):
                        dve.wait_ge(h_done, h0 + (16 * N + 4 * c + k + 1))
                        low_part(a_lo[:, 4 * c + k, :], a_hi[:, 4 * c + k, :], c, k, None)
                dve.wait_ge(block_done, d0 + (2 * N + 2))
                e0, e1 = f0 + 16 * N, f1 + 12 * N
                for k in range(4):
                    dve.tensor_tensor(meas_r[:, k, :], meas_r[:, k, :], bank(0, k), ALU.subtract)\
                        .then_inc(bank_free[0], 1)
                for k in range(4):
                    dve.wait_ge(bank_free[0], e0 + (8 + k + 1))
                    ins = dve.tensor_tensor(meas_r[:, k, :], meas_r[:, k, :], meas_r[:, k, :], ALU.mult)
                    ins.then_inc(dve_step, 1)
                    step.next()
                for k in range(4):
                    dve.wait_ge(dve_step, step.start + (step.n - 3 + k))
                    dve.wait_ge(bank_free[1], e1 + (8 + k + 1))
                    dve.tensor_tensor(meas_r[:, k, :], meas_r[:, k, :], meas_q[:, k, :], ALU.add)\
                        .then_inc(amp_in, 1)
                for k in range(4):
                    dve.wait_ge(h_done, h0 + (16 * N + 8 + k + 1))
                    dve.tensor_tensor(s_lo[:, k, :], gf[:, k % 2, :], s_hi[:, k, :].bitcast(F32), ALU.subtract)\
                        .then_inc(tmp_done, 1)
                dve.wait_ge(chunk_used, u1 + 3 * KD)
                for b in range(BT):
                    dve.tensor_tensor(post_z[:, b, :], bank(1, b), prow[:, :], ALU.add).then_inc(bank_free[1], 1)
                for b in range(BT):
                    dve.wait_ge(bank_free[1], e1 + (12 + b + 1))
                    dve.bn_stats(stats[:, b, 0, :], post_z[:, b, :]).then_inc(stats_done, 1)
                dve.wait_ge(stats_done, half * BT + (4 * BT * STEPS + BT))
                norm_scales(1, half + (STEPS + 1))
                for b in range(BT):
                    dve.tensor_scalar(post_z[:, b, :], post_z[:, b, :], ln[:, 1, b:b + 1], ln[:, 2, b:b + 1],
                                      ALU.mult, ALU.add).then_inc(normed, 1)
                for k in range(KD):
                    dve.wait_ge(bank_free[0], e0 + (12 + k + 1))
                    dve.tensor_tensor(s_lo[:, 4 + k, :], gf[:, k % 2, :], s_hi[:, 4 + k, :].bitcast(F32),
                                      ALU.subtract).then_inc(tmp_done, 1)
                dve.wait_ge(chunk_used, u1 + 4 * KD)
                for k in range(4):
                    dve.tensor_tensor(post_z[:, k, :], bank(1, k), top_part[:, k, :], ALU.add)\
                        .then_inc(bank_free[1], 1)
                for k in range(4):
                    dve.wait_ge(h_done, h0 + (16 * N + 12 + k + 1))
                    dve.tensor_tensor(s_lo[:, 8 + k, :], gf[:, k % 2, :], s_hi[:, 8 + k, :].bitcast(F32),
                                      ALU.subtract).then_inc(tmp_done, 1)
                dve.wait_ge(chunk_used, u1 + 5 * KD)
                for k in range(2):
                    dve.tensor_scalar(hid2[:, k, :], bank(0, k), mcols[:, 4 * KD + 4 + k:4 * KD + 5 + k], 0.0,
                                      ALU.add, ALU.max).then_inc(h2_done, 1)
                dve.wait_ge(block_done, d0 + (2 * N + 3))
                dve.tensor_copy(y_sb[:, bass.ds(half * HALF, HALF)], bank(0, 2)[0:1, :]).then_inc(bank_free[0], 4)
                assert step.n == MIX_LINKS, step.n


def kernel(**inputs):
    import numpy as np
    import concourse.bacc as bacc
    from concourse.bass_utils import run_bass_kernel_spmd

    a = {k: np.asarray(v) for k, v in inputs.items()}
    L = {k[len("L0_rec_"):]: v for k, v in a.items() if k.startswith("L0_rec_")}

    def chunks(w):
        k, n = w.shape
        return w.reshape(k // P, P, n // 512, 512).transpose(2, 0, 1, 3).reshape(-1, P, 512)

    def column(v):
        return v.reshape(-1, P).T

    def encoder(t, c):
        return np.concatenate([chunks(L[f"{t}_W1"].T), chunks(L[f"{t}_W2"].T)]
                              + [chunks(L[f"W{w}_{c}"].T) for w in "qkv"])

    arrays = {
        "enc_w": np.stack([encoder("er", "r"), encoder("ei", "i")]),
        "xs": a["r_x"].T.reshape(KX, P, HALVES, HALF).transpose(2, 0, 1, 3),
        "enc_rows": np.stack([np.concatenate([L[f"{t}_b1"]] + [L[f"b{w}_{c}"] for w in "qkv"])[None]
                              for t, c in (("er", "r"), ("ei", "i"))]),
        "enc_cols": np.stack([np.concatenate([column(L[f"{t}_{v}"]) for v in ("g1", "be1", "b2")], 1)
                              for t in ("er", "ei")]),
        "wo": np.stack([chunks(L[f"Wo_{c}"].T) for c in "ri"]),
        "int_w": np.stack([np.stack([chunks(L[f"int_W{c}"][n].T) for c in "ri"]) for n in range(N)]),
        "post_w": np.stack([chunks(L[w].T) for w in ("meas_Mr", "meas_Mi", "post_W")]),
        "top1": chunks(a["W_top1"]),
        "top2": a["W_top2"].reshape(KD, P, 256),
        "mix_cols": np.concatenate([column(L["bo_r"]), column(L["bo_i"]), column(L["post_g"]),
                                    column(L["post_be"]), column(a["b_top1"]), column(a["b_top2"]),
                                    column(a["W_top3"][:, 0])], 1),
        "post_row": L["post_b"][None],
        "ids": a["ids"].reshape(BATCH // P, P, N).transpose(1, 0, 2).reshape(P, -1),
        "tbl_0": a["tbl_0"], "tbl_1": a["tbl_1"], "tbl_2": a["tbl_2"], "tbl_3": a["tbl_3"],
    }
    nc = bacc.Bacc("TRN2", target_bir_lowering=False, num_devices=1)
    args = {}
    for name, x in arrays.items():
        arrays[name] = np.ascontiguousarray(x)
        args[name] = nc.dram_tensor(name, x.shape, I32 if name == "ids" else F32, kind="ExternalInput").ap()
    y = nc.dram_tensor("y", (BATCH, 1), F32, kind="ExternalOutput").ap()
    tables = [args.pop(f"tbl_{i}") for i in range(N)]
    build(nc, tables=tables, y=y, **args)
    r = run_bass_kernel_spmd(nc, [arrays], core_ids=[0])
    return r.results[0]["y"]
```

```python
from contextlib import ExitStack

import concourse.bass as bass
from concourse import mybir

F32 = mybir.dt.float32
F32R = mybir.dt.float32r
I32 = mybir.dt.int32
U32 = mybir.dt.uint32
ALU = mybir.AluOpType
ACT = mybir.ActivationFunctionType
AX_X = mybir.AxisListType.X

P = 128
BATCH, IN, HID, D, N, OUT, TOP = 1024, 2048, 2048, 512, 4, 512, 512
HEADS, HD = 8, 64
HALF = 512
HALVES = BATCH // HALF
BT = HALF // P
KX = IN // P
KH = HID // P
KD = D // P
STEPS = 2 * HALVES
RING = 4
G = 4
LN_EPS = 1e-5
EPS = 1e-8
SCALE = HD ** -0.5

RAW_STEP = KX + 4 * KH + N * KH + 3 * KD
USE_STEP = 4 * KH + N * KH + 3 * KD
SET0_STEP = 2 + 2 + 6
SET1_STEP = 2 + 4 + 2 + 6
RAW_MIX = N * 4 * KD + 2 * KX + 3 * KD + KD + 4
RAW_MIX0 = STEPS * RAW_STEP
USE_MIX0 = STEPS * USE_STEP
SET0_MIX, SET1_MIX = 4 * N + 5, 3 * N + 5

ENC_COLS = 3 * KH
MIX_COLS = 2 * KD + 2 * KD + 4 + 2 + 2


class Count:

    def __init__(self, sem, start=0):
        self.sem, self.start, self.n = sem, start, 0

    def at(self, start):
        self.start, self.n = start, 0

    def next(self):
        self.n += 1
        return self.start + self.n

    @property
    def now(self):
        return self.start + self.n


def build(nc, enc_w, xs, enc_rows, enc_cols, wo, int_w, post_w, top1, top2, mix_cols, post_row,
          ids, tables, y):
    ctx = ExitStack()
    with ctx:
        def sem(name):
            return ctx.enter_context(nc.semaphore(name))

        address = [(nc.sbuf_base + 31) // 32 * 32]

        def place(name, shape, dtype, offset=None):
            size = 4
            for d in shape[1:]:
                size *= d
            if offset is None:
                offset = address[0]
                address[0] += (size + 31) // 32 * 32
            return nc.alloc_sbuf_tensor_at(name, shape, dtype, offset=offset)

        a0 = address[0]
        a_hi = place("a_hi", [P, 16, HALF], F32R)
        a_lo = place("a_lo", [P, 16, HALF], F32R)
        s0 = address[0]
        s_hi = place("s_hi", [P, 16, HALF], F32R)
        s_lo = place("s_lo", [P, 16, HALF], F32R)
        hid = place("hid", [P, BT, HID], F32, s0)
        KB = 1024
        at_in = place("at_in", [P, BT, D], F32, a0 + 24 * KB)
        ph = place("ph", [P, 2, 6656], F32, a0)
        top_part = place("top_part", [P, 4, HALF], F32, a0 + 56 * KB)
        meas_r = place("meas_r", [P, 4, HALF], F32, a0 + 24 * KB)
        meas_q = place("meas_q", [P, 4, HALF], F32, a0 + 16 * KB)
        post_z = place("post_z", [P, BT, OUT], F32, a0 + 24 * KB)
        ri = place("ri", [P, BT, 2, N, D], F32, s0)
        hid2 = place("hid2", [P, 2, HALF], F32, s0 + 56 * KB)
        qk = place("qk", [P, 2, 3, N, P], F32)
        vv = place("vv", [P, 2, N, P], F32)
        prod = place("prod", [P, 3 * N * P], F32)
        pv = place("pv", [P, N * P], F32)
        pv2 = place("pv2", [P, 2 * P], F32)
        ao = place("ao", [P, 2, N, P], F32)
        dots = place("dots", [P, G, N, 3, 8], F32)
        sm = place("sm", [P, 5, G * N, 8], F32)

        raw = place("raw", [P, RING, 512], F32)
        w_hi = place("w_hi", [P, RING, 512], F32R)
        w_lo = place("w_lo", [P, RING, 512], F32R)
        gf = place("gf", [P, 2, HALF], F32)
        rows = place("rows", [P, HID], F32)
        stage = place("stage", [P, BT, D], F32)
        cols = place("cols", [P, ENC_COLS], F32)
        mcols = place("mcols", [P, MIX_COLS], F32)
        prow, y_sb = rows[:, 0:OUT], rows[0:1, OUT:OUT + BATCH]
        ident = place("ident", [P, P], F32)
        stats = place("stats", [P, BT, 4, 6], F32)
        mv = place("mv", [P, BT, 2], F32)
        ln = place("ln", [P, 3, BT], F32)
        epsc = place("epsc", [P, 2], F32)
        mx = place("mx", [P, 2, G * N, 2], F32)
        nrm = place("nrm", [P, 8], F32)
        ids_sb = place("ids_sb", [P, 8 * N], I32)
        strength = place("strength", [P, 8, N, N], F32)
        sh = place("sh", [P, BT, N * N], F32)

        ps = ctx.enter_context(nc.psum_tensor("ps", [P, 8, 512], F32))

        qkv = nc.dram_tensor("qkv_scratch", [STEPS, 3, N, BT, P, D], F32).ap()
        att = nc.dram_tensor("att_scratch", [HALVES, 2, N, BT, P, D], F32).ap()

        raw_loaded = [sem(f"raw_loaded{j}") for j in range(RING)]
        hi_done = sem("hi_done")
        lo_done = sem("lo_done")
        chunk_used = sem("chunk_used")
        block_done = sem("block_done")
        turned = sem("turned")
        bank_free = [sem("banks0_free"), sem("banks1_free")]
        h_done = sem("h_done")
        rows_loaded, cols_loaded = sem("rows_loaded"), sem("cols_loaded")
        consts = sem("consts")
        stats_seen = sem("stats_seen")
        stats_done, var_done, sd_done, rstd_done = sem("stats_done"), sem("var_done"), sem("sd_done"), sem("rstd_done")
        normed = sem("normed")
        tmp_done = sem("tmp_done")
        stored = [sem(f"stored{j}") for j in range(BT)]
        qk_loaded, v_loaded = sem("qk_loaded"), sem("v_loaded")
        products = sem("products")
        scored = sem("scored")
        weights_done = sem("weights_done")
        pv_step = sem("pv_step")
        ao_stored = sem("ao_stored")
        dve_step = sem("dve_step")
        mag_in, mag_out, exp_in, exp_out = sem("mag_in"), sem("mag_out"), sem("exp_in"), sem("exp_out")
        at_loaded = sem("at_loaded")
        squares, sq_sum, roots, ph_free = sem("squares"), sem("sq_sum"), sem("roots"), sem("ph_free")
        sup_sq, sup_sum, sup_root, sup_ready = sem("sup_sq"), sem("sup_sum"), sem("sup_root"), sem("sup_ready")
        ids_loaded, gathered = sem("ids_loaded"), sem("gathered")
        amp_in = sem("amp_in")
        h2_done, y_stored = sem("h2_done"), sem("y_stored")

        bank = lambda s, b: ps[:, 4 * s + b, :]
        block = ctx.enter_context(nc.Block())

        @block.sync
        def _(sp):
            def load(chunk, j, src, cols_=512):
                sp.wait_ge(lo_done, chunk + 1)
                sp.dma_start(raw[:, j, 0:cols_], src).then_inc(raw_loaded[j], 16)

            def item_qk(t0, bt, g, it):
                sp.wait_ge(products, it * (G * N) + (N * g + N))
                for w in range(2):
                    for c in range(2):
                        sp.dma_start(qk[:, w, c, :, :], heads_of(qkv[t0 + c, w, :, bt], g)).then_inc(qk_loaded, 16)

            def item_v(t0, bt, g):
                for c in range(2):
                    sp.dma_start(vv[:, c, :, :], heads_of(qkv[t0 + c, 2, :, bt], g)).then_inc(v_loaded, 16)

            def item_out(half, bt, g, it):
                sp.wait_ge(pv_step, it * (G * 24) + (24 * g + 27))
                for c in range(2):
                    sp.dma_start(heads_of(att[half, c, :, bt], g), ao[:, c, :, :]).then_inc(ao_stored, 16)

            def heads_of(x, g):
                return x[:, :, g * P:(g + 1) * P].rearrange("n p d -> p n d")

            def step_start(c0, half, enc):
                with sp.Fori(0, KX // 2) as q:
                    for j in range(RING):
                        k = q * 2 + j // 2
                        src = xs[half, k] if j % 2 == 0 else enc_w[enc, k]
                        load(c0 + q * RING + j, j, src)

            def step_quads(c0, enc, first, last):
                with sp.Fori(first, last) as q:
                    for j in range(RING):
                        load(c0 + 2 * KX + q * RING + j, j, enc_w[enc, q * RING + (KX + j)])

            QUADS = (USE_STEP - KX) // RING
            with sp.Fori(0, 2) as t:
                step_start(t * RAW_STEP, 0, t)
                step_quads(t * RAW_STEP, t, 0, QUADS)
            for b in range(BT):
                sp.wait_ge(stored[b], 16 * 2 * 3 * N + 16)
            with sp.Fori(0, 2) as e:
                c0, i0, i1 = e * RAW_STEP + 2 * RAW_STEP, e * 2, e * 2 + 1
                item_qk(0, i0, 0, i0)
                step_start(c0, 1, e)
                at = 0

                def quads_to(q):
                    nonlocal at
                    step_quads(c0, e, at, q)
                    at = q

                for q, it, g in ((2, i0, 1), (5, i0, 2), (7, i0, 3), (9, i1, 0)):
                    quads_to(q)
                    item_qk(0, it, g, it)
                quads_to(13)
                item_v(0, i0, 0)
                item_qk(0, i1, 1, i1)
                quads_to(17)
                item_out(0, i0, 0, i0)
                item_v(0, i0, 1)
                quads_to(18)
                item_qk(0, i1, 2, i1)
                quads_to(20)
                item_qk(0, i1, 3, i1)
                quads_to(21)
                item_out(0, i0, 1, i0)
                item_v(0, i0, 2)
                quads_to(25)
                item_out(0, i0, 2, i0)
                item_v(0, i0, 3)
                quads_to(29)
                item_out(0, i0, 3, i0)
                item_v(0, i1, 0)
                quads_to(30)
                for g in range(2):
                    item_out(0, i1, g, i1)
                    item_v(0, i1, g + 1)
                quads_to(31)
                item_out(0, i1, 2, i1)
                item_v(0, i1, 3)
                item_out(0, i1, 3, i1)

            for b in range(BT):
                sp.wait_ge(stored[b], 16 * STEPS * 3 * N + 16)
            item_qk(2, 0, 0, BT)

            def mix_quads(c0, n, qs):
                for q in qs:
                    for j in range(RING):
                        src = wo[q, j] if q < 2 else int_w[n, q - 2, j]
                        load(c0 + n * 16 + (4 * q + j), j, src)

            def mix_rest(c0, half, before_mi=None):
                c0 = c0 + 16 * N
                with sp.Fori(0, KX // 2) as q:
                    for j in range(RING):
                        k = q * 2 + j // 2
                        src = top1[k + KD] if j % 2 == 0 else xs[half, k]
                        load(c0 + q * RING + j, j, src)
                c0 = c0 + 2 * KX
                for q in range(3):
                    for j in range(RING):
                        load(c0 + (4 * q + j), j, post_w[q, j])
                    if q == 0 and before_mi:
                        before_mi()
                for j in range(RING):
                    load(c0 + (12 + j), j, top1[j])
                for j in range(RING):
                    load(c0 + (16 + j), j, top2[j], 256)

            def mix_stream(n, values):
                it = n + BT
                if values:
                    item_v(2, n - 1, 0)
                mix_quads(RAW_MIX0, n, (0, 1))
                if values:
                    item_out(1, n - 1, 0, it - 1)
                    item_v(2, n - 1, 1)
                mix_quads(RAW_MIX0, n, (2,))
                item_qk(2, n, 1, it)
                if values:
                    item_out(1, n - 1, 1, it - 1)
                    item_v(2, n - 1, 2)
                mix_quads(RAW_MIX0, n, (3,))
                item_qk(2, n, 2, it)
                item_qk(2, n, 3, it)
                if values:
                    item_out(1, n - 1, 2, it - 1)
                    item_v(2, n - 1, 3)

            mix_stream(0, False)
            with sp.Fori(1, N) as n:
                item_qk(2, n, 0, n + BT)
                mix_stream(n, True)
                item_out(1, n - 1, 3, n + (BT - 1))

            def last_values():
                for g in range(G):
                    item_v(2, BT - 1, g)
                    item_out(1, BT - 1, g, 2 * BT - 1)

            mix_rest(RAW_MIX0, 0, last_values)
            with sp.Fori(0, N) as n:
                mix_quads(RAW_MIX0 + RAW_MIX, n, range(4))
            mix_rest(RAW_MIX0 + RAW_MIX, 1)

        @block.gpsimd
        def _(pool):
            pool.memset(ident[:, :], 0.0).then_inc(consts, 1)
            pool.memset(epsc[:, 0:1], LN_EPS).then_inc(consts, 1)
            pool.memset(epsc[:, 1:2], EPS).then_inc(consts, 1)
            pool.wait_ge(consts, 3)
            pool.affine_select(out=ident[:, :], in_=ident[:, :], compare_op=ALU.not_equal, fill=1.0,
                               base=0, pattern=[[-1, P]], channel_multiplier=1).then_inc(consts, 1)

            def low(chunk, j, hi, lo, width=512):
                pool.wait_ge(hi_done, chunk + 1)
                pool.tensor_tensor(lo, raw[:, j, 0:width], hi.bitcast(F32), ALU.subtract)\
                    .then_inc(lo_done, 1)

            def lows(chunk):
                for j in range(RING):
                    low(chunk + j, j, w_hi[:, j, :], w_lo[:, j, :])

            def step_start(c0):
                for k in range(KX):
                    low(c0 + 2 * k, 2 * k % RING, a_hi[:, k, :], a_lo[:, k, :])
                    low(c0 + (2 * k + 1), (2 * k + 1) % RING, w_hi[:, k % RING, :], w_lo[:, k % RING, :])

            def step_quads(c0, first, last):
                with pool.Fori(first, last) as q:
                    lows(c0 + 2 * KX + q * RING)

            def value(it, g, r):
                c, n = r // N, r % N
                if r == 0:
                    pool.wait_ge(weights_done, it + 1)
                    pool.wait_ge(v_loaded, it * (32 * G) + (32 * g + 32))
                    pool.wait_ge(ao_stored, it * (32 * G) + (32 * g + 32))
                done = Count(pv_step, it * (24 * G) + (24 * g + 3 * r))
                pool.wait_ge(pv_step, done.now + 3)
                pool.tensor_tensor(pv[:, :].rearrange("p (a d) -> p a d", d=HD),
                                   sm[:, 4, N * g + n, :, None].broadcast_to([P, 8, HD]),
                                   vv[:, c].rearrange("p m (h d) -> p (m h) d", d=HD), ALU.mult).then_inc(pv_step, 1)
                pool.wait_ge(pv_step, done.next() + 3)
                pool.tensor_tensor(pv2[:, :], pv[:, 0:2 * P], pv[:, 2 * P:4 * P], ALU.add).then_inc(pv_step, 1)
                pool.wait_ge(pv_step, done.next() + 3)
                pool.tensor_tensor(ao[:, c, n, :], pv2[:, 0:P], pv2[:, P:2 * P], ALU.add).then_inc(pv_step, 1)

            def values(it, g):
                for r in range(8):
                    value(it, g, r)

            QUADS = (USE_STEP - KX) // RING
            with pool.Fori(0, 2) as t:
                step_start(t * RAW_STEP)
                step_quads(t * RAW_STEP, 0, QUADS)

            pool.wait_ge(ids_loaded, 16)
            for b in range(BATCH // P):
                for f in range(N):
                    pool.indirect_dma_start(
                        strength[:, b, f, :], None, tables[f],
                        bass.IndirectOffsetOnAxis(ap=ids_sb[:, N * b + f:N * b + f + 1].bitcast(U32), axis=0))\
                        .then_inc(gathered, 16)

            with pool.Fori(0, 2) as e:
                c0, i0, i1 = e * RAW_STEP + 2 * RAW_STEP, e * 2, e * 2 + 1
                step_start(c0)
                step_quads(c0, 0, 12)
                for g in range(G):
                    r = 0
                    for q in range(12 + 4 * g, 16 + 4 * g):
                        for j in range(RING):
                            low(c0 + (2 * KX + q * RING + j), j, w_hi[:, j, :], w_lo[:, j, :])
                            if q % 4 and j < 3 and r < 8:
                                value(i0, g, r)
                                r += 1
                cq = c0 + (2 * KX + 28 * RING)
                lows(cq)
                values(i1, 0)
                lows(cq + RING)
                values(i1, 1)
                values(i1, 2)
                lows(cq + 2 * RING)
                values(i1, 3)

            for q in range(4):
                lows(RAW_MIX0 + q * RING)
            with pool.Fori(1, N) as n:
                for q in range(4):
                    lows(n * 16 + (RAW_MIX0 + q * RING))
                    values(n + (BT - 1), q)
            with pool.Fori(4 * N, 4 * N + 2 * KX // RING + 1) as q:
                lows(q * RING + RAW_MIX0)
            for g in range(G):
                values(2 * BT - 1, g)

            def mix_end(c0, first):
                with pool.Fori(first, (RAW_MIX - 4) // RING) as q:
                    lows(q * RING + c0)
                for j in range(RING):
                    low(c0 + (RAW_MIX - 4 + j), j, w_hi[:, j, 0:256], w_lo[:, j, 0:256], 256)

            mix_end(RAW_MIX0, 4 * N + 2 * KX // RING + 1)
            mix_end(RAW_MIX0 + RAW_MIX, 0)

        @block.scalar
        def _(act):
            act.sem_inc(lo_done, RING)
            act.sem_inc(ao_stored, 32)
            act.dma_start(ids_sb[:, :], ids).then_inc(ids_loaded, 16)
            act.dma_start(mcols[:, :], mix_cols).then_inc(cols_loaded, 16)
            def high(chunk, use, j, dst, width=512):
                act.wait_ge(raw_loaded[j], chunk_loads(chunk, j))
                if use is not None:
                    act.wait_ge(chunk_used, use + 1)
                act.activation(dst, raw[:, j, 0:width], ACT.Identity).then_inc(hi_done, 1)

            def chunk_loads(chunk, j):
                return (chunk - j) * 4 + 16

            def high_part(dst, s, b, bias):
                if bias is None:
                    ins = act.activation(dst, bank(s, b), ACT.Copy)
                else:
                    ins = act.activation(dst, bank(s, b), ACT.Identity, bias=bias)
                ins.then_inc(h_done, 1)

            def softmax(it):
                act.wait_ge(mag_in, it + 1)
                act.activation(sm[:, 0, :, :], sm[:, 1, :, :], ACT.Sqrt).then_inc(mag_out, 1)
                act.wait_ge(exp_in, it + 1)
                act.activation(sm[:, 2, :, :], sm[:, 1, :, :], ACT.Exp, scale=SCALE).then_inc(exp_out, 1)

            def encoder_step(t, tiles=None):
                c0, u0 = t * RAW_STEP, t * USE_STEP
                act.wait_ge(bank_free[0], t * (4 * SET0_STEP) + 4)
                act.wait_ge(bank_free[1], t * (4 * SET1_STEP) + 4)
                act.dma_start(rows[:, :], enc_rows[t % 2, :, 0:HID].broadcast_to([P, HID])).then_inc(rows_loaded, 16)
                act.dma_start(cols[:, :], enc_cols[t % 2]).then_inc(cols_loaded, 16)
                for k in range(KX):
                    high(c0 + 2 * k, None, 2 * k % RING, a_hi[:, k, :])
                    high(c0 + (2 * k + 1), u0 + k, (2 * k + 1) % RING, w_hi[:, k % RING, :])

                def quads(first, last):
                    with act.Fori(first, last) as q:
                        for j in range(RING):
                            high(c0 + 2 * KX + q * RING + j, u0 + KX + q * RING + j, j, w_hi[:, j, :])

                if tiles is None:
                    quads(0, 3 * KH // RING + 1)
                else:
                    quads(0, 9)
                    softmax(tiles[0])
                    quads(9, 3 * KH // RING + 1)
                act.wait_ge(consts, 4)
                act.wait_ge(var_done, (t + 1) * BT)
                act.activation(ln[:, 0, :], mv[:, :, 1], ACT.Sqrt, bias=epsc[:, 0:1]).then_inc(sd_done, 1)
                act.dma_start(rows[:, 0:3 * D], enc_rows[t % 2, :, HID:HID + 3 * D].broadcast_to([P, 3 * D]))\
                    .then_inc(rows_loaded, 16)
                act.wait_ge(cols_loaded, t * 16 + 32)
                c1, u1 = c0 + 2 * KX + 3 * KH, u0 + 4 * KH
                for k in range(KH):
                    act.wait_ge(turned, t * KH + (k + 1))
                    act.wait_ge(tmp_done, t * KH + (k + 1))
                    act.activation(gf[:, k % 2, :], bank(1, k % 4), ACT.Gelu,
                                   scale=cols[:, k:k + 1], bias=cols[:, KH + k:KH + k + 1])
                    act.activation(a_hi[:, k, :], bank(1, k % 4), ACT.Gelu,
                                   scale=cols[:, k:k + 1], bias=cols[:, KH + k:KH + k + 1])\
                        .then_inc(bank_free[1], 1)
                    if k >= 4:
                        high(c1 + k, u1 + k, k % RING, w_hi[:, k % RING, :])
                for n in range(N):
                    q0 = c1 + (n + 1) * KH, u1 + (n + 1) * KH
                    for j in range(RING):
                        high(q0[0] + j, q0[1] + j, j, w_hi[:, j, :])
                    act.wait_ge(chunk_used, q0[1] + RING)
                    for b in range(KD):
                        high_part(s_hi[:, KD * n + b, :], n % 2, b,
                                  cols[:, 2 * KH + KD * n + b:2 * KH + KD * n + b + 1])
                    if n == 1 and tiles is not None:
                        softmax(tiles[1])
                    if n < N - 1:
                        with act.Fori(1, KH // RING) as q:
                            for j in range(RING):
                                high(q0[0] + q * RING + j, q0[1] + q * RING + j, j, w_hi[:, j, :])
                c2, u2 = c1 + N * KH, u1 + N * KH
                for w in range(3):
                    for n in range(N):
                        if n == N - 1 and w < 2:
                            for j in range(RING):
                                high(c2 + (KD * (w + 1) + j), u2 + (KD * (w + 1) + j), j, w_hi[:, j, :])
                        s = n % 2
                        for b in range(BT):
                            use = (4, 8)[s] + 2 * w + n // 2
                            act.wait_ge(bank_free[s], t * (4 * (SET0_STEP, SET1_STEP)[s]) + (4 * use + b + 5))
                            act.dma_start(qkv[t, w, n, b], stage[:, b, :]).then_inc(stored[b], 16)

            with act.Fori(0, 2) as t:
                encoder_step(t)
            with act.Fori(2, STEPS) as t:
                encoder_step(t, (t * 2 - 4, t * 2 - 3))
            act.wait_ge(bank_free[0], STEPS * (4 * SET0_STEP) + 4)
            act.wait_ge(bank_free[1], STEPS * (4 * SET1_STEP) + 4)
            act.dma_start(prow, post_row.broadcast_to([P, OUT])).then_inc(rows_loaded, 16)

            h0, f0 = STEPS * N * KD, STEPS * KH
            act.wait_ge(ao_stored, BT * G * 32 + 32)

            def mixing(half):
                c0, u0 = half * RAW_MIX + RAW_MIX0, half * RAW_MIX + USE_MIX0

                def highs(first, count=RING, width=512):
                    for j in range(count):
                        high(c0 + (first + j), u0 + (first + j), j, w_hi[:, j, 0:width], width)

                def stream(n, tile=None):
                    cn, un = n * 16 + c0, n * 16 + u0

                    def stream_highs(q):
                        for j in range(RING):
                            high(cn + (4 * q + j), un + (4 * q + j), j, w_hi[:, j, :])

                    for c in range(2):
                        act.wait_ge(turned, n * 8 + (STEPS * KH + half * (8 * N + 12) + 4 * c))
                        act.dma_start(at_in[:, :, :], att[half, c, n].rearrange("b p d -> p b d"))\
                            .then_inc(at_loaded, 16)
                        stream_highs(c)
                        for k in range(KD):
                            act.wait_ge(turned, n * 8 + (STEPS * KH + half * (8 * N + 12) + 4 * c + k + 1))
                            high_part(a_hi[:, k, :], 0, k, None)
                        if c == 0 and tile is not None:
                            softmax(tile)
                        act.wait_ge(chunk_used, un + (4 * c + 8))
                        for k in range(KD):
                            high_part(a_hi[:, 4 + 4 * c + k, :], 1, k, mcols[:, KD * c + k:KD * c + k + 1])
                    stream_highs(2)
                    act.wait_ge(block_done, n * 2 + (half * (2 * N + 3) + 9 * STEPS + 1))
                    for b in range(BT):
                        act.activation(ri[:, b, 0, n, :], bank(0, b), ACT.Copy).then_inc(bank_free[0], 1)
                    stream_highs(3)
                    act.wait_ge(chunk_used, un + 20)
                    for b in range(BT):
                        act.activation(ri[:, b, 1, n, :], bank(1, b), ACT.Copy).then_inc(bank_free[1], 1)

                if half == 0:
                    stream(0)
                    with act.Fori(1, N) as n:
                        stream(n, n + (BT - 1))
                    softmax(2 * BT - 1)
                else:
                    with act.Fori(0, N) as n:
                        stream(n)
                q = 16 * N
                for u in range(2 * BT):
                    bt, f = u // 2, u % 2
                    highs(q)
                    q += 4
                    uh = half * (2 * BT) + u
                    act.wait_ge(ph_free, uh + 1)
                    if u == 0:
                        act.wait_ge(bank_free[1], half * (4 * SET1_MIX) + (4 * STEPS * SET1_STEP + 4 + 12 * N))
                        act.wait_ge(bank_free[0], 4 * STEPS * SET0_STEP + 4 + half * (4 * SET0_MIX) + 16 * N)
                    for c in range(2):
                        act.activation(ph[:, u % 2, 1024 * c:1024 * c + 1024].rearrange("p (n d) -> p n d", n=N),
                                       ri[:, bt, c, :, 256 * f:256 * f + 256], ACT.Square).then_inc(squares, 1)
                    act.wait_ge(sq_sum, uh + 1)
                    act.activation(ph[:, u % 2, 1024:2048], ph[:, u % 2, 0:1024], ACT.Sqrt).then_inc(roots, 1)
                for bt in range(BT):
                    hb = half * BT + bt
                    act.wait_ge(ph_free, hb * 2 + 4)
                    for c in range(2):
                        act.activation(ri[:, bt, 1, 2 + c, :], ri[:, bt, 0, c, :], ACT.Square,
                                       accum_out=nrm[:, c:c + 1]).then_inc(sup_sq, 1)
                    act.wait_ge(sup_sum, hb + 1)
                    act.activation(nrm[:, 3:4], nrm[:, 2:3], ACT.Sqrt, bias=epsc[:, 1:2]).then_inc(sup_root, 1)
                tb = STEPS * KH + half * (8 * N + 12) + 8 * N
                highs(q)
                for c in range(2):
                    for k in range(KD):
                        act.wait_ge(turned, tb + (4 * c + k + 1))
                        high_part(a_hi[:, 4 * c + k, :], c, k, None)
                act.wait_ge(block_done, half * (2 * N + 3) + (9 * STEPS + 2 * N + 1))
                for k in range(4):
                    act.activation(meas_r[:, k, :], bank(0, k), ACT.Copy).then_inc(bank_free[0], 1)
                highs(q + 4)
                highs(q + 8)
                for k in range(4):
                    act.activation(meas_q[:, k, :], bank(1, k), ACT.Square).then_inc(bank_free[1], 1)
                fh = f0 + half * 12
                for k in range(4):
                    act.wait_ge(amp_in, half * 4 + (k + 1))
                    act.wait_ge(tmp_done, fh + (k + 1))
                    act.activation(gf[:, k % 2, :], meas_r[:, k, :], ACT.Sqrt)
                    act.activation(s_hi[:, k, :], meas_r[:, k, :], ACT.Sqrt).then_inc(h_done, 1)
                highs(q + 12)
                act.wait_ge(var_done, half * BT + (STEPS + 1) * BT)
                act.activation(ln[:, 0, :], mv[:, :, 1], ACT.Sqrt, bias=epsc[:, 0:1]).then_inc(sd_done, 1)
                for k in range(KD):
                    act.wait_ge(turned, tb + (9 + k))
                    act.wait_ge(tmp_done, fh + (5 + k))
                    for dst in (gf[:, k % 2, :], s_hi[:, 4 + k, :]):
                        ins = act.activation(dst, bank(0, k), ACT.Gelu, scale=mcols[:, 2 * KD + k:2 * KD + k + 1],
                                             bias=mcols[:, 3 * KD + k:3 * KD + k + 1])
                    ins.then_inc(bank_free[0], 1)
                highs(q + 16, width=256)
                for k in range(4):
                    act.wait_ge(bank_free[1], half * (4 * SET1_MIX) + (4 * STEPS * SET1_STEP + 4 + 12 * N + 16 + k + 1))
                    act.wait_ge(tmp_done, fh + (9 + k))
                    act.activation(gf[:, k % 2, :], post_z[:, k, :], ACT.Relu)
                    act.activation(s_hi[:, 8 + k, :], post_z[:, k, :], ACT.Relu).then_inc(h_done, 1)
                act.wait_ge(h_done, (half + 1) * (16 * N + 16) + STEPS * N * KD)

            mixing(0)
            act.wait_ge(ao_stored, 2 * BT * G * 32 + 32)
            mixing(1)
            act.wait_ge(bank_free[0], 4 * STEPS * SET0_STEP + 4 + 4 * HALVES * SET0_MIX)
            act.dma_start(y.rearrange("b o -> o b"), y_sb[:, :]).then_inc(y_stored, 16)
            act.wait_ge(y_stored, 16)

        @block.tensor
        def _(pe):
            pe.sem_inc(chunk_used, RING)
            for s in range(2):
                pe.sem_inc(bank_free[s], 4)

            def three(out, lh, ll, rh, rl, start, stop):
                pe.matmul(out, lh, rh, start=start, stop=False)
                pe.matmul(out, lh, rl, start=False, stop=False)
                return pe.matmul(out, ll, rh, start=False, stop=stop)

            def act_stationary(s, hi, lo, j, start, stop):
                for b in range(BT):
                    last = three(bank(s, b), hi[:, b * P:(b + 1) * P], lo[:, b * P:(b + 1) * P],
                                 w_hi[:, j, :], w_lo[:, j, :], start, stop)
                return last

            def weight_stationary(s, hi, lo, j, start, stop, tiles=4):
                for b in range(tiles):
                    last = three(bank(s, b), w_hi[:, j, b * P:(b + 1) * P], w_lo[:, j, b * P:(b + 1) * P],
                                 hi, lo, start, stop)
                return last

            def banks(s, value, n=4):
                pe.wait_ge(bank_free[s], value + (n - 1))

            def turn(s, b, srcs):
                for i, src in enumerate(srcs):
                    last = pe.transpose(bank(s, b)[:, i * P:(i + 1) * P], src, ident[:, :])
                last.then_inc(turned, 1)

            with pe.Fori(0, STEPS) as t:
                c0, f0, f1 = t * RAW_STEP + RING, t * (4 * SET0_STEP) + 1, t * (4 * SET1_STEP) + 1
                banks(0, f0)
                for k in range(KX):
                    pe.wait_ge(lo_done, c0 + (2 * k + 2))
                    act_stationary(0, a_hi[:, k, :], a_lo[:, k, :], k % RING, k == 0, k == KX - 1)\
                        .then_inc(chunk_used, 1)
                for m in range(1, 4):
                    s = m % 2
                    banks(s, (f0, f1)[s] + 4 * (m // 2))
                    for k in range(KX):
                        pe.wait_ge(lo_done, c0 + (2 * KX + KH * (m - 1) + k + 1))
                        act_stationary(s, a_hi[:, k, :], a_lo[:, k, :], k % RING, k == 0, k == KX - 1)\
                            .then_inc(chunk_used, 1)
                c1 = c0 + (2 * KX + 3 * KH)

                def turn_hidden(k):
                    pe.wait_ge(normed, t * (4 * BT) + BT * (k // 4 + 1))
                    pe.wait_ge(bank_free[1], f1 + (8 + k))
                    turn(1, k % 4, [hid[:, b, k * P:(k + 1) * P] for b in range(BT)])

                pe.wait_ge(consts, 4)
                for k in range(4):
                    turn_hidden(k)
                for n in range(N):
                    s = n % 2
                    banks(s, (f0 + 8, f1 + 24)[s] + 4 * (n // 2))
                    for k in range(KH):
                        if n == 0:
                            pe.wait_ge(tmp_done, t * KH + (k + 3))
                        pe.wait_ge(lo_done, c1 + (n * KH + k + 1))
                        weight_stationary(s, a_hi[:, k, :], a_lo[:, k, :], k % RING, k == 0, k == KH - 1)\
                            .then_inc(chunk_used, 1)
                        if n == 0 and k + 4 < KH:
                            turn_hidden(k + 4)
                c2 = c1 + N * KH
                for w in range(3):
                    for n in range(N):
                        s = n % 2
                        banks(s, (f0 + 16, f1 + 32)[s] + (8 * w + 4 * (n // 2)))
                        for k in range(KD):
                            if n == 0:
                                pe.wait_ge(lo_done, c2 + (KD * w + k + 1))
                            last = act_stationary(s, s_hi[:, KD * n + k, :], s_lo[:, KD * n + k, :], k,
                                                  k == 0, k == KD - 1)
                            if n == N - 1:
                                last.then_inc(chunk_used, 1)
                        if n < N - 1:
                            last.then_inc(block_done, 1)

            with pe.Fori(0, HALVES) as half:
                c0 = half * RAW_MIX + (RAW_MIX0 + RING)
                f0 = half * (4 * SET0_MIX) + (4 * STEPS * SET0_STEP + 1)
                f1 = half * (4 * SET1_MIX) + (4 * STEPS * SET1_STEP + 1)

                def product(way, s, regions, base, start, stop, chunk=None, release=True, done=None, tiles=4):
                    for k in range(KD):
                        if chunk is not None:
                            pe.wait_ge(lo_done, chunk + (k + 1))
                        hi, lo = regions
                        if way is weight_stationary:
                            last = way(s, hi[:, base + k, :], lo[:, base + k, :], k,
                                       start and k == 0, stop and k == KD - 1, tiles)
                        else:
                            last = way(s, hi[:, base + k, :], lo[:, base + k, :], k,
                                       start and k == 0, stop and k == KD - 1)
                        if release:
                            last.then_inc(chunk_used, 1)
                    if done is not None:
                        last.then_inc(done, 1)

                first, second = (a_hi, a_lo), (s_hi, s_lo)
                with pe.Fori(0, N) as n:
                    cn, g0, g1 = c0 + n * 16, f0 + n * 16, f1 + n * 12
                    for c in range(2):
                        pe.wait_ge(at_loaded, (half * (2 * N) + n * 2) * 16 + (16 * c + 16))
                        banks(0, g0 + 4 * c)
                        for k in range(KD):
                            turn(0, k, [at_in[:, b, k * P:(k + 1) * P] for b in range(BT)])
                        banks(1, g1 + 4 * c)
                        banks(0, g0 + (4 * c + 4))
                        product(weight_stationary, 1, first, 0, True, True, cn + 4 * c)
                    banks(0, g0 + 8)
                    banks(1, g1 + 8)
                    product(act_stationary, 0, first, 4, True, True, cn + 8, False, block_done)
                    product(act_stationary, 1, first, 8, True, False)
                    banks(0, g0 + 12)
                    product(act_stationary, 0, first, 8, True, True, cn + 12, False, block_done)
                    product(act_stationary, 1, first, 4, False, True)
                ct = c0 + 16 * N
                banks(1, f1 + 12 * N)
                for k in range(KX):
                    pe.wait_ge(lo_done, ct + (2 * k + 2))
                    jw, jx = 2 * k % RING, (2 * k + 1) % RING
                    for b in range(4):
                        last = three(bank(1, b), w_hi[:, jw, b * P:(b + 1) * P], w_lo[:, jw, b * P:(b + 1) * P],
                                     w_hi[:, jx, :], w_lo[:, jx, :], k == 0, k == KX - 1)
                    last.then_inc(chunk_used, 2)
                cm, e0, e1 = ct + 2 * KX, f0 + 16 * N, f1 + (12 * N + 4)
                pe.wait_ge(sup_ready, (half + 1) * BT)
                for c in range(2):
                    banks(c, (e0, e1)[c])
                    for k in range(KD):
                        turn(c, k, [ri[:, b, 0, c, k * P:(k + 1) * P] for b in range(BT)])
                banks(0, e0 + 4)
                banks(1, e1 + 4)
                product(weight_stationary, 0, first, 0, True, True, cm, False, block_done)
                product(weight_stationary, 1, first, 4, True, False)
                banks(0, e0 + 8)
                product(weight_stationary, 0, first, 4, True, True, cm + 4, False, block_done)
                product(weight_stationary, 1, first, 0, False, True)
                fh = half * 12 + STEPS * KH + 2
                pe.wait_ge(tmp_done, fh + 4)
                banks(1, e1 + 8)
                product(act_stationary, 1, second, 0, True, True, cm + 8)
                pe.wait_ge(normed, half * BT + (STEPS * 4 * BT + BT))
                banks(0, e0 + 12)
                for k in range(KD):
                    turn(0, k, [post_z[:, b, k * P:(k + 1) * P] for b in range(BT)])
                pe.wait_ge(tmp_done, fh + 8)
                banks(1, e1 + 12)
                product(weight_stationary, 1, second, 4, True, True, cm + 12)
                pe.wait_ge(tmp_done, fh + 12)
                banks(0, e0 + 16)
                product(weight_stationary, 0, second, 8, True, True, cm + 16, tiles=2)
                pe.wait_ge(h2_done, half * 2 + 2)
                for k in range(2):
                    last = pe.matmul(bank(0, 2)[0:1, :], mcols[:, MIX_COLS - 2 + k:MIX_COLS - 1 + k],
                                     hid2[:, k, :], start=(k == 0), stop=(k == 1))
                last.then_inc(block_done, 1)

        @block.vector
        def _(dve):
            dve.sem_inc(tmp_done, 2)
            for b in range(BT):
                dve.sem_inc(stored[b], 16)
            step = Count(dve_step)

            def link(ins):
                ins.then_inc(dve_step, 1)
                dve.wait_ge(dve_step, step.next())

            def low_part(lo, hi, s, b, bias):
                if bias is None:
                    ins = dve.tensor_tensor(lo, bank(s, b), hi.bitcast(F32), ALU.subtract)
                else:
                    ins = dve.scalar_tensor_tensor(out=lo, in0=bank(s, b), scalar=bias, in1=hi.bitcast(F32),
                                                   op0=ALU.add, op1=ALU.subtract)
                ins.then_inc(bank_free[s], 1)

            def norm_scales(count, var_at):
                dve.sem_inc(stats_seen, 1)
                for b in range(BT):
                    dve.bn_aggr(mv[:, b, :], stats[:, b, 0:count, :]).then_inc(var_done, 1)
                dve.wait_ge(sd_done, var_at)
                link(dve.reciprocal(ln[:, 1, :], ln[:, 0, :]))
                link(dve.scalar_tensor_tensor(out=ln[:, 2, :], in0=mv[:, :, 0], scalar=-1.0, in1=ln[:, 1, :],
                                              op0=ALU.mult, op1=ALU.mult))

            dve.sem_inc(products, N)
            dve.sem_inc(scored, N)
            dve.sem_inc(pv_step, 3)

            def scores(it, g):
                Q, K = qk[:, 0], qk[:, 1]
                dve.wait_ge(qk_loaded, it * (64 * G) + (64 * g + 64))
                dve.wait_ge(scored, it * (N * G) + (N * g + N))
                dve.tensor_tensor(Q[:, 2], Q[:, 0], Q[:, 1], ALU.add).then_inc(dve_step, 1)
                step.next()
                link(dve.tensor_tensor(K[:, 2], K[:, 0], K[:, 1], ALU.subtract))
                for n in range(N):
                    done = it * (N * G) + (N * g + n + 1 + N)
                    if n:
                        dve.wait_ge(scored, done - 1)
                    dve.tensor_tensor(prod[:, :].rearrange("p (x m d) -> p x m d", x=3, m=N),
                                      Q[:, :, n:n + 1, :].broadcast_to([P, 3, N, P]), K, ALU.mult)\
                        .then_inc(products, 1)
                    dve.wait_ge(products, done)
                    dve.tensor_reduce(dots[:, g, n, :, :].rearrange("p x m -> p (x m)"),
                                      prod[:, :].rearrange("p (a d) -> p a d", d=HD), AX_X, ALU.add)\
                        .then_inc(scored, 1)

            def softmax(it):
                dve.wait_ge(scored, it * (N * G) + (N * G + N))
                pr, pi, pm = (dots[:, :, :, x, :].rearrange("p g n m -> p (g n) m") for x in range(3))
                A = [sm[:, i, :, :] for i in range(5)]
                link(dve.tensor_tensor(A[2], pr, pi, ALU.add))
                link(dve.tensor_tensor(A[3], pm, pr, ALU.subtract))
                link(dve.tensor_tensor(A[3], A[3], pi, ALU.add))
                link(dve.tensor_tensor(A[2], A[2], A[2], ALU.mult))
                link(dve.tensor_tensor(A[3], A[3], A[3], ALU.mult))
                dve.scalar_tensor_tensor(out=A[1], in0=A[2], scalar=EPS, in1=A[3], op0=ALU.add, op1=ALU.add)\
                    .then_inc(mag_in, 1)
                dve.wait_ge(mag_out, it + 1)
                heads = lambda a: a.rearrange("p g (m h) -> p g h m", h=2)
                over = lambda a: a.rearrange("p g (m h) -> p g m h", h=2)
                spread = lambda a: a[:, :, None, :].broadcast_to([P, G * N, N, 2])
                link(dve.tensor_reduce(mx[:, 0], heads(A[0]), AX_X, ALU.max))
                dve.tensor_tensor(over(A[1]), over(A[0]), spread(mx[:, 0]), ALU.subtract).then_inc(exp_in, 1)
                dve.wait_ge(exp_out, it + 1)
                link(dve.tensor_reduce(mx[:, 1], heads(A[2]), AX_X, ALU.add))
                link(dve.reciprocal(mx[:, 0], mx[:, 1]))
                dve.wait_ge(pv_step, it * (24 * G) + 3)
                dve.tensor_tensor(over(A[4]), over(A[2]), spread(mx[:, 0]), ALU.mult).then_inc(weights_done, 1)

            SCORE_LINKS, SOFTMAX_LINKS = 2, 8
            STEP_LINKS = 2
            ATT_LINKS = 8 * SCORE_LINKS + 2 * SOFTMAX_LINKS

            def encoder_step(t, i0=None, i1=None):
                f = (t * (4 * SET0_STEP) + 4, t * (4 * SET1_STEP) + 4)
                u0 = t * USE_STEP + RING
                dve.wait_ge(rows_loaded, t * 32 + 16)
                dve.wait_ge(cols_loaded, t * 16 + 32)
                for m in range(4):
                    s = m % 2
                    dve.wait_ge(chunk_used, u0 + KX * (m + 1))
                    for b in range(BT):
                        dve.tensor_tensor(hid[:, b, m * 512:(m + 1) * 512], bank(s, b),
                                          rows[:, m * 512:(m + 1) * 512], ALU.add).then_inc(bank_free[s], 1)
                    for b in range(BT):
                        dve.wait_ge(bank_free[s], f[s] + (4 * (m // 2) + b + 1))
                        dve.bn_stats(stats[:, b, m, :], hid[:, b, m * 512:(m + 1) * 512]).then_inc(stats_done, 1)
                    if i0 is not None:
                        if m == 0:
                            scores(i0, 0)
                            scores(i0, 1)
                        elif m == 1:
                            scores(i0, 2)
                            scores(i0, 3)
                        elif m == 2:
                            softmax(i0)
                            scores(i1, 0)
                dve.wait_ge(stats_done, (t + 1) * (4 * BT))
                norm_scales(4, t + 1)
                for m in range(4):
                    for b in range(BT):
                        part = hid[:, b, m * 512:(m + 1) * 512]
                        dve.tensor_scalar(part, part, ln[:, 1, b:b + 1], ln[:, 2, b:b + 1], ALU.mult, ALU.add)\
                            .then_inc(normed, 1)
                for k in range(KH):
                    dve.wait_ge(bank_free[1], f[1] + (8 + k + 1))
                    dve.tensor_tensor(a_lo[:, k, :], gf[:, k % 2, :], a_hi[:, k, :].bitcast(F32), ALU.subtract)\
                        .then_inc(tmp_done, 1)
                for n in range(N):
                    for b in range(KD):
                        dve.wait_ge(h_done, t * (N * KD) + (KD * n + b + 1))
                        low_part(s_lo[:, KD * n + b, :], s_hi[:, KD * n + b, :], n % 2, b,
                                 cols[:, 2 * KH + KD * n + b:2 * KH + KD * n + b + 1])
                    if i0 is not None:
                        if n == 0:
                            scores(i1, 1)
                            scores(i1, 2)
                        elif n == 1:
                            scores(i1, 3)
                            softmax(i1)
                dve.wait_ge(rows_loaded, t * 32 + 32)
                u2 = u0 + (4 * KH + N * KH)
                for w in range(3):
                    for n in range(N):
                        s = n % 2
                        if n < N - 1:
                            dve.wait_ge(block_done, t * 9 + (3 * w + n + 1))
                        else:
                            dve.wait_ge(chunk_used, u2 + KD * (w + 1))
                        for b in range(BT):
                            dve.wait_ge(stored[b], t * (16 * 3 * N) + 16 * (4 * w + n + 1))
                            dve.tensor_tensor(stage[:, b, :], bank(s, b), rows[:, D * w:D * (w + 1)],
                                              ALU.add).then_inc(bank_free[s], 1)

            with dve.Fori(0, 2) as t:
                step.at(t * STEP_LINKS)
                encoder_step(t)
            with dve.Fori(0, 2) as e:
                step.at(e * (STEP_LINKS + ATT_LINKS) + 2 * STEP_LINKS)
                encoder_step(e + 2, e * 2, e * 2 + 1)
                assert step.n == STEP_LINKS + ATT_LINKS, step.n

            dve.wait_ge(gathered, 16 * N * BATCH // P)
            dve.sem_inc(ph_free, 2)
            dve.wait_ge(rows_loaded, STEPS * 32 + 16)
            step.at(4 * STEP_LINKS + 2 * ATT_LINKS)

            def mixing(half):
                u0 = half * RAW_MIX + (USE_MIX0 + RING)
                h0 = half * (16 * N + 16) + STEPS * N * KD
                d0 = half * (2 * N + 3) + 9 * STEPS
                f0 = half * (4 * SET0_MIX) + (4 * STEPS * SET0_STEP + 4)
                f1 = half * (4 * SET1_MIX) + (4 * STEPS * SET1_STEP + 4)
                dve.tensor_copy(sh[:, :, :], strength[:, half * BT:(half + 1) * BT, :, :]
                                .rearrange("p b i j -> p b (i j)")).then_inc(dve_step, 1)
                step.next()

                def stream(n, first, attention):
                    for c in range(2):
                        for k in range(KD):
                            dve.wait_ge(h_done, n * 16 + (h0 + 8 * c + k + 1))
                            low_part(a_lo[:, k, :], a_hi[:, k, :], 0, k, None)
                        if attention:
                            if c == 0 and not first:
                                softmax(n + (BT - 1))
                            scores(n + BT, c)
                        for k in range(KD):
                            dve.wait_ge(h_done, n * 16 + (h0 + 8 * c + k + 5))
                            low_part(a_lo[:, 4 + 4 * c + k, :], a_hi[:, 4 + 4 * c + k, :], 1, k,
                                     mcols[:, KD * c + k:KD * c + k + 1])
                    if attention:
                        scores(n + BT, 2)
                        scores(n + BT, 3)
                    dve.wait_ge(block_done, n * 2 + (d0 + 2))
                    for b in range(BT):
                        dve.tensor_tensor(ri[:, b, 0, n, :], ri[:, b, 0, n, :], bank(0, b), ALU.subtract)\
                            .then_inc(bank_free[0], 1)

                if half == 0:
                    stream(0, True, True)
                    before, links = step.now, G * SCORE_LINKS + SOFTMAX_LINKS
                    with dve.Fori(1, N) as n:
                        step.at(n * links + (before - links))
                        stream(n, False, True)
                        assert step.n == links, step.n
                    step.at(before + (N - 1) * links)
                    softmax(2 * BT - 1)
                else:
                    with dve.Fori(0, N) as n:
                        stream(n, True, False)

                off = {1: 0, 2: 3, 3: 5}

                def pair(i, j):
                    return off[abs(i - j)] + min(i, j)

                for u in range(2 * BT):
                    bt, f = u // 2, u % 2
                    uh = half * (2 * BT) + u
                    buf = lambda a, b: ph[:, u % 2, a:b].rearrange("p (n d) -> p n d", d=256)
                    m0, m1, ur, ui = (buf(1024 * i, 1024 * i + 1024) for i in range(4))
                    cc, ww = buf(4096, 5632), buf(5632, 6656)
                    R, I = (ri[:, bt, c, :, 256 * f:256 * f + 256] for c in range(2))
                    dve.wait_ge(squares, uh * 2 + 2)
                    dve.tensor_tensor(m0, m0, m1, ALU.add).then_inc(sq_sum, 1)
                    dve.wait_ge(roots, uh + 1)
                    link(dve.tensor_scalar(m0, m0, 0.0, None, ALU.is_equal))
                    link(dve.tensor_tensor(m1, m1, m0, ALU.add))
                    link(dve.reciprocal(m1, m1))
                    dve.tensor_tensor(ur, R, m1, ALU.mult).then_inc(dve_step, 1)
                    step.next()
                    link(dve.tensor_tensor(ui, I, m1, ALU.mult))
                    second = {1: ww[:, 0:3], 2: m1[:, 0:2], 3: m1[:, 2:3]}
                    for d in (1, 2, 3):
                        dve.tensor_tensor(cc[:, off[d]:off[d] + N - d], ur[:, 0:N - d], ur[:, d:N], ALU.mult)
                        ins = dve.tensor_tensor(second[d], ui[:, 0:N - d], ui[:, d:N], ALU.mult)
                    link(ins)
                    for more in (second, {d: m0[:, 0:N - d] for d in off}, {d: m0[:, d:N] for d in off}):
                        for d in (1, 2, 3):
                            c_ = cc[:, off[d]:off[d] + N - d]
                            ins = dve.tensor_tensor(c_, c_, more[d], ALU.add)
                        link(ins)
                    s_ = lambda i, j: sh[:, bt, N * i + j:N * i + j + 1]
                    for r in range(N - 1):
                        for j in range(N):
                            i = [i for i in range(N) if i != j][r]
                            if r == 0:
                                ins = dve.tensor_scalar(ww[:, j], cc[:, pair(i, j)], s_(i, j), s_(j, j),
                                                        ALU.mult, ALU.add)
                            else:
                                ins = dve.scalar_tensor_tensor(out=ww[:, j], in0=cc[:, pair(i, j)],
                                                               scalar=s_(i, j), in1=ww[:, j],
                                                               op0=ALU.mult, op1=ALU.add)
                        link(ins)
                    dve.tensor_tensor(ur, ww, R, ALU.mult)
                    link(dve.tensor_tensor(ui, ww, I, ALU.mult))
                    for c, x in ((0, ur), (1, ui)):
                        ins = dve.tensor_reduce(ri[:, bt, 0, c, 256 * f:256 * f + 256],
                                                x.rearrange("p n d -> p d n"), AX_X, ALU.add)
                    ins.then_inc(ph_free, 1)
                for bt in range(BT):
                    hb = half * BT + bt
                    dve.wait_ge(sup_sq, hb * 2 + 2)
                    dve.tensor_tensor(nrm[:, 2:3], nrm[:, 0:1], nrm[:, 1:2], ALU.add).then_inc(sup_sum, 1)
                    dve.wait_ge(sup_root, hb + 1)
                    link(dve.reciprocal(nrm[:, 4:5], nrm[:, 3:4]))
                    sup = ri[:, bt, 0, 0:2, :]
                    dve.tensor_scalar(sup, sup, nrm[:, 4:5], None, ALU.mult).then_inc(sup_ready, 1)
                u1 = u0 + (16 * N + 2 * KX)
                dve.wait_ge(chunk_used, u1)
                for k in range(4):
                    dve.tensor_scalar(top_part[:, k, :], bank(1, k), mcols[:, 4 * KD + k:4 * KD + k + 1], None,
                                      ALU.add).then_inc(bank_free[1], 1)
                for c in range(2):
                    for k in range(KD):
                        dve.wait_ge(h_done, h0 + (16 * N + 4 * c + k + 1))
                        low_part(a_lo[:, 4 * c + k, :], a_hi[:, 4 * c + k, :], c, k, None)
                dve.wait_ge(block_done, d0 + (2 * N + 2))
                e0, e1 = f0 + 16 * N, f1 + 12 * N
                for k in range(4):
                    dve.tensor_tensor(meas_r[:, k, :], meas_r[:, k, :], bank(0, k), ALU.subtract)\
                        .then_inc(bank_free[0], 1)
                for k in range(4):
                    dve.wait_ge(bank_free[0], e0 + (8 + k + 1))
                    ins = dve.tensor_tensor(meas_r[:, k, :], meas_r[:, k, :], meas_r[:, k, :], ALU.mult)
                    ins.then_inc(dve_step, 1)
                    step.next()
                for k in range(4):
                    dve.wait_ge(dve_step, step.now - 3 + k)
                    dve.wait_ge(bank_free[1], e1 + (8 + k + 1))
                    dve.tensor_tensor(meas_r[:, k, :], meas_r[:, k, :], meas_q[:, k, :], ALU.add)\
                        .then_inc(amp_in, 1)
                for k in range(4):
                    dve.wait_ge(h_done, h0 + (16 * N + 8 + k + 1))
                    dve.tensor_tensor(s_lo[:, k, :], gf[:, k % 2, :], s_hi[:, k, :].bitcast(F32), ALU.subtract)\
                        .then_inc(tmp_done, 1)
                dve.wait_ge(chunk_used, u1 + 3 * KD)
                for b in range(BT):
                    dve.tensor_tensor(post_z[:, b, :], bank(1, b), prow[:, :], ALU.add).then_inc(bank_free[1], 1)
                for b in range(BT):
                    dve.wait_ge(bank_free[1], e1 + (12 + b + 1))
                    dve.bn_stats(stats[:, b, 0, :], post_z[:, b, :]).then_inc(stats_done, 1)
                dve.wait_ge(stats_done, half * BT + (4 * BT * STEPS + BT))
                norm_scales(1, half + (STEPS + 1))
                for b in range(BT):
                    dve.tensor_scalar(post_z[:, b, :], post_z[:, b, :], ln[:, 1, b:b + 1], ln[:, 2, b:b + 1],
                                      ALU.mult, ALU.add).then_inc(normed, 1)
                for k in range(KD):
                    dve.wait_ge(bank_free[0], e0 + (12 + k + 1))
                    dve.tensor_tensor(s_lo[:, 4 + k, :], gf[:, k % 2, :], s_hi[:, 4 + k, :].bitcast(F32),
                                      ALU.subtract).then_inc(tmp_done, 1)
                dve.wait_ge(chunk_used, u1 + 4 * KD)
                for k in range(4):
                    dve.tensor_tensor(post_z[:, k, :], bank(1, k), top_part[:, k, :], ALU.add)\
                        .then_inc(bank_free[1], 1)
                for k in range(4):
                    dve.wait_ge(h_done, h0 + (16 * N + 12 + k + 1))
                    dve.tensor_tensor(s_lo[:, 8 + k, :], gf[:, k % 2, :], s_hi[:, 8 + k, :].bitcast(F32),
                                      ALU.subtract).then_inc(tmp_done, 1)
                dve.wait_ge(chunk_used, u1 + 5 * KD)
                for k in range(2):
                    dve.tensor_scalar(hid2[:, k, :], bank(0, k), mcols[:, 4 * KD + 4 + k:4 * KD + 5 + k], 0.0,
                                      ALU.add, ALU.max).then_inc(h2_done, 1)
                dve.wait_ge(block_done, d0 + (2 * N + 3))
                dve.tensor_copy(y_sb[:, half * HALF:(half + 1) * HALF], bank(0, 2)[0:1, :]).then_inc(bank_free[0], 4)

            mixing(0)
            mixing(1)


def kernel(**inputs):
    import numpy as np
    import concourse.bacc as bacc
    from concourse.bass_utils import run_bass_kernel_spmd

    a = {k: np.asarray(v) for k, v in inputs.items()}
    L = {k[len("L0_rec_"):]: v for k, v in a.items() if k.startswith("L0_rec_")}

    def chunks(w):
        k, n = w.shape
        return w.reshape(k // P, P, n // 512, 512).transpose(2, 0, 1, 3).reshape(-1, P, 512)

    def column(v):
        return v.reshape(-1, P).T

    def encoder(t, c):
        return np.concatenate([chunks(L[f"{t}_W1"].T), chunks(L[f"{t}_W2"].T)]
                              + [chunks(L[f"W{w}_{c}"].T) for w in "qkv"])

    arrays = {
        "enc_w": np.stack([encoder("er", "r"), encoder("ei", "i")]),
        "xs": a["r_x"].T.reshape(KX, P, HALVES, HALF).transpose(2, 0, 1, 3),
        "enc_rows": np.stack([np.concatenate([L[f"{t}_b1"]] + [L[f"b{w}_{c}"] for w in "qkv"])[None]
                              for t, c in (("er", "r"), ("ei", "i"))]),
        "enc_cols": np.stack([np.concatenate([column(L[f"{t}_{v}"]) for v in ("g1", "be1", "b2")], 1)
                              for t in ("er", "ei")]),
        "wo": np.stack([chunks(L[f"Wo_{c}"].T) for c in "ri"]),
        "int_w": np.stack([np.stack([chunks(L[f"int_W{c}"][n].T) for c in "ri"]) for n in range(N)]),
        "post_w": np.stack([chunks(L[w].T) for w in ("meas_Mr", "meas_Mi", "post_W")]),
        "top1": chunks(a["W_top1"]),
        "top2": a["W_top2"].reshape(KD, P, 256),
        "mix_cols": np.concatenate([column(L["bo_r"]), column(L["bo_i"]), column(L["post_g"]),
                                    column(L["post_be"]), column(a["b_top1"]), column(a["b_top2"]),
                                    column(a["W_top3"][:, 0])], 1),
        "post_row": L["post_b"][None],
        "ids": a["ids"].reshape(BATCH // P, P, N).transpose(1, 0, 2).reshape(P, -1),
        "tbl_0": a["tbl_0"], "tbl_1": a["tbl_1"], "tbl_2": a["tbl_2"], "tbl_3": a["tbl_3"],
    }
    nc = bacc.Bacc("TRN2", target_bir_lowering=False, num_devices=1)
    args = {}
    for name, x in arrays.items():
        arrays[name] = np.ascontiguousarray(x)
        args[name] = nc.dram_tensor(name, x.shape, I32 if name == "ids" else F32, kind="ExternalInput").ap()
    y = nc.dram_tensor("y", (BATCH, 1), F32, kind="ExternalOutput").ap()
    tables = [args.pop(f"tbl_{i}") for i in range(N)]
    build(nc, tables=tables, y=y, **args)
    r = run_bass_kernel_spmd(nc, [arrays], core_ids=[0])
    return r.results[0]["y"]
```

```python
from contextlib import ExitStack

import concourse.bass as bass
from concourse import mybir

F32 = mybir.dt.float32
F32R = mybir.dt.float32r
I32 = mybir.dt.int32
U32 = mybir.dt.uint32
ALU = mybir.AluOpType
ACT = mybir.ActivationFunctionType
AX_X = mybir.AxisListType.X

P = 128
BATCH, IN, HID, D, N, OUT, TOP = 1024, 2048, 2048, 512, 4, 512, 512
HEADS, HD = 8, 64
HALF = 512
HALVES = BATCH // HALF
BT = HALF // P
KX = IN // P
KH = HID // P
KD = D // P
STEPS = 2 * HALVES
RING = 4
G = 4
LN_EPS = 1e-5
EPS = 1e-8
SCALE = HD ** -0.5

RAW_STEP = KX + 4 * KH + N * KH + 3 * KD
USE_STEP = 4 * KH + N * KH + 3 * KD
SET0_STEP = 2 + 2 + 6
SET1_STEP = 2 + 4 + 2 + 6
STREAMS = N * 4 * KD
RAW_MIX = STREAMS + 2 * KX
RAW_TAIL = 3 * KD + KD + 4
RAW_MIX0 = STEPS * RAW_STEP
USE_MIX0 = STEPS * USE_STEP
TAIL0 = HALVES * RAW_MIX
SET0_MIX, SET1_MIX = 12 * N, 16 * N + 4
SET0_ALL, SET1_ALL = HALVES * SET0_MIX + HALVES * 20, HALVES * SET1_MIX + HALVES * 16
UNITS = 2 * BT

ENC_COLS = 3 * KH
MIX_COLS = 2 * KD + 2 * KD + 4 + 2 + 2


class Count:

    def __init__(self, sem, start=0):
        self.sem, self.start, self.n = sem, start, 0

    def at(self, start):
        self.start, self.n = start, 0

    def next(self):
        self.n += 1
        return self.start + self.n

    @property
    def now(self):
        return self.start + self.n


def build(nc, enc_w, xs, enc_rows, enc_cols, wo, int_w, post_w, top1, top2, mix_cols, post_row,
          ids, tables, y):
    ctx = ExitStack()
    with ctx:
        def sem(name):
            return ctx.enter_context(nc.semaphore(name))

        address = [(nc.sbuf_base + 31) // 32 * 32]

        def place(name, shape, dtype, offset=None):
            size = 4
            for d in shape[1:]:
                size *= d
            if offset is None:
                offset = address[0]
                address[0] += (size + 31) // 32 * 32
            return nc.alloc_sbuf_tensor_at(name, shape, dtype, offset=offset)

        a0 = address[0]
        a_hi = place("a_hi", [P, 16, HALF], F32R)
        a_lo = place("a_lo", [P, 16, HALF], F32R)
        s0 = address[0]
        s_hi = place("s_hi", [P, 16, HALF], F32R)
        s_lo = place("s_lo", [P, 16, HALF], F32R)
        hid = place("hid", [P, BT, HID], F32, s0)
        KB = 1024
        at_in = [place(f"at_in{c}", [P, BT, D], F32, a0 + (24 + 32 * c) * KB) for c in range(2)]
        rstage = place("rstage", [P, 2, BT, D], F32, s0)
        top_part = [place(f"top_part{i}", [P, 4, HALF], F32, s0 + (16 - 8 * i) * KB) for i in range(HALVES)]
        vv2 = [place(f"vv2_{i}", [P, 2, N, P], F32, s0 + (24 + 20 * i) * KB) for i in range(2)]
        ao2 = [place(f"ao2_{i}", [P, 2, N, P], F32, s0 + (28 + 20 * i) * KB) for i in range(2)]
        qk2 = place("qk2", [P, 2, 3, N, P], F32, s0 + 32 * KB)
        sup = place("sup", [P, BT, 2, D], F32, s0 + 24 * KB)
        rl = place("rl", [P, 2, 2, N, 256], F32, s0 + 40 * KB)
        uu = place("uu", [P, 2, N, 256], F32, s0 + 56 * KB)
        meas_q = place("meas_q", [P, 4, HALF], F32, s0)
        hid2 = place("hid2", [P, 2, HALF], F32, s0)
        q0 = address[0]
        qk = place("qk", [P, 2, 3, N, P], F32)
        vv = place("vv", [P, 2, N, P], F32)
        prod = place("prod", [P, 3 * N * P], F32)
        pv = place("pv", [P, N * P], F32)
        pv2 = place("pv2", [P, 2 * P], F32)
        ao = place("ao", [P, 2, N, P], F32)
        mm = place("mm", [P, 2, 2, N, 256], F32, q0)
        cc = place("cc", [P, 6, 256], F32, q0 + 16 * KB)
        ww = place("ww", [P, N, 256], F32, q0 + 22 * KB)
        c2 = place("c2", [P, 2, 256], F32, q0 + 26 * KB)
        y_sb = place("y_sb", [1, BATCH], F32, address[0])
        dots = place("dots", [P, G, N, 3, 8], F32)
        sm = place("sm", [P, 5, G * N, 8], F32)

        raw = place("raw", [P, RING, 512], F32)
        w_hi = place("w_hi", [P, RING, 512], F32R)
        w_lo = place("w_lo", [P, RING, 512], F32R)
        gf = place("gf", [P, 2, HALF], F32)
        rows = place("rows", [P, HID], F32)
        stage = place("stage", [P, BT, D], F32)
        meas_r = post_z = stage
        junk = stage[:, 0, :]
        cols = place("cols", [P, ENC_COLS], F32)
        mcols = place("mcols", [P, MIX_COLS], F32)
        prow = rows[:, 0:OUT]
        pm = rows[:, OUT:HID].rearrange("p (a d) -> p a d", d=256)
        ident = place("ident", [P, P], F32)
        stats = place("stats", [P, BT, 4, 6], F32)
        mv = place("mv", [P, BT, 2], F32)
        ln = place("ln", [P, 3, BT], F32)
        epsc = place("epsc", [P, 2], F32)
        warm = place("warm", [P, 1], F32)
        mx = place("mx", [P, 2, G * N, 2], F32)
        nrm = place("nrm", [P, 4, BT], F32)
        ids_sb = place("ids_sb", [P, 8 * N], I32)
        strength = place("strength", [P, 8, N, N], F32)
        sh = place("sh", [P, N * N], F32)

        ps = ctx.enter_context(nc.psum_tensor("ps", [P, 8, 512], F32))

        qkv = nc.dram_tensor("qkv_scratch", [STEPS, 3, N, BT, P, D], F32).ap()
        ri = nc.dram_tensor("ri_scratch", [HALVES, N, 2, BT, P, D], F32).ap()
        att = nc.dram_tensor("att_scratch", [HALVES, 2, N, BT, P, D], F32).ap()

        raw_loaded = [sem(f"raw_loaded{j}") for j in range(RING)]
        hi_done = sem("hi_done")
        lo_done = sem("lo_done")
        chunk_used = sem("chunk_used")
        block_done = sem("block_done")
        turned = sem("turned")
        bank_free = [sem("banks0_free"), sem("banks1_free")]
        h_done = sem("h_done")
        rows_loaded, cols_loaded = sem("rows_loaded"), sem("cols_loaded")
        consts = sem("consts")
        warmed = sem("warmed")
        stats_seen = sem("stats_seen")
        stats_done, var_done, sd_done = sem("stats_done"), sem("var_done"), sem("sd_done")
        normed = sem("normed")
        tmp_done = sem("tmp_done")
        stored = [sem(f"stored{j}") for j in range(BT)]
        qk_loaded, v_loaded = sem("qk_loaded"), sem("v_loaded")
        qk2_loaded = sem("qk2_loaded")
        products = sem("products")
        scored = sem("scored")
        weights_done = sem("weights_done")
        pv_step = sem("pv_step")
        ao_stored = sem("ao_stored")
        dve_step = sem("dve_step")
        mag_in, mag_out, exp_in, exp_out = sem("mag_in"), sem("mag_out"), sem("exp_in"), sem("exp_out")
        at_loaded = [sem("at_r_loaded"), sem("at_i_loaded")]
        own_done = sem("own_done")
        own_loaded = [sem("own_loaded0"), sem("own_loaded1")]
        own_stored = [sem("own_stored0"), sem("own_stored1")]
        ri_stored = [sem("r_stored"), sem("i_stored")]
        rl_loaded = [sem("rl_loaded0"), sem("rl_loaded1")]
        squares, sq_sum, roots = sem("squares"), sem("sq_sum"), sem("roots")
        cos_done = sem("cos_done")
        sup_step = sem("sup_step")
        sup_seen = sem("sup_seen")
        masked = sem("masked")
        mask_step = sem("mask_step")
        sup_sq, sup_sum, sup_root = sem("sup_sq"), sem("sup_sum"), sem("sup_root")
        ids_loaded, gathered = sem("ids_loaded"), sem("gathered")
        amp_in = sem("amp_in")
        h2_done, y_stored = sem("h2_done"), sem("y_stored")

        bank = lambda s, b: ps[:, 4 * s + b, :]
        block = ctx.enter_context(nc.Block())

        @block.sync
        def _(sp):
            def load(chunk, j, src, cols_=512):
                sp.wait_ge(lo_done, chunk + 1)
                sp.dma_start(raw[:, j, 0:cols_], src).then_inc(raw_loaded[j], 16)

            def item_qk(t0, bt, g, it, buffer=qk, loaded=qk_loaded, back=1):
                sp.wait_ge(products, it * (G * N) + (N * (g + 1 - back) + N))
                for w in range(2):
                    for c in range(2):
                        sp.dma_start(buffer[:, w, c, :, :], heads_of(qkv[t0 + c, w, :, bt], g))\
                            .then_inc(loaded, 16)

            def mix_qk(n, g):
                item_qk(2, n, g, n + BT, (qk, qk2)[g % 2], (qk_loaded, qk2_loaded)[g % 2], 2)

            def item_v(t0, bt, g):
                for c in range(2):
                    sp.dma_start(vv[:, c, :, :], heads_of(qkv[t0 + c, 2, :, bt], g)).then_inc(v_loaded, 16)

            def item_out(half, bt, g, k):
                sp.wait_ge(pv_step, k * 24 + 27)
                for c in range(2):
                    sp.dma_start(heads_of(att[half, c, :, bt], g), ao[:, c, :, :]).then_inc(ao_stored, 16)

            def heads_of(x, g):
                return x[:, :, g * P:(g + 1) * P].rearrange("n p d -> p n d")

            def step_start(c0, half, enc, first=0, last=KX // 2):
                with sp.Fori(first, last) as q:
                    for j in range(RING):
                        k = q * 2 + j // 2
                        src = xs[half, k] if j % 2 == 0 else enc_w[enc, k]
                        load(c0 + q * RING + j, j, src)

            def step_quads(c0, enc, first, last):
                with sp.Fori(first, last) as q:
                    for j in range(RING):
                        load(c0 + 2 * KX + q * RING + j, j, enc_w[enc, q * RING + (KX + j)])

            QUADS = (USE_STEP - KX) // RING
            with sp.Fori(0, 2) as t:
                step_start(t * RAW_STEP, 0, t)
                step_quads(t * RAW_STEP, t, 0, QUADS)
            with sp.Fori(0, 2) as e:
                c0, i0, i1 = e * RAW_STEP + 2 * RAW_STEP, e * 2, e * 2 + 1
                step_start(c0, 1, e, 0, 3)
                for b in range(BT):
                    sp.wait_ge(stored[b], 16 * 2 * 3 * N + 16)
                item_qk(0, i0, 0, i0)
                step_start(c0, 1, e, 3)
                at = 0

                def quads_to(q):
                    nonlocal at
                    step_quads(c0, e, at, q)
                    at = q

                for q, it, g in ((4, i0, 1), (5, i0, 2), (8, i0, 3), (9, i1, 0)):
                    quads_to(q)
                    item_qk(0, it, g, it)
                quads_to(13)
                item_v(0, i0, 0)
                item_qk(0, i1, 1, i1)
                quads_to(17)
                item_out(0, i0, 0, i0 * G + 0)
                item_v(0, i0, 1)
                quads_to(21)
                item_qk(0, i1, 2, i1)
                item_out(0, i0, 1, i0 * G + 1)
                item_v(0, i0, 2)
                quads_to(22)
                item_qk(0, i1, 3, i1)
                quads_to(25)
                item_out(0, i0, 2, i0 * G + 2)
                item_v(0, i0, 3)
                quads_to(29)
                item_out(0, i0, 3, i0 * G + 3)
                item_v(0, i1, 0)
                quads_to(30)
                for g in range(2):
                    item_out(0, i1, g, i1 * G + g)
                    item_v(0, i1, g + 1)
                quads_to(31)
                item_out(0, i1, 2, i1 * G + 2)
                item_v(0, i1, 3)
                item_out(0, i1, 3, i1 * G + 3)


            def mix_quads(half, n, qs, first=0, last=RING):
                for q in qs:
                    for j in range(first, last):
                        src = wo[q, j] if q < 2 else int_w[n, q - 2, j]
                        load(n * 16 + (RAW_MIX0 + half * RAW_MIX + 4 * q + j), j, src)

            def dense_quads(half, first, last):
                c0 = RAW_MIX0 + half * RAW_MIX + STREAMS
                with sp.Fori(first, last) as q:
                    for j in range(RING):
                        k = q * 2 + j // 2
                        src = top1[k + KD] if j % 2 == 0 else xs[half, k]
                        load(c0 + q * RING + j, j, src)

            def tail_quad(half, q):
                for j in range(RING):
                    src, width = ((post_w[q, j], 512) if q < 3 else (top1[j], 512) if q == 3 else (top2[j], 256))
                    load(RAW_MIX0 + TAIL0 + half * RAW_TAIL + 4 * q + j, j, src, width)

            def store_ri(half, n):
                sp.wait_ge(bank_free[1], n * 16 + (4 * STEPS * SET1_STEP + half * SET1_MIX + 4 + 16))
                sp.dma_start(ri[half, n, 0].rearrange("b p d -> p b d"), rstage[:, 0, :, :]).then_inc(ri_stored[0], 16)
                sp.wait_ge(bank_free[0], n * 12 + (4 * STEPS * SET0_STEP + half * SET0_MIX + 4 + 12))
                sp.dma_start(ri[half, n, 1].rearrange("b p d -> p b d"), rstage[:, 1, :, :]).then_inc(ri_stored[1], 16)

            def own_v(k, bt, g, buffer=0, back=0):
                if back is not None:
                    sp.wait_ge(own_done, k + 1 - back)
                for c in range(2):
                    sp.dma_start(vv2[buffer][:, c, :, :], heads_of(qkv[2 + c, 2, :, bt], g))\
                        .then_inc(own_loaded[buffer], 16)

            def own_out(k, bt, g, buffer=0):
                sp.wait_ge(own_done, k + 2)
                for c in range(2):
                    sp.dma_start(heads_of(att[1, c, :, bt], g), ao2[buffer][:, c, :, :])\
                        .then_inc(own_stored[buffer], 16)

            def unit_load(half, bt, f, k):
                sp.wait_ge(sup_step, k * 6 + 6)
                for c in range(2):
                    src = ri[half, :, c, bt, :, 256 * f:256 * f + 256].rearrange("n p d -> p n d")
                    sp.dma_start(rl[:, f, c, :, :], src).then_inc(rl_loaded[f], 16)

            def mix_stream(n, values, last=False):
                k = n * 3 + (BT * G - 3)
                mix_qk(n, 1)
                if values:
                    item_v(2, n - 1, 0)
                mix_quads(0, n, (0, 1) if values else (1,))
                mix_qk(n, 2)
                mix_quads(0, n, (2,), 0, 2)
                if values:
                    item_out(1, n - 1, 0, k)
                    item_v(2, n - 1, 1)
                    store_ri(0, n - 1)
                    own_v(n - 1, n - 1, 3)
                mix_quads(0, n, (2,), 2, 4)
                mix_quads(0, n, (3,), 0, 1)
                mix_qk(n, 3)
                mix_quads(0, n, (3,), 1, 3)
                if values:
                    item_out(1, n - 1, 1, k + 1)
                    item_v(2, n - 1, 2)
                mix_quads(0, n, (3,), 3, 4)
                if not last:
                    mix_qk(n + 1, 0)
                if values:
                    item_out(1, n - 1, 2, k + 2)
                    own_out(n - 1, n - 1, 3)

            mix_quads(0, 0, (0,))
            for b in range(BT):
                sp.wait_ge(stored[b], 16 * STEPS * 3 * N + 16)
            item_qk(2, 0, 0, BT)
            mix_stream(0, False)
            with sp.Fori(1, N - 1) as n:
                mix_stream(n, True)
            mix_stream(N - 1, True, True)
            own = BT - 1
            own_v(own, BT - 1, 0, 1, None)
            own_v(own + 1, BT - 1, 1, 0, 1)
            for g in range(G):
                dense_quads(0, 2 * g, 2 * g + 2)
                if g == 0:
                    store_ri(0, N - 1)
                own_out(own + g, BT - 1, g, 1 - g % 2)
                if g + 2 < G:
                    own_v(own + g + 2, BT - 1, g + 2, 1 - g % 2, 1)

            for c in range(2):
                sp.wait_ge(ri_stored[c], 16 * N + 16)
            for i, count in enumerate((own + G // 2, G // 2)):
                sp.wait_ge(own_stored[i], 32 * count + 32)
            unit_load(0, 0, 0, 0)
            unit_load(0, 0, 1, 1)
            mix_quads(1, 0, range(4))
            unit_load(0, 1, 0, 2)
            with sp.Fori(1, N - 1) as n:
                mix_quads(1, n, (0,))
                unit_load(0, n, 1, n * 2 + 1)
                mix_quads(1, n, (1,))
                store_ri(1, n - 1)
                mix_quads(1, n, (2, 3))
                unit_load(0, n + 1, 0, n * 2 + 2)
            mix_quads(1, N - 1, (0,))
            unit_load(0, BT - 1, 1, UNITS - 1)
            mix_quads(1, N - 1, (1,))
            store_ri(1, N - 2)
            mix_quads(1, N - 1, (2, 3))

            dense_quads(1, 0, 1)
            store_ri(1, N - 1)
            for c in range(2):
                sp.wait_ge(ri_stored[c], 2 * 16 * N + 16)
            unit_load(1, 0, 0, UNITS)
            dense_quads(1, 1, 2)
            unit_load(1, 0, 1, UNITS + 1)
            dense_quads(1, 2, 6)
            unit_load(1, 1, 0, UNITS + 2)
            dense_quads(1, 6, 8)
            for u, qs in ((3, (0,)), (4, (1, 2)), (5, (3,)), (6, (4,)), (7, ())):
                unit_load(1, u // 2, u % 2, UNITS + u)
                for q in qs:
                    tail_quad(0, q)
            for q in range(5):
                tail_quad(1, q)

        @block.gpsimd
        def _(pool):
            pool.memset(ident[:, :], 0.0).then_inc(consts, 1)
            pool.memset(epsc[:, 0:1], LN_EPS).then_inc(consts, 1)
            pool.memset(epsc[:, 1:2], EPS).then_inc(consts, 1)
            pool.wait_ge(consts, 3)
            pool.affine_select(out=ident[:, :], in_=ident[:, :], compare_op=ALU.not_equal, fill=1.0,
                               base=0, pattern=[[-1, P]], channel_multiplier=1).then_inc(consts, 1)

            def low(chunk, j, hi, lo, width=512):
                pool.wait_ge(hi_done, chunk + 1)
                pool.tensor_tensor(lo, raw[:, j, 0:width], hi.bitcast(F32), ALU.subtract)\
                    .then_inc(lo_done, 1)

            def lows(chunk):
                for j in range(RING):
                    low(chunk + j, j, w_hi[:, j, :], w_lo[:, j, :])

            def step_start(c0):
                for k in range(KX):
                    low(c0 + 2 * k, 2 * k % RING, a_hi[:, k, :], a_lo[:, k, :])
                    low(c0 + (2 * k + 1), (2 * k + 1) % RING, w_hi[:, k % RING, :], w_lo[:, k % RING, :])

            def step_quads(c0, first, last):
                with pool.Fori(first, last) as q:
                    lows(c0 + 2 * KX + q * RING)

            def value(it, g, r, k=None):
                c, n = r // N, r % N
                k = it * G + g if k is None else k
                if r == 0:
                    pool.wait_ge(weights_done, it + 1)
                    pool.wait_ge(v_loaded, k * 32 + 32)
                    pool.wait_ge(ao_stored, k * 32 + 32)
                done = Count(pv_step, k * 24 + 3 * r)
                pool.wait_ge(pv_step, done.now + 3)
                pool.tensor_tensor(pv[:, :].rearrange("p (a d) -> p a d", d=HD),
                                   sm[:, 4, N * g + n, :, None].broadcast_to([P, 8, HD]),
                                   vv[:, c].rearrange("p m (h d) -> p (m h) d", d=HD), ALU.mult).then_inc(pv_step, 1)
                pool.wait_ge(pv_step, done.next() + 3)
                pool.tensor_tensor(pv2[:, :], pv[:, 0:2 * P], pv[:, 2 * P:4 * P], ALU.add).then_inc(pv_step, 1)
                pool.wait_ge(pv_step, done.next() + 3)
                pool.tensor_tensor(ao[:, c, n, :], pv2[:, 0:P], pv2[:, P:2 * P], ALU.add).then_inc(pv_step, 1)

            def values(it, g, k=None):
                for r in range(8):
                    value(it, g, r, k)

            QUADS = (USE_STEP - KX) // RING
            with pool.Fori(0, 2) as t:
                step_start(t * RAW_STEP)
                step_quads(t * RAW_STEP, 0, QUADS)

            pool.wait_ge(ids_loaded, 16)
            for b in range(BATCH // P):
                for f in range(N):
                    pool.indirect_dma_start(
                        strength[:, b, f, :], None, tables[f],
                        bass.IndirectOffsetOnAxis(ap=ids_sb[:, N * b + f:N * b + f + 1].bitcast(U32), axis=0))\
                        .then_inc(gathered, 16)

            with pool.Fori(0, 2) as e:
                c0, i0, i1 = e * RAW_STEP + 2 * RAW_STEP, e * 2, e * 2 + 1
                step_start(c0)
                step_quads(c0, 0, 12)
                for g in range(G):
                    r = 0
                    for q in range(12 + 4 * g, 16 + 4 * g):
                        for j in range(RING):
                            low(c0 + (2 * KX + q * RING + j), j, w_hi[:, j, :], w_lo[:, j, :])
                            if q % 4 and j < 3 and r < 8:
                                value(i0, g, r)
                                r += 1
                cq = c0 + (2 * KX + 28 * RING)
                lows(cq)
                values(i1, 0)
                lows(cq + RING)
                values(i1, 1)
                for r in range(3):
                    value(i1, 2, r)
                lows(cq + 2 * RING)
                for r in range(3, 8):
                    value(i1, 2, r)
                values(i1, 3)

            pool.sem_inc(sup_step, 12)
            for q in range(4):
                lows(RAW_MIX0 + q * RING)
            with pool.Fori(1, N) as n:
                r = 0
                for i, steps in enumerate((0, 1, 1, 1, 1, 2, 2, 0, 2, 2, 2, 2, 0, 3, 3, 2)):
                    low(n * 16 + (RAW_MIX0 + i), i % RING, w_hi[:, i % RING, :], w_lo[:, i % RING, :])
                    for _ in range(steps):
                        value(n + (BT - 1), r // 8, r % 8, n * 3 + (BT * G - 3 + r // 8))
                        r += 1
                assert r == 24
            dense = RAW_MIX0 + STREAMS
            for q in range(8):
                lows(dense + q * RING)

            def square_sum(k, f):
                pool.wait_ge(squares, k * 2 + 2)
                pool.tensor_tensor(mm[:, f, 0], mm[:, f, 0], mm[:, f, 1], ALU.add).then_inc(sq_sum, 1)

            def mask_pairs(k, f):
                pool.wait_ge(masked, k + 1)
                pool.wait_ge(cos_done, k + 2)
                for d, at in ((1, 0), (2, 3), (3, 5)):
                    ins = pool.tensor_tensor(pm[:, at:at + N - d], mm[:, f, 0, 0:N - d], mm[:, f, 0, d:N], ALU.add)
                ins.then_inc(mask_step, 1)

            def finish(k, bt, f, half, last=False):
                if not last:
                    mask_pairs(k + 1, 1 - f)
                pool.wait_ge(cos_done, k + 3)
                R = [rl[:, f, c] for c in range(2)]
                for c in range(2):
                    pool.tensor_tensor(R[c], R[c], ww[:, :, :], ALU.mult).then_inc(sup_step, 1)
                for c in range(2):
                    pool.wait_ge(sup_step, k * 6 + (13 + c))
                    pool.tensor_tensor(R[c][:, 0:2], R[c][:, 0:2], R[c][:, 2:4], ALU.add).then_inc(sup_step, 1)
                if half == 1:
                    pool.wait_ge(turned, STEPS * KH + HALVES * 8 * N + 8)
                    pool.wait_ge(sup_sq, 2 * BT)
                for c in range(2):
                    pool.wait_ge(sup_step, k * 6 + (15 + c))
                    pool.sem_inc(sup_seen, 1)
                    pool.tensor_tensor(sup[:, bt, c, 256 * f:256 * f + 256], R[c][:, 0], R[c][:, 1],
                                       ALU.add).then_inc(sup_step, 1)

            square_sum(0, 0)
            mask_pairs(0, 0)
            mix1 = RAW_MIX0 + RAW_MIX

            def stream(n, last):
                for q in range(4):
                    lows(n * 16 + (mix1 + q * RING))
                    if q == 0:
                        square_sum(n * 2 + 1, 1)
                    if q == 2:
                        finish(n * 2, n, 0, 0)
                if not last:
                    square_sum(n * 2 + 2, 0)
                finish(n * 2 + 1, n, 1, 0, last)

            with pool.Fori(0, N - 1) as n:
                stream(n, False)
            stream(N - 1, True)

            dense, tail = mix1 + STREAMS, RAW_MIX0 + TAIL0

            def tail_lows(half, q):
                width = 512 if q < 4 else 256
                for j in range(RING):
                    low(tail + half * RAW_TAIL + 4 * q + j, j, w_hi[:, j, 0:width], w_lo[:, j, 0:width], width)

            def steps(u):
                finish(UNITS + u, u // 2, u % 2, 1, u == UNITS - 1)

            def sums(u):
                square_sum(UNITS + u, u % 2)

            for q in range(8):
                lows(dense + q * RING)
                if q == 0:
                    sums(0)
                    mask_pairs(UNITS, 0)
                elif q == 2:
                    sums(1)
                elif q == 3:
                    steps(0)
                elif q == 5:
                    sums(2)
                elif q == 6:
                    steps(1)
            sums(3)
            tail_lows(0, 0)
            steps(2)
            tail_lows(0, 1)
            tail_lows(0, 2)
            sums(4)
            steps(3)
            sums(5)
            tail_lows(0, 3)
            steps(4)
            sums(6)
            steps(5)
            tail_lows(0, 4)
            sums(7)
            steps(6)
            steps(7)
            for q in range(5):
                tail_lows(1, q)

        @block.scalar
        def _(act):
            act.sem_inc(warmed, 1)
            act.sem_inc(lo_done, RING)
            act.sem_inc(ao_stored, 32)
            for i in range(2):
                act.sem_inc(own_stored[i], 32)
            for c in range(2):
                act.sem_inc(ri_stored[c], 16)
            act.dma_start(ids_sb[:, :], ids).then_inc(ids_loaded, 16)
            act.dma_start(mcols[:, :], mix_cols).then_inc(cols_loaded, 16)
            def high(chunk, use, j, dst, width=512):
                act.wait_ge(raw_loaded[j], chunk_loads(chunk, j))
                if use is not None:
                    act.wait_ge(chunk_used, use + 1)
                act.activation(dst, raw[:, j, 0:width], ACT.Identity).then_inc(hi_done, 1)

            def chunk_loads(chunk, j):
                return (chunk - j) * 4 + 16

            def high_part(dst, s, b, bias):
                if bias is None:
                    ins = act.activation(dst, bank(s, b), ACT.Copy)
                else:
                    ins = act.activation(dst, bank(s, b), ACT.Identity, bias=bias)
                ins.then_inc(h_done, 1)

            def prepare(func, count):
                act.wait_ge(warmed, count + 1)
                act.activation(warm[:, :], epsc[:, 0:1], func).then_inc(warmed, 1)

            def softmax(it):
                act.wait_ge(mag_in, it + 1)
                act.activation(sm[:, 0, :, :], sm[:, 1, :, :], ACT.Sqrt).then_inc(mag_out, 1)
                act.wait_ge(exp_in, it + 1)
                act.activation(sm[:, 2, :, :], sm[:, 1, :, :], ACT.Exp, scale=SCALE).then_inc(exp_out, 1)

            AHEAD = 3

            def x_and_w1(t, first, last):
                for k in range(first, last):
                    high(t * RAW_STEP + 2 * k, None, 2 * k % RING, a_hi[:, k, :])
                    high(t * RAW_STEP + (2 * k + 1), t * USE_STEP + k, (2 * k + 1) % RING, w_hi[:, k % RING, :])

            def encoder_step(t, tiles=None, last_step=False):
                c0, u0 = t * RAW_STEP, t * USE_STEP
                act.wait_ge(bank_free[0], t * (4 * SET0_STEP) + 4)
                act.wait_ge(bank_free[1], t * (4 * SET1_STEP) + 4)
                act.dma_start(rows[:, :], enc_rows[t % 2, :, 0:HID].broadcast_to([P, HID])).then_inc(rows_loaded, 16)
                act.dma_start(cols[:, :], enc_cols[t % 2]).then_inc(cols_loaded, 16)
                x_and_w1(t, AHEAD, KX)
                def quads(first, last):
                    with act.Fori(first, last) as q:
                        for j in range(RING):
                            high(c0 + 2 * KX + q * RING + j, u0 + KX + q * RING + j, j, w_hi[:, j, :])

                if tiles is None:
                    quads(0, 3 * KH // RING + 1)
                else:
                    quads(0, 11)
                    softmax(tiles[0])
                    quads(11, 3 * KH // RING + 1)
                act.wait_ge(consts, 4)
                prepare(ACT.Sqrt, t * 2)
                act.wait_ge(var_done, (t + 1) * BT)
                act.activation(ln[:, 0, :], mv[:, :, 1], ACT.Sqrt, bias=epsc[:, 0:1]).then_inc(sd_done, 1)
                prepare(ACT.Gelu, t * 2 + 1)
                act.dma_start(rows[:, 0:3 * D], enc_rows[t % 2, :, HID:HID + 3 * D].broadcast_to([P, 3 * D]))\
                    .then_inc(rows_loaded, 16)
                act.wait_ge(cols_loaded, t * 16 + 32)
                c1, u1 = c0 + 2 * KX + 3 * KH, u0 + 4 * KH
                for k in range(KH):
                    act.wait_ge(turned, t * KH + (k + 1))
                    act.wait_ge(tmp_done, t * KH + (k + 1))
                    act.activation(gf[:, k % 2, :], bank(1, k % 4), ACT.Gelu,
                                   scale=cols[:, k:k + 1], bias=cols[:, KH + k:KH + k + 1])
                    act.activation(a_hi[:, k, :], bank(1, k % 4), ACT.Gelu,
                                   scale=cols[:, k:k + 1], bias=cols[:, KH + k:KH + k + 1])\
                        .then_inc(bank_free[1], 1)
                    if k >= 4:
                        high(c1 + k, u1 + k, k % RING, w_hi[:, k % RING, :])
                for n in range(N):
                    q0 = c1 + (n + 1) * KH, u1 + (n + 1) * KH
                    for j in range(RING):
                        high(q0[0] + j, q0[1] + j, j, w_hi[:, j, :])
                    act.wait_ge(chunk_used, q0[1] + RING)
                    for b in range(KD):
                        high_part(s_hi[:, KD * n + b, :], n % 2, b,
                                  cols[:, 2 * KH + KD * n + b:2 * KH + KD * n + b + 1])
                    if n < N - 1:
                        with act.Fori(1, KH // RING) as q:
                            for j in range(RING):
                                high(q0[0] + q * RING + j, q0[1] + q * RING + j, j, w_hi[:, j, :])
                    if n == 1 and tiles is not None:
                        softmax(tiles[1])
                c2, u2 = c1 + N * KH, u1 + N * KH
                for w in range(3):
                    for n in range(N):
                        if n == N - 1 and w < 2:
                            for j in range(RING):
                                high(c2 + (KD * (w + 1) + j), u2 + (KD * (w + 1) + j), j, w_hi[:, j, :])
                        if (w, n) == (2, N - 1) and not last_step:
                            x_and_w1(t + 1, 0, AHEAD)
                        s = n % 2
                        for b in range(BT):
                            use = (4, 8)[s] + 2 * w + n // 2
                            act.wait_ge(bank_free[s], t * (4 * (SET0_STEP, SET1_STEP)[s]) + (4 * use + b + 5))
                            act.dma_start(qkv[t, w, n, b], stage[:, b, :]).then_inc(stored[b], 16)

            x_and_w1(0, 0, AHEAD)
            with act.Fori(0, 2) as t:
                encoder_step(t)
            encoder_step(2, (0, 1))
            encoder_step(3, (2, 3), True)
            act.wait_ge(bank_free[0], STEPS * (4 * SET0_STEP) + 4)
            act.wait_ge(bank_free[1], STEPS * (4 * SET1_STEP) + 4)
            act.dma_start(prow, post_row.broadcast_to([P, OUT])).then_inc(rows_loaded, 16)

            h0, f0 = STEPS * N * KD, STEPS * KH
            act.wait_ge(ao_stored, BT * G * 32 + 32)
            f0 = STEPS * KH

            def at_load(half, n):
                act.wait_ge(turned, n * 8 + (f0 + half * (8 * N)))
                for c in range(2):
                    act.dma_start(at_in[c][:, :, :], att[half, c, n].rearrange("b p d -> p b d"))\
                        .then_inc(at_loaded[c], 16)

            def stream(half, n, tile=None, units=False, last=False):
                cn = n * 16 + (RAW_MIX0 + half * RAW_MIX)
                un = n * 16 + (USE_MIX0 + half * RAW_MIX)

                def stream_highs(q):
                    for j in range(RING):
                        high(cn + (4 * q + j), un + (4 * q + j), j, w_hi[:, j, :])

                stream_highs(0)
                for c in range(2):
                    for k in range(KD):
                        act.wait_ge(turned, n * 8 + (f0 + half * (8 * N) + 4 * c + k + 1))
                        high_part(a_hi[:, 8 * c + k, :], 1 - c, k, None)
                if not last:
                    at_load(half, n + 1)
                if units:
                    magnitudes(n * 2 + 1, 1)
                for c in range(2):
                    stream_highs(c + 1)
                    act.wait_ge(chunk_used, un + (4 * c + 8))
                    for k in range(KD):
                        high_part(a_hi[:, 4 + 4 * c + k, :], 1 - c, k, mcols[:, KD * c + k:KD * c + k + 1])
                act.wait_ge(block_done, n * 2 + (half * (2 * N) + 9 * STEPS + 1))
                act.wait_ge(ri_stored[0], n * 16 + (half * (16 * N) + 16))
                for b in range(BT):
                    act.activation(rstage[:, 0, b, :], bank(1, b), ACT.Copy).then_inc(bank_free[1], 1)
                stream_highs(3)
                if tile is not None:
                    softmax(tile)
                if units and not last:
                    magnitudes(n * 2 + 2, 0)
                act.wait_ge(chunk_used, un + 20)
                act.wait_ge(ri_stored[1], n * 16 + (half * (16 * N) + 16))
                for b in range(BT):
                    act.activation(rstage[:, 1, b, :], bank(0, b), ACT.Copy).then_inc(bank_free[0], 1)

            def dense_highs(half, first, last):
                q0 = half * RAW_MIX + STREAMS
                for q in range(first, last):
                    for j in range(RING):
                        high(RAW_MIX0 + q0 + 4 * q + j, USE_MIX0 + q0 + 4 * q + j, j, w_hi[:, j, :])

            def magnitudes(k, f):
                act.wait_ge(rl_loaded[f], (k - f) * 16 + 32)
                act.wait_ge(cos_done, k + 1)
                for c in range(2):
                    act.activation(mm[:, f, c], rl[:, f, c], ACT.Square).then_inc(squares, 1)
                act.wait_ge(sq_sum, k + 1)
                act.activation(mm[:, f, 1], mm[:, f, 0], ACT.Sqrt).then_inc(roots, 1)

            at_load(0, 0)
            with act.Fori(0, N - 1) as n:
                stream(0, n, n + BT)
            stream(0, N - 1, N + BT - 1, last=True)
            dense_highs(0, 0, 7)
            act.wait_ge(ao_stored, (BT * G + 3 * (BT - 1)) * 32 + 32)
            for i, count in enumerate((BT - 1 + G // 2, G // 2)):
                act.wait_ge(own_stored[i], 32 * count + 32)
            at_load(1, 0)
            dense_highs(0, 7, 8)
            magnitudes(0, 0)
            with act.Fori(0, N - 1) as n:
                stream(1, n, units=True)
            stream(1, N - 1, units=True, last=True)

            def tail_pieces(half):
                tb = f0 + HALVES * 8 * N + 12 * half
                fh = f0 + 12 * half
                m1 = 4 * STEPS * SET1_STEP + 4 + HALVES * SET1_MIX + 16 * half

                def highs(q, width=512):
                    c = TAIL0 + half * RAW_TAIL + 4 * q
                    for j in range(RING):
                        high(RAW_MIX0 + c + j, USE_MIX0 + c + j, j, w_hi[:, j, 0:width], width)

                def transposes():
                    for c in range(2):
                        for k in range(KD):
                            act.wait_ge(turned, tb + (4 * c + k + 1))
                            high_part(a_hi[:, 4 * c + k, :], c, k, None)

                def norm_squares():
                    act.wait_ge(h_done, STEPS * N * KD + HALVES * 16 * N + 16 * half + 8)
                    for b in range(BT):
                        for c in range(2):
                            i = half * (2 * BT) + 2 * b + c
                            if i:
                                act.wait_ge(sup_sq, i)
                            act.activation(junk, sup[:, b, c, :], ACT.Square,
                                           accum_out=nrm[:, c, b:b + 1]).then_inc(sup_sq, 1)

                def norm_root():
                    act.wait_ge(sup_sum, half + 1)
                    act.activation(nrm[:, 2, :], nrm[:, 2, :], ACT.Sqrt, bias=epsc[:, 1:2]).then_inc(sup_root, 1)

                def measure():
                    d0 = 9 * STEPS + 2 * N * HALVES + 3 * half
                    act.wait_ge(block_done, d0 + 1)
                    for k in range(4):
                        act.activation(meas_r[:, k, :], bank(0, k), ACT.Copy).then_inc(bank_free[0], 1)
                    highs(1)
                    highs(2)
                    for c in range(2):
                        act.wait_ge(ri_stored[c], 2 * 16 * N + 16)
                    for k in range(4):
                        act.activation(meas_q[:, k, :], bank(1, k), ACT.Square).then_inc(bank_free[1], 1)

                def amplitude():
                    for k in range(4):
                        act.wait_ge(amp_in, half * 4 + (k + 1))
                        act.wait_ge(tmp_done, fh + (k + 1))
                        act.activation(gf[:, k % 2, :], meas_r[:, k, :], ACT.Sqrt)
                        act.activation(a_hi[:, 8 + k, :], meas_r[:, k, :], ACT.Sqrt).then_inc(h_done, 1)

                def post():
                    highs(3)
                    act.wait_ge(var_done, half * BT + (STEPS + 1) * BT)
                    act.activation(ln[:, 0, :], mv[:, :, 1], ACT.Sqrt, bias=epsc[:, 0:1]).then_inc(sd_done, 1)
                    if half:
                        prepare(ACT.Gelu, 2 * STEPS)

                def post_gelu():
                    for k in range(KD):
                        act.wait_ge(turned, tb + (9 + k))
                        act.wait_ge(tmp_done, fh + (5 + k))
                        for dst in (gf[:, k % 2, :], a_hi[:, 12 + k, :]):
                            ins = act.activation(dst, bank(0, k), ACT.Gelu,
                                                 scale=mcols[:, 2 * KD + k:2 * KD + k + 1],
                                                 bias=mcols[:, 3 * KD + k:3 * KD + k + 1])
                        ins.then_inc(bank_free[0], 1)
                    highs(4, 256)

                def top():
                    for k in range(4):
                        act.wait_ge(bank_free[1], m1 + (12 + k + 1))
                        act.wait_ge(tmp_done, fh + (9 + k))
                        act.activation(gf[:, k % 2, :], post_z[:, k, :], ACT.Relu)
                        act.activation(a_hi[:, k, :], post_z[:, k, :], ACT.Relu).then_inc(h_done, 1)

                return highs, transposes, norm_squares, norm_root, measure, amplitude, post, post_gelu, top

            tail_highs, transposes, norm_squares, norm_root, measured, amplitude, post, post_gelu, top = tail_pieces(0)
            dense_highs(1, 0, 1)
            magnitudes(UNITS, 0)
            transposes()
            dense_highs(1, 1, 3)
            norm_squares()
            magnitudes(UNITS + 1, 1)
            dense_highs(1, 3, 6)
            magnitudes(UNITS + 2, 0)
            dense_highs(1, 6, 8)
            norm_root()
            magnitudes(UNITS + 3, 1)
            tail_highs(0)
            measured()
            magnitudes(UNITS + 4, 0)
            amplitude()
            magnitudes(UNITS + 5, 1)
            post()
            magnitudes(UNITS + 6, 0)
            post_gelu()
            magnitudes(UNITS + 7, 1)
            top()
            tail_highs, transposes, norm_squares, norm_root, measured, amplitude, post, post_gelu, top = \
                tail_pieces(1)
            tail_highs(0)
            transposes()
            norm_squares()
            norm_root()
            measured()
            amplitude()
            post()
            post_gelu()
            top()
            act.wait_ge(bank_free[0], 4 * STEPS * SET0_STEP + 4 + SET0_ALL)
            act.dma_start(y.rearrange("b o -> o b"), y_sb[:, :]).then_inc(y_stored, 16)
            act.wait_ge(y_stored, 16)

        @block.tensor
        def _(pe):
            pe.sem_inc(chunk_used, RING)
            for s in range(2):
                pe.sem_inc(bank_free[s], 4)

            def three(out, lh, ll, rh, rl, start, stop):
                pe.matmul(out, lh, rh, start=start, stop=False)
                pe.matmul(out, lh, rl, start=False, stop=False)
                return pe.matmul(out, ll, rh, start=False, stop=stop)

            def act_stationary(s, hi, lo, j, start, stop):
                for b in range(BT):
                    last = three(bank(s, b), hi[:, b * P:(b + 1) * P], lo[:, b * P:(b + 1) * P],
                                 w_hi[:, j, :], w_lo[:, j, :], start, stop)
                return last

            def weight_stationary(s, hi, lo, j, start, stop, tiles=4):
                for b in range(tiles):
                    last = three(bank(s, b), w_hi[:, j, b * P:(b + 1) * P], w_lo[:, j, b * P:(b + 1) * P],
                                 hi, lo, start, stop)
                return last

            def banks(s, value, n=4):
                pe.wait_ge(bank_free[s], value + (n - 1))

            def turn(s, b, srcs):
                for i, src in enumerate(srcs):
                    last = pe.transpose(bank(s, b)[:, i * P:(i + 1) * P], src, ident[:, :])
                last.then_inc(turned, 1)

            with pe.Fori(0, STEPS) as t:
                c0, f0, f1 = t * RAW_STEP + RING, t * (4 * SET0_STEP) + 1, t * (4 * SET1_STEP) + 1
                banks(0, f0)
                for k in range(KX):
                    pe.wait_ge(lo_done, c0 + (2 * k + 2))
                    act_stationary(0, a_hi[:, k, :], a_lo[:, k, :], k % RING, k == 0, k == KX - 1)\
                        .then_inc(chunk_used, 1)
                for m in range(1, 4):
                    s = m % 2
                    banks(s, (f0, f1)[s] + 4 * (m // 2))
                    for k in range(KX):
                        pe.wait_ge(lo_done, c0 + (2 * KX + KH * (m - 1) + k + 1))
                        act_stationary(s, a_hi[:, k, :], a_lo[:, k, :], k % RING, k == 0, k == KX - 1)\
                            .then_inc(chunk_used, 1)
                c1 = c0 + (2 * KX + 3 * KH)

                def turn_hidden(k):
                    pe.wait_ge(normed, t * (4 * BT) + BT * (k // 4 + 1))
                    pe.wait_ge(bank_free[1], f1 + (8 + k))
                    turn(1, k % 4, [hid[:, b, k * P:(k + 1) * P] for b in range(BT)])

                pe.wait_ge(consts, 4)
                for k in range(4):
                    turn_hidden(k)
                for n in range(N):
                    s = n % 2
                    banks(s, (f0 + 8, f1 + 24)[s] + 4 * (n // 2))
                    for k in range(KH):
                        if n == 0:
                            pe.wait_ge(tmp_done, t * KH + (k + 3))
                        pe.wait_ge(lo_done, c1 + (n * KH + k + 1))
                        weight_stationary(s, a_hi[:, k, :], a_lo[:, k, :], k % RING, k == 0, k == KH - 1)\
                            .then_inc(chunk_used, 1)
                        if n == 0 and k + 4 < KH:
                            turn_hidden(k + 4)
                c2 = c1 + N * KH
                for w in range(3):
                    for n in range(N):
                        s = n % 2
                        banks(s, (f0 + 16, f1 + 32)[s] + (8 * w + 4 * (n // 2)))
                        for k in range(KD):
                            if n == 0:
                                pe.wait_ge(lo_done, c2 + (KD * w + k + 1))
                            last = act_stationary(s, s_hi[:, KD * n + k, :], s_lo[:, KD * n + k, :], k,
                                                  k == 0, k == KD - 1)
                            if n == N - 1:
                                last.then_inc(chunk_used, 1)
                        if n < N - 1:
                            last.then_inc(block_done, 1)

            f0 = 4 * STEPS * SET0_STEP + 1
            f1 = 4 * STEPS * SET1_STEP + 1

            def product(way, s, base, start, stop, chunk=None, release=True, done=None, tiles=4):
                for k in range(KD):
                    if chunk is not None:
                        pe.wait_ge(lo_done, chunk + (k + 1))
                    args = (s, a_hi[:, base + k, :], a_lo[:, base + k, :], k, start and k == 0, stop and k == KD - 1)
                    last = way(*args, tiles) if way is weight_stationary else way(*args)
                    if release:
                        last.then_inc(chunk_used, 1)
                if done is not None:
                    last.then_inc(done, 1)

            def streams(half):
                with pe.Fori(0, N) as n:
                    cn = n * 16 + (RAW_MIX0 + RING + half * RAW_MIX)
                    g0, g1 = n * 12 + (f0 + half * SET0_MIX), n * 16 + (f1 + half * SET1_MIX)
                    for c in range(2):
                        pe.wait_ge(at_loaded[c], n * 16 + (half * (16 * N) + 16))
                        banks(1 - c, (g1, g0)[c])
                        for k in range(KD):
                            turn(1 - c, k, [at_in[c][:, b, k * P:(k + 1) * P] for b in range(BT)])
                    banks(1, g1 + 4)
                    product(weight_stationary, 1, 0, True, True, cn)
                    banks(0, g0 + 4)
                    product(weight_stationary, 0, 8, True, True, cn + 4)
                    banks(1, g1 + 8)
                    product(act_stationary, 1, 4, True, True, cn + 8, False, block_done)
                    banks(0, g0 + 8)
                    product(act_stationary, 0, 8, True, False)
                    banks(1, g1 + 12)
                    product(act_stationary, 1, 8, True, True, cn + 12, False, block_done)
                    product(act_stationary, 0, 4, False, True)

            def dense(half):
                ct = RAW_MIX0 + RING + half * RAW_MIX + STREAMS
                banks(1, f1 + half * (SET1_MIX + 4) + 16 * N)
                for k in range(KX):
                    pe.wait_ge(lo_done, ct + (2 * k + 2))
                    jw, jx = 2 * k % RING, (2 * k + 1) % RING
                    for b in range(4):
                        last = three(bank(1, b), w_hi[:, jw, b * P:(b + 1) * P], w_lo[:, jw, b * P:(b + 1) * P],
                                     w_hi[:, jx, :], w_lo[:, jx, :], k == 0, k == KX - 1)
                    last.then_inc(chunk_used, 2)

            def turn_sup(half, e0, e1):
                pe.wait_ge(sup_step, 12 + 6 * UNITS * (half + 1))
                for c in range(2):
                    banks(c, (e0, e1)[c])
                    for k in range(KD):
                        turn(c, k, [sup[:, b, c, k * P:(k + 1) * P] for b in range(BT)])

            def tail(half, e0, e1):
                cm = RAW_MIX0 + RING + TAIL0 + half * RAW_TAIL
                banks(0, e0)
                banks(1, e1)
                product(weight_stationary, 0, 0, True, True, cm, False, block_done)
                product(weight_stationary, 1, 4, True, False)
                banks(0, e0 + 4)
                product(weight_stationary, 0, 4, True, True, cm + 4, False, block_done)
                product(weight_stationary, 1, 0, False, True)
                fh = half * 12 + STEPS * KH + 2
                pe.wait_ge(tmp_done, fh + 4)
                banks(1, e1 + 4)
                product(act_stationary, 1, 8, True, True, cm + 8)
                pe.wait_ge(normed, half * BT + (STEPS * 4 * BT + BT))
                banks(0, e0 + 8)
                for k in range(KD):
                    turn(0, k, [post_z[:, b, k * P:(k + 1) * P] for b in range(BT)])
                pe.wait_ge(tmp_done, fh + 8)
                banks(1, e1 + 8)
                product(weight_stationary, 1, 12, True, True, cm + 12)
                pe.wait_ge(tmp_done, fh + 12)
                banks(0, e0 + 12)
                product(weight_stationary, 0, 0, True, True, cm + 16, tiles=2)
                pe.wait_ge(h2_done, half * 2 + 2)
                for k in range(2):
                    last = pe.matmul(bank(0, 2)[0:1, :], mcols[:, MIX_COLS - 2 + k:MIX_COLS - 1 + k],
                                     hid2[:, k, :], start=(k == 0), stop=(k == 1))
                last.then_inc(block_done, 1)

            streams(0)
            dense(0)
            streams(1)
            e0, e1 = f0 + HALVES * SET0_MIX, f1 + 2 * 16 * N + 4
            turn_sup(0, e0, e1)
            dense(1)
            tail(0, e0 + 4, e1 + 8)
            turn_sup(1, e0 + 20, e1 + 20)
            tail(1, e0 + 24, e1 + 24)

        @block.vector
        def _(dve):
            dve.sem_inc(tmp_done, 2)
            for b in range(BT):
                dve.sem_inc(stored[b], 16)
            step = Count(dve_step)

            def link(ins):
                ins.then_inc(dve_step, 1)
                dve.wait_ge(dve_step, step.next())

            def low_part(lo, hi, s, b, bias):
                if bias is None:
                    ins = dve.tensor_tensor(lo, bank(s, b), hi.bitcast(F32), ALU.subtract)
                else:
                    ins = dve.scalar_tensor_tensor(out=lo, in0=bank(s, b), scalar=bias, in1=hi.bitcast(F32),
                                                   op0=ALU.add, op1=ALU.subtract)
                ins.then_inc(bank_free[s], 1)

            def norm_scales(count, var_at):
                dve.sem_inc(stats_seen, 1)
                for b in range(BT):
                    dve.bn_aggr(mv[:, b, :], stats[:, b, 0:count, :]).then_inc(var_done, 1)
                dve.wait_ge(sd_done, var_at)
                link(dve.reciprocal(ln[:, 1, :], ln[:, 0, :]))
                link(dve.scalar_tensor_tensor(out=ln[:, 2, :], in0=mv[:, :, 0], scalar=-1.0, in1=ln[:, 1, :],
                                              op0=ALU.mult, op1=ALU.mult))

            dve.sem_inc(products, N)
            dve.sem_inc(scored, N)
            dve.sem_inc(pv_step, 3)

            def scores(it, g, pair=None):
                buffer = qk if pair is None or g % 2 == 0 else qk2
                Q, K = buffer[:, 0], buffer[:, 1]
                if pair is None:
                    dve.wait_ge(qk_loaded, it * (64 * G) + (64 * g + 64))
                elif g % 2 == 0:
                    dve.wait_ge(qk_loaded, pair * 64 + (64 * G * BT + 64))
                else:
                    dve.wait_ge(qk2_loaded, pair * 64 + 64)
                dve.wait_ge(scored, it * (N * G) + (N * g + N))
                dve.tensor_tensor(Q[:, 2], Q[:, 0], Q[:, 1], ALU.add).then_inc(dve_step, 1)
                step.next()
                link(dve.tensor_tensor(K[:, 2], K[:, 0], K[:, 1], ALU.subtract))
                for n in range(N):
                    done = it * (N * G) + (N * g + n + 1 + N)
                    if n:
                        dve.wait_ge(scored, done - 1)
                    dve.tensor_tensor(prod[:, :].rearrange("p (x m d) -> p x m d", x=3, m=N),
                                      Q[:, :, n:n + 1, :].broadcast_to([P, 3, N, P]), K, ALU.mult)\
                        .then_inc(products, 1)
                    dve.wait_ge(products, done)
                    dve.tensor_reduce(dots[:, g, n, :, :].rearrange("p x m -> p (x m)"),
                                      prod[:, :].rearrange("p (a d) -> p a d", d=HD), AX_X, ALU.add)\
                        .then_inc(scored, 1)

            def softmax(it, k=None, own_before=None):
                dve.wait_ge(scored, it * (N * G) + (N * G + N))
                pr, pi, pm = (dots[:, :, :, x, :].rearrange("p g n m -> p (g n) m") for x in range(3))
                A = [sm[:, i, :, :] for i in range(5)]
                link(dve.tensor_tensor(A[2], pr, pi, ALU.add))
                link(dve.tensor_tensor(A[3], pm, pr, ALU.subtract))
                link(dve.tensor_tensor(A[3], A[3], pi, ALU.add))
                link(dve.tensor_tensor(A[2], A[2], A[2], ALU.mult))
                link(dve.tensor_tensor(A[3], A[3], A[3], ALU.mult))
                dve.scalar_tensor_tensor(out=A[1], in0=A[2], scalar=EPS, in1=A[3], op0=ALU.add, op1=ALU.add)\
                    .then_inc(mag_in, 1)
                dve.wait_ge(mag_out, it + 1)
                heads = lambda a: a.rearrange("p g (m h) -> p g h m", h=2)
                over = lambda a: a.rearrange("p g (m h) -> p g m h", h=2)
                spread = lambda a: a[:, :, None, :].broadcast_to([P, G * N, N, 2])
                link(dve.tensor_reduce(mx[:, 0], heads(A[0]), AX_X, ALU.max))
                dve.tensor_tensor(over(A[1]), over(A[0]), spread(mx[:, 0]), ALU.subtract).then_inc(exp_in, 1)
                dve.wait_ge(exp_out, it + 1)
                link(dve.tensor_reduce(mx[:, 1], heads(A[2]), AX_X, ALU.add))
                link(dve.reciprocal(mx[:, 0], mx[:, 1]))
                dve.wait_ge(pv_step, it * (24 * G) + 3 if k is None else k * 24 + 3)
                if own_before is not None:
                    dve.wait_ge(own_done, own_before)
                dve.tensor_tensor(over(A[4]), over(A[2]), spread(mx[:, 0]), ALU.mult).then_inc(weights_done, 1)

            SCORE_LINKS, SOFTMAX_LINKS = 2, 8
            STEP_LINKS = 2
            ATT_LINKS = 8 * SCORE_LINKS + 2 * SOFTMAX_LINKS

            def encoder_step(t, i0=None, i1=None):
                f = (t * (4 * SET0_STEP) + 4, t * (4 * SET1_STEP) + 4)
                u0 = t * USE_STEP + RING
                dve.wait_ge(rows_loaded, t * 32 + 16)
                dve.wait_ge(cols_loaded, t * 16 + 32)
                for m in range(4):
                    s = m % 2
                    dve.wait_ge(chunk_used, u0 + KX * (m + 1))
                    for b in range(BT):
                        dve.tensor_tensor(hid[:, b, m * 512:(m + 1) * 512], bank(s, b),
                                          rows[:, m * 512:(m + 1) * 512], ALU.add).then_inc(bank_free[s], 1)
                    for b in range(BT):
                        dve.wait_ge(bank_free[s], f[s] + (4 * (m // 2) + b + 1))
                        dve.bn_stats(stats[:, b, m, :], hid[:, b, m * 512:(m + 1) * 512]).then_inc(stats_done, 1)
                    if i0 is not None:
                        if m == 0:
                            scores(i0, 0)
                            scores(i0, 1)
                        elif m == 1:
                            scores(i0, 2)
                            scores(i0, 3)
                        elif m == 2:
                            softmax(i0)
                            scores(i1, 0)
                dve.wait_ge(stats_done, (t + 1) * (4 * BT))
                norm_scales(4, t + 1)

                def normalise(m, b):
                    part = hid[:, b, m * 512:(m + 1) * 512]
                    dve.tensor_scalar(part, part, ln[:, 1, b:b + 1], ln[:, 2, b:b + 1], ALU.mult, ALU.add)\
                        .then_inc(normed, 1)

                for b in range(BT):
                    normalise(0, b)
                for k in range(KH):
                    if k < 6:
                        for i in (2 * k, 2 * k + 1):
                            normalise(1 + i // BT, i % BT)
                    dve.wait_ge(bank_free[1], f[1] + (8 + k + 1))
                    dve.tensor_tensor(a_lo[:, k, :], gf[:, k % 2, :], a_hi[:, k, :].bitcast(F32), ALU.subtract)\
                        .then_inc(tmp_done, 1)
                for n in range(N):
                    for b in range(KD):
                        dve.wait_ge(h_done, t * (N * KD) + (KD * n + b + 1))
                        low_part(s_lo[:, KD * n + b, :], s_hi[:, KD * n + b, :], n % 2, b,
                                 cols[:, 2 * KH + KD * n + b:2 * KH + KD * n + b + 1])
                    if i0 is not None:
                        if n == 0:
                            scores(i1, 1)
                            scores(i1, 2)
                        elif n == 1:
                            scores(i1, 3)
                            softmax(i1)
                dve.wait_ge(rows_loaded, t * 32 + 32)
                u2 = u0 + (4 * KH + N * KH)
                for w in range(3):
                    for n in range(N):
                        s = n % 2
                        if n < N - 1:
                            dve.wait_ge(block_done, t * 9 + (3 * w + n + 1))
                        else:
                            dve.wait_ge(chunk_used, u2 + KD * (w + 1))
                        for b in range(BT):
                            dve.wait_ge(stored[b], t * (16 * 3 * N) + 16 * (4 * w + n + 1))
                            dve.tensor_tensor(stage[:, b, :], bank(s, b), rows[:, D * w:D * (w + 1)],
                                              ALU.add).then_inc(bank_free[s], 1)

            with dve.Fori(0, 2) as t:
                step.at(t * STEP_LINKS)
                encoder_step(t)
            with dve.Fori(0, 2) as e:
                step.at(e * (STEP_LINKS + ATT_LINKS) + 2 * STEP_LINKS)
                encoder_step(e + 2, e * 2, e * 2 + 1)
                assert step.n == STEP_LINKS + ATT_LINKS, step.n

            dve.sem_inc(own_done, 1)
            dve.wait_ge(gathered, 16 * N * BATCH // P)
            dve.sem_inc(cos_done, 2)
            step.at(4 * STEP_LINKS + 2 * ATT_LINKS)
            OWN_LINKS = 7

            def own(it, k, g, tiles, buffer=0, i=None):
                i = k if i is None else i
                dve.wait_ge(own_loaded[buffer], i * 32 + 32)
                dve.wait_ge(own_stored[buffer], i * 32 + 32)
                dve.wait_ge(weights_done, it + 1)
                dve.wait_ge(scored, tiles * (N * G) + N)
                for c in range(2):
                    for n in (0, 2):
                        w_ = sm[:, 4, N * g + n:N * g + n + 2, :, None].broadcast_to([P, 2, 8, HD])
                        v_ = vv2[buffer][:, c].rearrange("p m (h d) -> p (m h) d", d=HD)[:, None, :, :]\
                            .broadcast_to([P, 2, 8, HD])
                        link(dve.tensor_tensor(prod[:, 0:1024].rearrange("p (n a d) -> p n a d", n=2, a=8),
                                               w_, v_, ALU.mult))
                        ins = dve.tensor_reduce(ao2[buffer][:, c, n:n + 2, :],
                                                prod[:, 0:1024].rearrange("p (n m e) -> p n e m", n=2, m=N),
                                                AX_X, ALU.add)
                        if (c, n) == (1, 2):
                            ins.then_inc(own_done, 1)
                        else:
                            link(ins)
                dve.wait_ge(own_done, k + 2)

            h0 = STEPS * N * KD

            def stream(half, n, pieces):
                hn = n * 16 + (h0 + half * (16 * N))
                for c in range(2):
                    for k in range(KD):
                        dve.wait_ge(h_done, hn + (4 * c + k + 1))
                        low_part(a_lo[:, 8 * c + k, :], a_hi[:, 8 * c + k, :], 1 - c, k, None)
                for c in range(2):
                    pieces[c]()
                    for k in range(KD):
                        dve.wait_ge(h_done, hn + (8 + 4 * c + k + 1))
                        low_part(a_lo[:, 4 + 4 * c + k, :], a_hi[:, 4 + 4 * c + k, :], 1 - c, k,
                                 mcols[:, KD * c + k:KD * c + k + 1])
                pieces[2]()
                dve.wait_ge(block_done, n * 2 + (9 * STEPS + half * (2 * N) + 2))
                for b in range(BT):
                    dve.tensor_tensor(rstage[:, 0, b, :], rstage[:, 0, b, :], bank(1, b), ALU.subtract)\
                        .then_inc(bank_free[1], 1)

            def dense(half):
                dve.wait_ge(chunk_used, USE_MIX0 + RING + (half + 1) * RAW_MIX)
                if half:
                    dve.wait_ge(ri_stored[1], 2 * 16 * N + 16)
                for k in range(4):
                    dve.tensor_scalar(top_part[half][:, k, :], bank(1, k),
                                      mcols[:, 4 * KD + k:4 * KD + k + 1], None, ALU.add).then_inc(bank_free[1], 1)

            def attention(n, values):
                def first():
                    scores(n + BT, 0, n * 2 + 0)

                def second():
                    scores(n + BT, 1, n * 2)

                def then():
                    for g in (2, 3):
                        scores(n + BT, g, n * 2 + 1)
                    if values:
                        own(n + (BT - 1), n - 1, G - 1, n + (BT + 1))
                    softmax(n + BT, n * 3 + BT * G, n + 1)

                return first, second, then

            stream(0, 0, attention(0, False))
            before, links = step.now, G * SCORE_LINKS + SOFTMAX_LINKS + OWN_LINKS
            with dve.Fori(1, N) as n:
                step.at(n * links + (before - links))
                stream(0, n, attention(n, True))
                assert step.n == links, step.n
            step.at(before + (N - 1) * links)
            for g in range(G):
                own(2 * BT - 1, BT - 1 + g, g, 2 * BT, 1 - g % 2, g // 2 + (BT - 1 if g % 2 else 0))
            dense(0)

            off = {1: 0, 2: 3, 3: 5}

            def pair(i, j):
                return off[abs(i - j)] + min(i, j)

            def cosines(k, f):
                m1 = mm[:, f, 1]
                R, I = rl[:, f, 0], rl[:, f, 1]
                ur, ui = uu[:, 0], uu[:, 1]
                dve.wait_ge(masked, k + 1)
                dve.wait_ge(cos_done, k + 2)
                link(dve.tensor_tensor(m1, m1, mm[:, f, 0], ALU.add))
                link(dve.reciprocal(m1, m1))
                dve.tensor_tensor(ur, R, m1, ALU.mult)
                link(dve.tensor_tensor(ui, I, m1, ALU.mult))
                second = {1: m1[:, 0:3], 2: c2[:, 0:2], 3: m1[:, 3:4]}
                for d in (1, 2, 3):
                    dve.tensor_tensor(cc[:, off[d]:off[d] + N - d], ur[:, 0:N - d], ur[:, d:N], ALU.mult)
                    ins = dve.tensor_tensor(second[d], ui[:, 0:N - d], ui[:, d:N], ALU.mult)
                link(ins)
                for d in (1, 2, 3):
                    c_ = cc[:, off[d]:off[d] + N - d]
                    ins = dve.tensor_tensor(c_, c_, second[d], ALU.add)
                link(ins)
                dve.wait_ge(mask_step, k + 1)
                link(dve.tensor_tensor(cc[:, :, :], cc[:, :, :], pm[:, :, :], ALU.add))

            def weights(k):
                dve.wait_ge(sup_step, k * 6 + 8)
                s_ = lambda i, j: sh[:, N * i + j:N * i + j + 1]
                for r in range(N - 1):
                    for j in range(N):
                        i = [i for i in range(N) if i != j][r]
                        if r == 0:
                            ins = dve.tensor_scalar(ww[:, j], cc[:, pair(i, j)], s_(i, j), s_(j, j),
                                                    ALU.mult, ALU.add)
                        else:
                            ins = dve.scalar_tensor_tensor(out=ww[:, j], in0=cc[:, pair(i, j)],
                                                           scalar=s_(i, j), in1=ww[:, j],
                                                           op0=ALU.mult, op1=ALU.add)
                    if r < N - 2:
                        link(ins)
                    else:
                        ins.then_inc(cos_done, 1)

            def zeros(k, f):
                dve.wait_ge(roots, k + 1)
                dve.tensor_scalar(mm[:, f, 0], mm[:, f, 0], 0.0, None, ALU.is_equal).then_inc(masked, 1)

            def strengths(k, b):
                dve.wait_ge(cos_done, k + 2)
                dve.sem_inc(stats_seen, 1)
                link(dve.tensor_copy(sh[:, :], strength[:, b, :, :].rearrange("p i j -> p (i j)")))

            UNIT_LINKS = 8
            before, links = step.now, 2 * UNIT_LINKS + 1
            zeros(0, 0)

            def streamed(n, last):
                step.at(n * links + before)

                def first():
                    strengths(n * 2, n)
                    cosines(n * 2, 0)

                def second():
                    weights(n * 2)
                    zeros(n * 2 + 1, 1)

                def then():
                    cosines(n * 2 + 1, 1)
                    weights(n * 2 + 1)
                    if not last:
                        zeros(n * 2 + 2, 0)

                stream(1, n, (first, second, then))
                assert step.n == links, step.n

            with dve.Fori(0, N - 1) as n:
                streamed(n, False)
            streamed(N - 1, True)
            step.at(before + N * links)

            def tail_pieces(half):
                hs = h0 + HALVES * 16 * N + 16 * half
                e0 = 4 * STEPS * SET0_STEP + 4 + HALVES * SET0_MIX + 20 * half
                e1 = 4 * STEPS * SET1_STEP + 4 + HALVES * SET1_MIX + 16 * half
                d0 = 9 * STEPS + HALVES * 2 * N + 3 * half
                used = USE_MIX0 + RING + TAIL0 + RAW_TAIL * half

                def transposes():
                    for c in range(2):
                        for k in range(KD):
                            dve.wait_ge(h_done, hs + (4 * c + k + 1))
                            low_part(a_lo[:, 4 * c + k, :], a_hi[:, 4 * c + k, :], c, k, None)

                def norm():
                    dve.wait_ge(sup_sq, 2 * BT * (half + 1))
                    dve.tensor_tensor(nrm[:, 2, :], nrm[:, 0, :], nrm[:, 1, :], ALU.add).then_inc(sup_sum, 1)

                def measure():
                    dve.wait_ge(sup_root, half + 1)
                    link(dve.reciprocal(nrm[:, 3, :], nrm[:, 2, :]))
                    dve.wait_ge(block_done, d0 + 2)
                    for k in range(4):
                        dve.tensor_tensor(meas_r[:, k, :], meas_r[:, k, :], bank(0, k), ALU.subtract)\
                            .then_inc(bank_free[0], 1)
                    for k in range(4):
                        dve.wait_ge(bank_free[0], e0 + (8 + k + 1))
                        dve.tensor_tensor(meas_r[:, k, :], meas_r[:, k, :], meas_r[:, k, :], ALU.mult)\
                            .then_inc(dve_step, 1)
                        step.next()
                    for k in range(4):
                        dve.wait_ge(dve_step, step.now - 3 + k)
                        dve.wait_ge(bank_free[1], e1 + (4 + k + 1))
                        dve.tensor_tensor(meas_r[:, k, :], meas_r[:, k, :], meas_q[:, k, :], ALU.add)\
                            .then_inc(amp_in, 1)
                    split(8, 8)

                def split(dst, h):
                    for k in range(4):
                        dve.wait_ge(h_done, hs + (h + k + 1))
                        dve.tensor_tensor(a_lo[:, dst + k, :], gf[:, k % 2, :], a_hi[:, dst + k, :].bitcast(F32),
                                          ALU.subtract).then_inc(tmp_done, 1)

                def post():
                    dve.wait_ge(chunk_used, used + 3 * KD)
                    for b in range(BT):
                        dve.scalar_tensor_tensor(out=post_z[:, b, :], in0=bank(1, b), scalar=nrm[:, 3, b:b + 1],
                                                 in1=prow, op0=ALU.mult, op1=ALU.add).then_inc(bank_free[1], 1)
                    for b in range(BT):
                        dve.wait_ge(bank_free[1], e1 + (8 + b + 1))
                        dve.bn_stats(stats[:, b, 0, :], post_z[:, b, :]).then_inc(stats_done, 1)
                    dve.wait_ge(stats_done, half * BT + (4 * BT * STEPS + BT))
                    norm_scales(1, half + (STEPS + 1))
                    for b in range(BT):
                        dve.tensor_scalar(post_z[:, b, :], post_z[:, b, :], ln[:, 1, b:b + 1], ln[:, 2, b:b + 1],
                                          ALU.mult, ALU.add).then_inc(normed, 1)

                def post_gelu():
                    for k in range(KD):
                        dve.wait_ge(bank_free[0], e0 + (12 + k + 1))
                        dve.tensor_tensor(a_lo[:, 12 + k, :], gf[:, k % 2, :], a_hi[:, 12 + k, :].bitcast(F32),
                                          ALU.subtract).then_inc(tmp_done, 1)

                def top():
                    dve.wait_ge(chunk_used, used + 4 * KD)
                    for k in range(4):
                        dve.tensor_tensor(post_z[:, k, :], bank(1, k), top_part[half][:, k, :], ALU.add)\
                            .then_inc(bank_free[1], 1)
                    split(0, 12)

                def out():
                    dve.wait_ge(chunk_used, used + 5 * KD)
                    for k in range(2):
                        dve.tensor_scalar(hid2[:, k, :], bank(0, k), mcols[:, 4 * KD + 4 + k:4 * KD + 5 + k], 0.0,
                                          ALU.add, ALU.max).then_inc(h2_done, 1)
                    dve.wait_ge(block_done, d0 + 3)
                    dve.tensor_copy(y_sb[:, half * HALF:(half + 1) * HALF], bank(0, 2)[0:1, :])\
                        .then_inc(bank_free[0], 4)

                return transposes, norm, measure, post, post_gelu, top, out

            def unit(u):
                k = UNITS + u
                if u % 2 == 0:
                    strengths(k, BT + u // 2)
                cosines(k, u % 2)
                weights(k)
                if u < UNITS - 1:
                    zeros(k + 1, 1 - u % 2)

            transposes, norm, measured, post, post_gelu, top, out = tail_pieces(0)
            zeros(UNITS, 0)
            transposes()
            unit(0)
            norm()
            unit(1)
            unit(2)
            dense(1)
            unit(3)
            measured()
            unit(4)
            post()
            unit(5)
            post_gelu()
            unit(6)
            top()
            unit(7)
            out()
            for piece in tail_pieces(1):
                piece()


def kernel(**inputs):
    import numpy as np
    import concourse.bacc as bacc
    from concourse.bass_utils import run_bass_kernel_spmd

    a = {k: np.asarray(v) for k, v in inputs.items()}
    L = {k[len("L0_rec_"):]: v for k, v in a.items() if k.startswith("L0_rec_")}

    def chunks(w):
        k, n = w.shape
        return w.reshape(k // P, P, n // 512, 512).transpose(2, 0, 1, 3).reshape(-1, P, 512)

    def column(v):
        return v.reshape(-1, P).T

    def encoder(t, c):
        return np.concatenate([chunks(L[f"{t}_W1"].T), chunks(L[f"{t}_W2"].T)]
                              + [chunks(L[f"W{w}_{c}"].T) for w in "qkv"])

    arrays = {
        "enc_w": np.stack([encoder("er", "r"), encoder("ei", "i")]),
        "xs": a["r_x"].T.reshape(KX, P, HALVES, HALF).transpose(2, 0, 1, 3),
        "enc_rows": np.stack([np.concatenate([L[f"{t}_b1"]] + [L[f"b{w}_{c}"] for w in "qkv"])[None]
                              for t, c in (("er", "r"), ("ei", "i"))]),
        "enc_cols": np.stack([np.concatenate([column(L[f"{t}_{v}"]) for v in ("g1", "be1", "b2")], 1)
                              for t in ("er", "ei")]),
        "wo": np.stack([chunks(L[f"Wo_{c}"].T) for c in "ri"]),
        "int_w": np.stack([np.stack([chunks(L[f"int_W{c}"][n].T) for c in "ri"]) for n in range(N)]),
        "post_w": np.stack([chunks(L[w].T) for w in ("meas_Mr", "meas_Mi", "post_W")]),
        "top1": chunks(a["W_top1"]),
        "top2": a["W_top2"].reshape(KD, P, 256),
        "mix_cols": np.concatenate([column(L["bo_r"]), column(L["bo_i"]), column(L["post_g"]),
                                    column(L["post_be"]), column(a["b_top1"]), column(a["b_top2"]),
                                    column(a["W_top3"][:, 0])], 1),
        "post_row": L["post_b"][None],
        "ids": a["ids"].reshape(BATCH // P, P, N).transpose(1, 0, 2).reshape(P, -1),
        "tbl_0": a["tbl_0"], "tbl_1": a["tbl_1"], "tbl_2": a["tbl_2"], "tbl_3": a["tbl_3"],
    }
    nc = bacc.Bacc("TRN2", target_bir_lowering=False, num_devices=1)
    args = {}
    for name, x in arrays.items():
        arrays[name] = np.ascontiguousarray(x)
        args[name] = nc.dram_tensor(name, x.shape, I32 if name == "ids" else F32, kind="ExternalInput").ap()
    y = nc.dram_tensor("y", (BATCH, 1), F32, kind="ExternalOutput").ap()
    tables = [args.pop(f"tbl_{i}") for i in range(N)]
    build(nc, tables=tables, y=y, **args)
    r = run_bass_kernel_spmd(nc, [arrays], core_ids=[0])
    return r.results[0]["y"]
```
